# Optimizing a Trainium2 kernel written in Bass

```python
import numpy as np
import jax
import jax.numpy as jnp

def _softmax(x, axis=-1):
    return jax.nn.softmax(x, axis=axis)

def _gelu(x):
    return jax.nn.gelu(x, approximate=True)

def _silu(x):
    return jax.nn.silu(x)

def _sigmoid(x):
    return jax.nn.sigmoid(x)

def _layernorm(x, axis=-1, eps=1e-05):
    m = jnp.mean(x, axis=axis, keepdims=True)
    v = jnp.var(x, axis=axis, keepdims=True)
    return (x - m) / jnp.sqrt(v + eps)

def _scatter_add(tgt, idx, src, axis=0):
    return tgt.at[idx].add(src)

def _segment_sum(src, seg, n):
    return jax.ops.segment_sum(src, seg, n)
kernel_name = 'mk_pixart_seq_d2_seqx_r8_0e164b'

def setup_inputs(seed: int=0):
    np.random.seed(seed)
    _w = jnp.asarray

    def _rec_inputs():
        import jax
        import jax.numpy as jnp
        _rk = jax.random.key(seed)
        x = -0.0002928 + 1 * jax.random.normal(jax.random.fold_in(_rk, 1), (32, 128, 128), jnp.float32)
        _lenS = 128 - jax.random.randint(jax.random.fold_in(_rk, 7), (32,), 0, max(1, 128 // 4) + 1, jnp.int32)
        _lenS2 = 128 - jax.random.randint(jax.random.fold_in(_rk, 8), (32,), 0, max(1, 128 // 4) + 1, jnp.int32)
        cond_1024 = 0.0061147 + 1.02565 * jax.random.normal(jax.random.fold_in(_rk, 11), (32, 128), jnp.float32)
        _ctx_1024P = jax.random.normal(jax.random.fold_in(_rk, 12), (32, 16, 128), jnp.float32)
        _ctx_1024c = jax.random.dirichlet(jax.random.fold_in(_rk, 512), 0.3 * jnp.ones((16,), jnp.float32), (32, 128))
        _ctx_1024t = jnp.einsum('bsk,bkd->bsd', _ctx_1024c, _ctx_1024P)
        _ctx_1024t = _ctx_1024t * jax.lax.rsqrt(jnp.mean(jnp.square(_ctx_1024t)) + 1e-12) * 0.953939
        ctx_1024 = -0.00265004 + 0.998804 * (_ctx_1024t + 0.3 * jax.random.normal(jax.random.fold_in(_rk, 612), (32, 128, 128), jnp.float32))
        return (x, cond_1024, ctx_1024)
    x, cond_1024, ctx_1024 = _rec_inputs()

    def _L0_xcond_setup():
        import jax, jax.numpy as jnp
        import numpy as np
        LN_EPS = 1e-06

        def _ln(x):
            mu = jnp.mean(x, axis=-1, keepdims=True)
            var = jnp.var(x, axis=-1, keepdims=True)
            return (x - mu) * jax.lax.rsqrt(var + LN_EPS)
        key = jax.random.key(seed)
        H, NH = (128, 16)
        B, N, S = (4, 128, 77)
        MLP = int(H * 4.0)
        ks = jax.random.split(key, 20)
        s = 1.0 / np.sqrt(H)
        return {'x': jax.random.normal(ks[0], (B, N, H), jnp.float32), 'c': jax.random.normal(ks[1], (B, H), jnp.float32), 'context': jax.random.normal(ks[2], (B, S, H), jnp.float32), 'W_mod': jax.random.normal(ks[3], (H, 6 * H), jnp.float32) * s, 'b_mod': jnp.zeros((6 * H,), jnp.float32), 'W_qkv': jax.random.normal(ks[4], (H, 3 * H), jnp.float32) * s, 'b_qkv': jnp.zeros((3 * H,), jnp.float32), 'W_proj': jax.random.normal(ks[5], (H, H), jnp.float32) * s, 'b_proj': jnp.zeros((H,), jnp.float32), 'W_qc': jax.random.normal(ks[6], (H, H), jnp.float32) * s, 'b_qc': jnp.zeros((H,), jnp.float32), 'W_kvc': jax.random.normal(ks[7], (H, 2 * H), jnp.float32) * s, 'b_kvc': jnp.zeros((2 * H,), jnp.float32), 'W_cproj': jax.random.normal(ks[8], (H, H), jnp.float32) * s, 'b_cproj': jnp.zeros((H,), jnp.float32), 'W_mlp1': jax.random.normal(ks[9], (H, MLP), jnp.float32) * s, 'b_mlp1': jnp.zeros((MLP,), jnp.float32), 'W_mlp2': jax.random.normal(ks[10], (MLP, H), jnp.float32) * (1.0 / np.sqrt(MLP)), 'b_mlp2': jnp.zeros((H,), jnp.float32)}
    _L0_xcond_all = _L0_xcond_setup()
    _L0_xcond_in = {k: v for k, v in _L0_xcond_all.items() if k in ('W_mod', 'b_mod', 'W_qkv', 'b_qkv', 'W_proj', 'b_proj', 'W_qc', 'b_qc', 'W_kvc', 'b_kvc', 'W_cproj', 'b_cproj', 'W_mlp1', 'b_mlp1', 'W_mlp2', 'b_mlp2')}
    del _L0_xcond_all

    def _L1_xcond_setup():
        import jax, jax.numpy as jnp
        import numpy as np
        H = 128
        RH = 2 * H
        E = 3
        B, T, P = (8, 256, 64)
        LN_EPS = 1e-05

        def _layer_norm(x, gamma, beta):
            mu = jnp.mean(x, axis=-1, keepdims=True)
            var = jnp.mean(jnp.square(x - mu), axis=-1, keepdims=True)
            return (x - mu) * jax.lax.rsqrt(var + LN_EPS) * gamma + beta
        key = jax.random.key(seed)
        ks = jax.random.split(key, 24)
        s = lambda fan_in: 1.0 / np.sqrt(fan_in)
        inp = {'mix_hidden_states': jax.random.normal(ks[0], (B, T, H), jnp.float32), 'global_anchor': jax.random.normal(ks[1], (B, H), jnp.float32), 'prototype_bank': jax.random.normal(ks[2], (B, P, H), jnp.float32), 'ln_gamma': jnp.ones((H,), jnp.float32), 'ln_beta': jnp.zeros((H,), jnp.float32), 'Wq': jax.random.normal(ks[3], (H, H), jnp.float32) * s(H), 'Wk': jax.random.normal(ks[4], (H, H), jnp.float32) * s(H), 'Wv': jax.random.normal(ks[5], (H, H), jnp.float32) * s(H), 'router_W': jax.random.normal(ks[6], (3 * H, E), jnp.float32) * s(3 * H), 'router_b': jnp.zeros((E,), jnp.float32), 'e_w1': jax.random.normal(ks[7], (E, 3 * H, RH), jnp.float32) * s(3 * H), 'e_b1': jnp.zeros((E, RH), jnp.float32), 'e_w2': jax.random.normal(ks[8], (E, RH, H), jnp.float32) * s(RH), 'e_b2': jnp.zeros((E, H), jnp.float32), 'gate_w1': jax.random.normal(ks[9], (3 * H, H), jnp.float32) * s(3 * H), 'gate_b1': jnp.zeros((H,), jnp.float32), 'gate_w2': jax.random.normal(ks[10], (H, H), jnp.float32) * s(H), 'gate_b2': jnp.zeros((H,), jnp.float32), 'out_w': jax.random.normal(ks[11], (H, H), jnp.float32) * s(H), 'out_b': jnp.zeros((H,), jnp.float32)}
        return inp
    _L1_xcond_all = _L1_xcond_setup()
    _L1_xcond_in = {k: v for k, v in _L1_xcond_all.items() if k in ('ln_gamma', 'ln_beta', 'Wq', 'Wk', 'Wv', 'router_W', 'router_b', 'e_w1', 'e_b1', 'e_w2', 'e_b2', 'gate_w1', 'gate_b1', 'gate_w2', 'gate_b2', 'out_w', 'out_b')}
    del _L1_xcond_all
    return {'x': x, 'cond_1024': cond_1024, 'ctx_1024': ctx_1024, 'L0_xcond_W_mod': _L0_xcond_in['W_mod'], 'L0_xcond_b_mod': _L0_xcond_in['b_mod'], 'L0_xcond_W_qkv': _L0_xcond_in['W_qkv'], 'L0_xcond_b_qkv': _L0_xcond_in['b_qkv'], 'L0_xcond_W_proj': _L0_xcond_in['W_proj'], 'L0_xcond_b_proj': _L0_xcond_in['b_proj'], 'L0_xcond_W_qc': _L0_xcond_in['W_qc'], 'L0_xcond_b_qc': _L0_xcond_in['b_qc'], 'L0_xcond_W_kvc': _L0_xcond_in['W_kvc'], 'L0_xcond_b_kvc': _L0_xcond_in['b_kvc'], 'L0_xcond_W_cproj': _L0_xcond_in['W_cproj'], 'L0_xcond_b_cproj': _L0_xcond_in['b_cproj'], 'L0_xcond_W_mlp1': _L0_xcond_in['W_mlp1'], 'L0_xcond_b_mlp1': _L0_xcond_in['b_mlp1'], 'L0_xcond_W_mlp2': _L0_xcond_in['W_mlp2'], 'L0_xcond_b_mlp2': _L0_xcond_in['b_mlp2'], 'L1_xcond_ln_gamma': _L1_xcond_in['ln_gamma'], 'L1_xcond_ln_beta': _L1_xcond_in['ln_beta'], 'L1_xcond_Wq': _L1_xcond_in['Wq'], 'L1_xcond_Wk': _L1_xcond_in['Wk'], 'L1_xcond_Wv': _L1_xcond_in['Wv'], 'L1_xcond_router_W': _L1_xcond_in['router_W'], 'L1_xcond_router_b': _L1_xcond_in['router_b'], 'L1_xcond_e_w1': _L1_xcond_in['e_w1'], 'L1_xcond_e_b1': _L1_xcond_in['e_b1'], 'L1_xcond_e_w2': _L1_xcond_in['e_w2'], 'L1_xcond_e_b2': _L1_xcond_in['e_b2'], 'L1_xcond_gate_w1': _L1_xcond_in['gate_w1'], 'L1_xcond_gate_b1': _L1_xcond_in['gate_b1'], 'L1_xcond_gate_w2': _L1_xcond_in['gate_w2'], 'L1_xcond_gate_b2': _L1_xcond_in['gate_b2'], 'L1_xcond_out_w': _L1_xcond_in['out_w'], 'L1_xcond_out_b': _L1_xcond_in['out_b']}

def reference(x, cond_1024, ctx_1024, L0_xcond_W_mod, L0_xcond_b_mod, L0_xcond_W_qkv, L0_xcond_b_qkv, L0_xcond_W_proj, L0_xcond_b_proj, L0_xcond_W_qc, L0_xcond_b_qc, L0_xcond_W_kvc, L0_xcond_b_kvc, L0_xcond_W_cproj, L0_xcond_b_cproj, L0_xcond_W_mlp1, L0_xcond_b_mlp1, L0_xcond_W_mlp2, L0_xcond_b_mlp2, L1_xcond_ln_gamma, L1_xcond_ln_beta, L1_xcond_Wq, L1_xcond_Wk, L1_xcond_Wv, L1_xcond_router_W, L1_xcond_router_b, L1_xcond_e_w1, L1_xcond_e_b1, L1_xcond_e_w2, L1_xcond_e_b2, L1_xcond_gate_w1, L1_xcond_gate_b1, L1_xcond_gate_w2, L1_xcond_gate_b2, L1_xcond_out_w, L1_xcond_out_b):
    import jax
    import jax.numpy as jnp

    def _L0_xcond_ref(x, c, context, W_mod, b_mod, W_qkv, b_qkv, W_proj, b_proj, W_qc, b_qc, W_kvc, b_kvc, W_cproj, b_cproj, W_mlp1, b_mlp1, W_mlp2, b_mlp2):
        import jax, jax.numpy as jnp
        import numpy as np
        LN_EPS = 1e-06

        def _ln(x):
            mu = jnp.mean(x, axis=-1, keepdims=True)
            var = jnp.var(x, axis=-1, keepdims=True)
            return (x - mu) * jax.lax.rsqrt(var + LN_EPS)
        B, N, H = x.shape
        NH = 16
        hd = H // NH
        scale = hd ** (-0.5)
        c_proj = jax.nn.silu(c) @ W_mod + b_mod
        shift_a, scale_a, gate_a, shift_m, scale_m, gate_m = jnp.split(c_proj, 6, axis=-1)

        def modulate(t, shift, sc):
            return t * (1 + sc[:, None]) + shift[:, None]
        x_norm = modulate(_ln(x), shift_a, scale_a)
        qkv = x_norm @ W_qkv + b_qkv
        q, k, v = jnp.split(qkv, 3, axis=-1)
        q = q.reshape(B, N, NH, hd).transpose(0, 2, 1, 3)
        k = k.reshape(B, N, NH, hd).transpose(0, 2, 1, 3)
        v = v.reshape(B, N, NH, hd).transpose(0, 2, 1, 3)
        attn_w = jax.nn.softmax(jnp.einsum('bhqd,bhkd->bhqk', q, k) * scale, axis=-1)
        attn_out = jnp.einsum('bhqk,bhkd->bhqd', attn_w, v)
        attn_out = attn_out.transpose(0, 2, 1, 3).reshape(B, N, H)
        attn_out = attn_out @ W_proj + b_proj
        x = x + gate_a[:, None] * attn_out
        S = context.shape[1]
        q_c = _ln(x) @ W_qc + b_qc
        kv_c = _ln(context) @ W_kvc + b_kvc
        k_c, v_c = jnp.split(kv_c, 2, axis=-1)
        q_c = q_c.reshape(B, N, NH, hd).transpose(0, 2, 1, 3)
        k_c = k_c.reshape(B, S, NH, hd).transpose(0, 2, 1, 3)
        v_c = v_c.reshape(B, S, NH, hd).transpose(0, 2, 1, 3)
        c_attn_w = jax.nn.softmax(jnp.einsum('bhqd,bhsd->bhqs', q_c, k_c) * scale, axis=-1)
        c_attn_out = jnp.einsum('bhqs,bhsd->bhqd', c_attn_w, v_c)
        c_attn_out = c_attn_out.transpose(0, 2, 1, 3).reshape(B, N, H)
        c_attn_out = c_attn_out @ W_cproj + b_cproj
        x = x + c_attn_out
        x_norm2 = modulate(_ln(x), shift_m, scale_m)
        h = jax.nn.gelu(x_norm2 @ W_mlp1 + b_mlp1)
        h = h @ W_mlp2 + b_mlp2
        x = x + gate_m[:, None] * h
        return x

    def _L1_xcond_ref(mix_hidden_states, global_anchor, prototype_bank, ln_gamma, ln_beta, Wq, Wk, Wv, router_W, router_b, e_w1, e_b1, e_w2, e_b2, gate_w1, gate_b1, gate_w2, gate_b2, out_w, out_b):
        import jax, jax.numpy as jnp
        import numpy as np
        H = 128
        RH = 2 * H
        E = 3
        B, T, P = (8, 256, 64)
        LN_EPS = 1e-05

        def _layer_norm(x, gamma, beta):
            mu = jnp.mean(x, axis=-1, keepdims=True)
            var = jnp.mean(jnp.square(x - mu), axis=-1, keepdims=True)
            return (x - mu) * jax.lax.rsqrt(var + LN_EPS) * gamma + beta
        x = mix_hidden_states
        nx = _layer_norm(x, ln_gamma, ln_beta)
        q = nx @ Wq
        k = prototype_bank @ Wk
        v = prototype_bank @ Wv
        scores = jnp.einsum('bth,bph->btp', q, k) * H ** (-0.5)
        weights = jax.nn.softmax(scores, axis=-1)
        evidence = jnp.einsum('btp,bph->bth', weights, v)
        anchor = jnp.broadcast_to(global_anchor[:, None, :], nx.shape)
        combined = jnp.concatenate([nx, evidence, anchor], axis=-1)
        router_logits = combined @ router_W + router_b
        router_probs = jax.nn.softmax(router_logits, axis=-1)
        h = jax.nn.silu(jnp.einsum('btc,ecr->bter', combined, e_w1) + e_b1)
        expert_out = jnp.einsum('bter,erh->bteh', h, e_w2) + e_b2
        routed = jnp.sum(expert_out * router_probs[..., None], axis=-2)
        g = jax.nn.sigmoid(jax.nn.silu(combined @ gate_w1 + gate_b1) @ gate_w2 + gate_b2)
        refined_delta = g * (routed @ out_w + out_b)
        return x + refined_delta
    x = _L0_xcond_ref(x, cond_1024, ctx_1024, L0_xcond_W_mod, L0_xcond_b_mod, L0_xcond_W_qkv, L0_xcond_b_qkv, L0_xcond_W_proj, L0_xcond_b_proj, L0_xcond_W_qc, L0_xcond_b_qc, L0_xcond_W_kvc, L0_xcond_b_kvc, L0_xcond_W_cproj, L0_xcond_b_cproj, L0_xcond_W_mlp1, L0_xcond_b_mlp1, L0_xcond_W_mlp2, L0_xcond_b_mlp2)
    x = _L1_xcond_ref(x, cond_1024, ctx_1024, L1_xcond_ln_gamma, L1_xcond_ln_beta, L1_xcond_Wq, L1_xcond_Wk, L1_xcond_Wv, L1_xcond_router_W, L1_xcond_router_b, L1_xcond_e_w1, L1_xcond_e_b1, L1_xcond_e_w2, L1_xcond_e_b2, L1_xcond_gate_w1, L1_xcond_gate_b1, L1_xcond_gate_w2, L1_xcond_gate_b2, L1_xcond_out_w, L1_xcond_out_b)
    return x

_drawn_inputs = setup_inputs


def setup_inputs(seed=0):
    import zlib

    import numpy as np

    out = dict(_drawn_inputs(seed))
    spreads = {'L0_xcond_b_mod': (0.0, 0.1),
     'L0_xcond_b_qkv': (0.0, 0.1),
     'L0_xcond_b_proj': (0.0, 0.1),
     'L0_xcond_b_qc': (0.0, 0.502),
     'L0_xcond_b_kvc': (0.0, 0.1),
     'L0_xcond_b_cproj': (0.0, 0.1),
     'L0_xcond_b_mlp1': (0.0, 0.1),
     'L0_xcond_b_mlp2': (0.0, 0.1),
     'L1_xcond_ln_gamma': (1.0, 0.6),
     'L1_xcond_ln_beta': (0.0, 0.788),
     'L1_xcond_router_b': (0.0, 0.561),
     'L1_xcond_e_b1': (0.0, 0.512),
     'L1_xcond_e_b2': (0.0, 0.304),
     'L1_xcond_gate_b1': (0.0, 0.8),
     'L1_xcond_gate_b2': (0.0, 0.8),
     'L1_xcond_out_b': (0.0, 0.1)}
    factors = {}
    for name, (base, spread) in spreads.items():
        noise = np.random.default_rng([zlib.crc32(name.encode()), seed]).standard_normal(out[name].shape)
        drawn = base * np.exp(spread * noise) if base else spread * noise
        out[name] = jnp.asarray(drawn.astype(out[name].dtype))
    for name, factor in factors.items():
        out[name] = (out[name] * factor).astype(out[name].dtype)
    return out
```

```python
import concourse.bass as bass
from concourse import mybir
from contextlib import ExitStack

F32 = mybir.dt.float32
BF16 = mybir.dt.bfloat16
ALU = mybir.AluOpType
ACT = mybir.ActivationFunctionType
AX = mybir.AxisListType

P = 128
B = 32
GB = 4
NG = B // GB
GT = GB * P
NH = 16
HD = P // NH
NJ = NH // 2
VW = 32
NCORE = 2 * B
SCALE = float(HD) ** -0.5
SCALE1 = float(P) ** -0.5
Q_PART = (0, 1, 2, 0, 1, 0)
K_PART = (0, 0, 0, 1, 1, 2)
MAX_ROW = 6
STACK_MOVES = len(Q_PART) + len(K_PART) + 1
STACK_DMAS = 16 * STACK_MOVES

W_COLS = {}
_at = 0
for _name, _n in (("mod", 6 * P), ("q", P), ("k", P), ("v", P), ("proj", P), ("qc", P), ("kc", P), ("vc", P),
                  ("cproj", P), ("mlp1", 4 * P), ("mlp2", 4 * P), ("wqT", P), ("wkT", P), ("wvT", P),
                  ("r_nx", 3), ("r_ev", 3), ("r_an", 3), ("e_nx", 6 * P), ("g_nx", P), ("e_ev", 6 * P), ("g_ev", P),
                  ("e_an", 6 * P), ("g_an", P), ("gate2", P), ("e2T", 6 * P), ("outw", P)):
    W_COLS[_name] = (_at, _n)
    _at += _n
W_TOTAL = _at
V_COLS = {}
_at = 0
for _name, _n in (("bmod", 6), ("bq", 1), ("bk", 1), ("bv", 1), ("bproj", 1), ("bqc", 1), ("bkc", 1), ("bvc", 1),
                  ("bcproj", 1), ("bmlp1", 4), ("bmlp2", 1), ("gamma", 1), ("beta", 1), ("be1", 6), ("bg1", 1),
                  ("be2", 3)):
    V_COLS[_name] = (_at, _n)
    _at += _n
V_TOTAL = _at


class Core:

    def __init__(self, n, mod, kind, group, b):
        self.n, self.mod, self.kind, self.group, self.b = n, mod, kind, group, b


def core_at(i, s, steady):
    kind, b = (0, s) if s < GB else (1, s - GB)
    g = i - kind
    if steady:
        return Core(8 * i + (s - GB), (s + GB) % 8, kind, g, b)
    if not 0 <= g < NG:
        return None
    n = s if i == 0 else NCORE - GB + b if i == NG else 8 * i + (s - GB)
    return Core(n, n % 8, kind, g, b)


GROUP_STEPS = sorted([
    (0, "load", "ln_c", 0), (7, "stats", "ln_c", 0), (10, "norm", "ln_c", 0),
    (0, "stats", "ln_s", 1), (2, "norm", "ln_s", 1),
    (1, "fill", "v_c", -1), (2, "read", "v_c", -1),
    (3, "fill", "xt_s", 1), (4, "read", "xt_s", 1),
    (5, "fill", "q_s", 1), (6, "read", "q_s", 1),
    (7, "fill", "k_s", 1), (8, "read", "k_s", 1),
    (9, "fill", "proj_c", -2), (10, "read", "proj_c", -2),
    (11, "fill", "yt_c", -2), (12, "read", "yt_c", -2),
    (13, "fill", "xt_c", 0), (14, "read", "xt_c", 0),
    (15, "fill", "k_c", 0), (16, "read", "k_c", 0),
    (18, "fill", "v_s", 1), (19, "read", "v_s", 1),
    (21, "fill", "proj_s", 0), (22, "read", "proj_s", 0),
    (23, "fill", "yt_s", 0), (24, "read", "yt_s", 0),
    (24, "stats", "ln_x", 0), (26, "norm", "ln_x", 0),
    (27, "fill", "xt_x", 0), (28, "read", "xt_x", 0),
    (29, "fill", "q_c", 0), (30, "read", "q_c", 0),
])
BANK_ORDER = [name for _, step, name, _ in GROUP_STEPS if step == "fill"]
BANK_LAG = {name: lag for _, step, name, lag in GROUP_STEPS if step == "fill"}


def attention_events(i, steady=False):
    def valid(g):
        return steady or 0 <= g < NG

    def before(name):
        at, it = BANK_ORDER.index(name), i
        while True:
            at -= 1
            if at < 0:
                at, it = len(BANK_ORDER) - 1, it - 1
                if not steady and it < -1:
                    return None
            g = it + BANK_LAG[BANK_ORDER[at]]
            if valid(g):
                return BANK_ORDER[at], g

    for s in range(8):
        here = core_at(i, s, steady)
        back1 = core_at(i, s - 1, steady) if s else core_at(i - 1, 7, steady)
        back2 = core_at(i, s - 2, steady) if s > 1 else core_at(i - 1, s + 6, steady)
        ahead1 = core_at(i, s + 1, steady) if s < 7 else core_at(i + 1, 0, steady)
        ahead2 = core_at(i, s + 2, steady) if s < 6 else core_at(i + 1, s - 6, steady)
        for u in range(4):
            kind, lag, last = (1, -1, core_at(i - 1, 7, steady)) if s < 4 else (0, 1, core_at(i, 3, steady))
            if valid(i + lag):
                for m in range(8 * (s % 4) + 2 * u, 8 * (s % 4) + 2 * u + 2):
                    if m < STACK_MOVES:
                        yield ("stack", kind, i + lag, last, m)
            if u == 1 and back2:
                yield ("o_back", back2, back2.n + 1 + bool(back1) + bool(here) + bool(ahead1))
            if ahead2:
                yield ("score", ahead2, u)
            if here:
                yield ("shifted", here, u)
            if u == 0 and ahead1:
                yield ("max_turn", ahead1, ahead1.n - bool(here) - bool(back1) - bool(back2))
            if u > 1 and here:
                yield ("value", here, u - 2)
            if u < 2 and back1:
                yield ("value", back1, u + 2)
            if u == 2 and back1:
                yield ("o_turn", back1)
            if u == 3 and back1:
                yield ("o_norm", back1)
            if u == 3 and ahead2:
                yield ("max_parts", ahead2)
            for t, step, name, lag in (x for x in GROUP_STEPS if x[0] == 4 * s + u):
                if valid(i + lag):
                    if step == "fill":
                        last = {"proj_s": core_at(i, 3, steady), "proj_c": core_at(i - 1, 7, steady)}.get(name)
                        yield (step, name, i + lag, before(name), last)
                    else:
                        yield (step, name, i + lag)


def build_block(nc, xin, cond, ctxin, weights, vectors, ident_in, rowb, out):
    stack = ExitStack()
    with stack:
        def sb(name, shape, dt=F32):
            return stack.enter_context(nc.sbuf_tensor(name, shape, dt))

        def sem(name):
            return stack.enter_context(nc.semaphore(name))

        attention_memory = ExitStack()

        def asb(name, shape, dt=F32):
            return attention_memory.enter_context(nc.sbuf_tensor(name, shape, dt))

        X = sb("X", [P, B * P])
        W = sb("W", [P, W_TOTAL])
        V = sb("V", [P, V_TOTAL])
        ident = sb("ident", [P, P])
        identb = sb("identb", [P, P], BF16)

        def w(name, lo=0, n=None):
            at, size = W_COLS[name]
            return W[:, at + lo:at + lo + (size if n is None else n)]

        def vec(name, k=0):
            return V[:, V_COLS[name][0] + k:V_COLS[name][0] + k + 1]

        condr = sb("condr", [B, P])
        rows1 = sb("rows1", [1, 2 * P + 3])
        condT = sb("condT", [P, B])
        condS = sb("condS", [P, B])
        mod = sb("mod", [P, 6, B])
        gba = sb("gba", [P, B])
        gbm = sb("gbm", [P, B])
        bpr = sb("bpr", [P, 2])
        half = sb("half", [P, GB])
        eps = sb("eps", [P, GB])
        seen = sb("seen", [P, 1])
        zeros = sb("zeros", [P, GT])
        XN = [asb(f"XN{k}", [P, GT]) for k in range(3)]
        XT = [asb(f"XT{k}", [P, GT]) for k in range(3)]
        CTXG = asb("CTXG", [P, GB, P])
        stat = asb("stat", [P, 3, GB, 6])
        mv = asb("mv", [P, 3, GB, 2])
        veps = asb("veps", [P, 3, GB])
        rstd = asb("rstd", [P, 3, GB])
        Qp = [asb(f"Qp{k}", [P, 3, GT], BF16) for k in range(2)]
        Kp = [asb(f"Kp{k}", [P, 3, GT], BF16) for k in range(2)]
        full = asb("full", [P, 2, GT])
        rest = asb("rest", [P, GT])
        Qs = [asb(f"Qs{k}", [P, NJ, GT], BF16) for k in range(2)]
        Ks = [asb(f"Ks{k}", [P, NJ, GT], BF16) for k in range(2)]
        zrow = asb("zrow", [32, GT], BF16)
        orow = asb("orow", [32, GT], BF16)
        Va = [asb(f"Va{k}", [P, GB, NH, VW]) for k in range(2)]
        NM = asb("NM", [P, 2, NH])
        M2 = asb("M2", [P, 2, 2, 2, NJ], BF16)
        MT = asb("MT", [32, 2, P], BF16)
        PR = asb("PR", [P, 4, 4 * P])
        OTs = asb("OTs", [P, 4 * P])
        rden = asb("rden", [P, NH])
        On = asb("On", [P, 2, P])
        OgT = [asb(f"OgT{k}", [P, GT]) for k in range(2)]
        YT = [asb(f"YT{k}", [P, GT]) for k in range(2)]

        PS = [stack.enter_context(nc.psum_tensor(f"PS{k}", [P, 512], F32)) for k in range(8)]
        S_BANK, T_BANK, O_BANK, TURN_BANK, GROUP_BANK, SMALL_BANK = PS[0:2], PS[2:4], PS[4], PS[5], PS[6], PS[7]

        load_small = sem("load_small")
        load_w = sem("load_w")
        load_w2 = sem("load_w2")
        load_x = [sem(f"load_x{g}") for g in range(NG)]
        consts = sem("consts")
        stack_init = sem("stack_init")
        setup_pe = sem("setup_pe")
        setup_act = sem("setup_act")
        setup_dve = sem("setup_dve")

        kinds = ("s", "x", "c")
        ln_stat = [sem(f"ln_stat_{k}") for k in kinds]
        ln_mv = [sem(f"ln_mv_{k}") for k in kinds]
        ln_var = [sem(f"ln_var_{k}") for k in kinds]
        ln_rstd = [sem(f"ln_rstd_{k}") for k in kinds]
        ln_done = [sem(f"ln_done_{k}") for k in kinds]
        bank_filled = {e: sem(f"filled_{e}") for e in BANK_ORDER}
        bank_read = {e: sem(f"read_{e}") for e in BANK_ORDER}
        split = {e: sem(f"split_{e}") for e in ("q_s", "k_s", "q_c", "k_c")}
        parts_ready = {e: sem(f"parts_{e}") for e in ("q_s", "k_s", "q_c", "k_c")}
        stacked = [sem("stacked_self"), sem("stacked_cross")]
        ctx_loaded = sem("ctx_loaded")
        score_done = sem("score_done")
        max_done = sem("max_done")
        max_high = sem("max_high")
        max_parts = sem("max_parts")
        max_turned = sem("max_turned")
        max_copied = sem("max_copied")
        max_rows = sem("max_rows")
        shifted_done = sem("shifted_done")
        exp_done = sem("exp_done")
        value_done = sem("value_done")
        o_copied = sem("o_copied")
        o_turned = sem("o_turned")
        den_done = sem("den_done")
        o_normed = sem("o_normed")
        o_backed = sem("o_backed")
        o_stored = sem("o_stored")

        LN_KIND = {"ln_s": 0, "ln_x": 1, "ln_c": 2, "xt_s": 0, "xt_x": 1, "xt_c": 2}
        WEIGHT = {"q_s": "q", "k_s": "k", "q_c": "qc", "k_c": "kc", "v_s": "v", "v_c": "vc", "proj_s": "proj",
                  "proj_c": "cproj"}
        SOURCE = {"q_s": 0, "k_s": 0, "v_s": 0, "q_c": 1, "k_c": 2, "v_c": 2}
        BIAS = {"q_s": "bq", "k_s": "bk", "q_c": "bqc", "k_c": "bkc"}
        PARTS = {"q_s": Qp[0], "k_s": Kp[0], "q_c": Qp[1], "k_c": Kp[1]}
        FULL = {"q_s": 0, "k_s": 1, "q_c": 0, "k_c": 1}
        KIND = {"q_s": 0, "k_s": 0, "q_c": 1, "k_c": 1, "v_s": 0, "v_c": 1, "proj_s": 0, "proj_c": 1, "yt_s": 0,
                "yt_c": 1}

        def attention_loop(eng, body):
            for i in range(-1, 3):
                for ev in attention_events(i):
                    body(ev)
            with eng.Fori(3, 7) as i:
                for ev in attention_events(i, steady=True):
                    body(ev)
            for i in range(7, 10):
                for ev in attention_events(i):
                    body(ev)

        block = attention_memory.enter_context(nc.Block())

        @block.sync
        def _(sp):
            sp.dma_start(ident[:, :], ident_in).then_inc(load_small, 16)
            sp.dma_start(condr[:, :], cond).then_inc(load_small, 16)
            sp.dma_start(V[:, :], vectors).then_inc(load_small, 16)
            sp.dma_start(rows1[:, :], rowb).then_inc(load_w2, 16)
            sp.dma_start(W[:, 0:W_COLS["mlp1"][0]], weights[:, 0:W_COLS["mlp1"][0]]).then_inc(load_w, 16)
            for g in range(NG):
                sp.dma_start(X[:, g * GT:(g + 1) * GT].rearrange("p (b h) -> p b h", b=GB),
                             xin[g * GB:(g + 1) * GB].rearrange("b p h -> p b h")).then_inc(load_x[g], 16)
            sp.dma_start(W[:, W_COLS["mlp1"][0]:], weights[:, W_COLS["mlp1"][0]:]).then_inc(load_w2, 16)
            sp.wait_ge(stack_init, 1)
            for k in range(2):
                sp.dma_start(Ks[k][MAX_ROW::32, :, :], orow[:, :]).then_inc(consts, 16)

            def body(ev):
                name = ev[0]
                if name == "stack":
                    _, kind, g, last, m = ev
                    q, k = ("q_s", "k_s") if kind == 0 else ("q_c", "k_c")
                    if m == 0:
                        if last is not None:
                            sp.wait_ge(shifted_done, 4 * last.n + 4)
                        to, source = Qs[kind][MAX_ROW::32, :, :], zrow[:, :]
                    elif m <= len(K_PART):
                        if m == 1:
                            sp.wait_ge(parts_ready[k], g + 1)
                        to, source = Ks[kind][m - 1::8, :, :], Kp[kind][:, K_PART[m - 1], :]
                    else:
                        r = m - 1 - len(K_PART)
                        if r == 0:
                            sp.wait_ge(parts_ready[q], g + 1)
                        to, source = Qs[kind][r::8, :, :], Qp[kind][:, Q_PART[r], :]
                    sp.dma_start(to, source).then_inc(stacked[kind], 16)
                elif name == "max_turn":
                    c = ev[1]
                    sp.wait_ge(max_copied, c.n + 1)
                    sp.dma_start(Qs[c.kind][MAX_ROW::32, :, c.b * P:(c.b + 1) * P],
                                 MT[:, c.mod % 2, :]).then_inc(max_rows, 16)
                elif name == "load":
                    g = ev[2]
                    if not isinstance(g, int) or g > 0:
                        sp.wait_ge(ln_done[2], g)
                    sp.dma_start(CTXG[:, :, :], ctxin[bass.ds(g * GB, GB)].rearrange("b p h -> p b h"))\
                        .then_inc(ctx_loaded, 16)

            attention_loop(sp, body)

        @block.gpsimd
        def _(pool):
            nc.gpsimd.memset(zrow[:, :], 0.0)
            nc.gpsimd.memset(orow[:, :], 1.0)
            nc.gpsimd.memset(half[:, :], -0.5)
            nc.gpsimd.memset(eps[:, :], 1e-6)
            nc.gpsimd.memset(zeros[:, :], 0.0)
            for k in range(2):
                nc.gpsimd.memset(Qs[k][:, :, :].bitcast(F32), 0.0)
                last = nc.gpsimd.memset(Ks[k][:, :, :].bitcast(F32), 0.0)
            last.then_inc(stack_init, 1)
            pool.wait_ge(stack_init, 1)

            def body(ev):
                name = ev[0]
                if name == "stats":
                    g, k = ev[2], LN_KIND[ev[1]]
                    pool.wait_ge(ln_mv[k], g + 1)
                    nc.gpsimd.tensor_tensor(veps[:, k, :], mv[:, k, :, 1], eps[:, :], ALU.add)\
                        .then_inc(ln_var[k], 1)
                    pool.wait_ge(ln_var[k], g + 1)
                    nc.gpsimd.tensor_tensor(rstd[:, k, :], veps[:, k, :], half[:, :], ALU.pow)\
                        .then_inc(ln_rstd[k], 1)
                elif name == "read" and ev[1] in PARTS:
                    name, g = ev[1:]
                    kind, f, r = KIND[name], full[:, FULL[name], :], rest[:, :]
                    parts, done = PARTS[name], split[name]
                    pool.wait_ge(bank_read[name], g + 1)
                    if not isinstance(g, int) or g > 0:
                        pool.wait_ge(stacked[kind], STACK_DMAS * g)
                    nc.gpsimd.tensor_tensor(parts[:, 0, :], f, zeros[:, :], ALU.add).then_inc(done, 1)
                    pool.wait_ge(done, 3 * g + 1)
                    nc.gpsimd.tensor_tensor(r, f, parts[:, 0, :], ALU.subtract).then_inc(done, 1)
                    pool.wait_ge(done, 3 * g + 2)
                    nc.gpsimd.tensor_tensor(parts[:, 1, :], r, zeros[:, :], ALU.add).then_inc(done, 1)
                    pool.wait_ge(done, 3 * g + 3)
                    nc.gpsimd.tensor_tensor(parts[:, 2, :], r, parts[:, 1, :], ALU.subtract)\
                        .then_inc(parts_ready[name], 1)

            attention_loop(pool, body)

        @block.scalar
        def _(act):
            act.wait_ge(setup_pe, 1)
            nc.scalar.activation(condS[:, :], PS[0][:, 0:B], ACT.Silu).then_inc(setup_act, 1)
            act.wait_ge(setup_pe, 2)
            for k in range(6):
                nc.scalar.activation(mod[:, k, :], PS[1][:, k * B:(k + 1) * B], ACT.Identity,
                                     bias=vec("bmod", k))
            nc.scalar.activation(bpr[:, 0:1], PS[1][:, 6 * B:6 * B + 1], ACT.Identity, bias=vec("bproj"))
            nc.scalar.activation(bpr[:, 1:2], PS[1][:, 6 * B + 1:6 * B + 2], ACT.Identity,
                                 bias=vec("bcproj")).then_inc(setup_act, 1)
            act.wait_ge(setup_dve, 3)

            def body(ev):
                name = ev[0]
                if name == "shifted":
                    _, c, u = ev
                    act.wait_ge(shifted_done, 4 * c.n + (u + 1))
                    if not isinstance(c.n, int) or c.n > 0:
                        act.wait_ge(value_done, 4 * c.n + (u - 3))
                    nc.scalar.activation(PR[:, u, :], T_BANK[u % 2][:, :], ACT.Exp, scale=SCALE)\
                        .then_inc(exp_done, 1)
                elif name == "value" and ev[2] == 3:
                    c = ev[1]
                    act.wait_ge(value_done, 4 * c.n + 4)
                    if not isinstance(c.n, int) or c.n > 0:
                        act.wait_ge(o_turned, c.n)
                    nc.scalar.activation(OTs[:, :], O_BANK[:, :], ACT.Copy).then_inc(o_copied, 1)
                elif name == "max_turn":
                    c = ev[1]
                    act.wait_ge(max_turned, c.n + 1)
                    if not isinstance(c.n, int) or c.n > 1:
                        act.wait_ge(max_rows, 16 * (c.n - 1))
                    nc.scalar.activation(MT[:, c.mod % 2, :], SMALL_BANK[0:32, 0:P // 2].bitcast(BF16), ACT.Copy)\
                        .then_inc(max_copied, 1)
                elif name == "o_back":
                    c = ev[1]
                    act.wait_ge(o_backed, c.n + 1)
                    e = "proj_s" if c.kind == 0 else "proj_c"
                    if not isinstance(c.group, int) or c.group > 0:
                        act.wait_ge(bank_filled[e], c.group)
                    nc.scalar.activation(OgT[c.kind][:, c.b * P:(c.b + 1) * P], SMALL_BANK[:, 0:P], ACT.Copy)\
                        .then_inc(o_stored, 1)
                elif name == "read" and ev[1] in ("xt_s", "xt_x", "xt_c"):
                    name, g = ev[1:]
                    k = LN_KIND[name]
                    act.wait_ge(bank_filled[name], g + 1)
                    if k == 0:
                        for b in range(GB):
                            nb = bass.ds(g * GB + b, 1)
                            last = nc.scalar.activation(XT[0][:, b * P:(b + 1) * P],
                                                        GROUP_BANK[:, b * P:(b + 1) * P], ACT.Identity,
                                                        scale=mod[:, 1, nb], bias=mod[:, 0, nb])
                        last.then_inc(bank_read[name], 1)
                    else:
                        nc.scalar.activation(XT[k][:, :], GROUP_BANK[:, :], ACT.Copy).then_inc(bank_read[name], 1)
                elif name == "read" and ev[1] in PARTS:
                    name, g = ev[1:]
                    act.wait_ge(bank_filled[name], g + 1)
                    before = {"q_s": g - 1, "k_s": g - 1, "q_c": g + 2, "k_c": g + 2}[name]
                    other = {"q_s": "q_c", "k_s": "k_c", "q_c": "q_s", "k_c": "k_s"}[name]
                    if isinstance(before, int):
                        before = min(before, NG)
                    if not isinstance(before, int) or before > 0:
                        act.wait_ge(parts_ready[other], before)
                    nc.scalar.activation(full[:, FULL[name], :], GROUP_BANK[:, :], ACT.Identity,
                                         bias=vec(BIAS[name])).then_inc(bank_read[name], 1)
                elif name == "read" and ev[1] in ("v_s", "v_c"):
                    name, g = ev[1:]
                    kind = KIND[name]
                    act.wait_ge(bank_filled[name], g + 1)
                    nc.scalar.activation(Va[kind][:, :, :, 0:HD].rearrange("p b h d -> p (b h) d"),
                                         GROUP_BANK[:, :].rearrange("p (n d) -> p n d", d=HD), ACT.Copy)\
                        .then_inc(bank_read[name], 1)
                elif ev[:2] == ("read", "proj_c"):
                    name, g = ev[1:]
                    act.wait_ge(bank_filled[name], g + 1)
                    if not isinstance(g, int) or g > 0:
                        act.wait_ge(bank_filled["yt_c"], g)
                    nc.scalar.activation(YT[1][:, :], GROUP_BANK[:, :], ACT.Identity, bias=bpr[:, 1:2])\
                        .then_inc(bank_read[name], 1)

            attention_loop(act, body)

        @block.vector
        def _(dve):
            for k in range(2):
                nc.vector.memset(Va[k][:, :, :, :], 0.0)
            dve.drain()
            for k in range(2):
                nc.vector.memset(Va[k][:, :, :, HD:HD + 1], 1.0)
            dve.wait_ge(load_small, 48)
            nc.vector.tensor_copy(identb[:, :], ident[:, :]).then_inc(setup_dve, 1)
            dve.wait_ge(setup_pe, 1)
            dve.wait_ge(setup_act, 2)
            nc.vector.tensor_copy(condT[:, :], PS[0][:, 0:B])
            nc.vector.tensor_scalar(mod[:, 1, :], mod[:, 1, :], 1.0, None, ALU.add)
            nc.vector.tensor_scalar(mod[:, 4, :], mod[:, 4, :], 1.0, None, ALU.add).then_inc(setup_dve, 1)
            nc.vector.tensor_scalar(gba[:, :], mod[:, 2, :], bpr[:, 0:1], None, ALU.mult)
            nc.vector.tensor_scalar(gbm[:, :], mod[:, 5, :], vec("bmlp2"), None, ALU.mult).then_inc(setup_dve, 1)
            dve.wait_ge(setup_dve, 3)

            def ln_source(k, g, b):
                return CTXG[:, b, :] if k == 2 else X[:, bass.ds(g * GT + b * P, P)]

            def body(ev):
                name = ev[0]
                if name == "score":
                    _, c, u = ev
                    r = c.mod % 2
                    dve.wait_ge(score_done, 4 * c.n + (u + 1))
                    nc.vector.tensor_reduce(out=NM[:, r, 4 * u:4 * u + 4],
                                            in_=S_BANK[u % 2][:, :].rearrange("p (h k) -> p h k", k=P),
                                            axis=AX.X, op=ALU.max, negate=True).then_inc(max_done, 1)
                elif name == "max_parts":
                    c = ev[1]
                    r = c.mod % 2
                    nm = NM[:, r, :].rearrange("p (e j) -> p e j", e=2)
                    dve.wait_ge(max_done, 4 * c.n + 4)
                    if not isinstance(c.n, int) or c.n > 1:
                        dve.wait_ge(max_turned, c.n - 1)
                    nc.vector.tensor_copy(M2[:, r, :, 0, :], nm).then_inc(max_high, 1)
                    dve.wait_ge(max_high, c.n + 1)
                    nc.vector.tensor_tensor(M2[:, r, :, 1, :], nm, M2[:, r, :, 0, :], ALU.subtract)\
                        .then_inc(max_parts, 1)
                elif name == "o_norm":
                    c = ev[1]
                    r = c.mod % 2
                    turned = TURN_BANK[:, :].rearrange("p (h d) -> p h d", d=VW)
                    dve.wait_ge(o_turned, c.n + 1)
                    nc.vector.reciprocal(rden[:, :].unsqueeze(2), turned[:, :, HD:HD + 1]).then_inc(den_done, 1)
                    dve.wait_ge(den_done, c.n + 1)
                    if not isinstance(c.n, int) or c.n > 1:
                        dve.wait_ge(o_backed, c.n - 1)
                    nc.vector.tensor_tensor(On[:, r, :].rearrange("p (h d) -> p h d", d=HD), turned[:, :, 0:HD],
                                            rden[:, :].unsqueeze(2).to_broadcast([P, NH, HD]), ALU.mult)\
                        .then_inc(o_normed, 1)
                elif name == "stats":
                    g, k = ev[2], LN_KIND[ev[1]]
                    if k == 0 and isinstance(g, int):
                        dve.wait_ge(load_x[g], 16)
                    elif k == 0:
                        for q in range(NG):
                            dve.wait_ge(load_x[q], 16)
                    if k == 1:
                        dve.wait_ge(bank_read["yt_s"], g + 1)
                    if k == 2:
                        dve.wait_ge(ctx_loaded, 16 * (g + 1))
                    if k > 0:
                        nc.vector.tensor_copy(seen[:, :], half[:, 0:1])
                    for b in range(GB):
                        last = nc.vector.bn_stats(stat[:, k, b, :], ln_source(k, g, b))
                    last.then_inc(ln_stat[k], 1)
                    dve.wait_ge(ln_stat[k], g + 1)
                    nc.vector.tensor_copy(seen[:, :], stat[:, k, GB - 1, 0:1])
                    for b in range(GB):
                        last = nc.vector.bn_aggr(mv[:, k, b, :], stat[:, k, b, :])
                    last.then_inc(ln_mv[k], 1)
                elif name == "norm":
                    g, k = ev[2], LN_KIND[ev[1]]
                    dve.wait_ge(ln_rstd[k], g + 1)
                    xt = ("xt_s", "xt_x", "xt_c")[k]
                    if not isinstance(g, int) or g > 0:
                        dve.wait_ge(bank_filled[xt], g)
                    for b in range(GB):
                        last = nc.vector.tensor_scalar(XN[k][:, b * P:(b + 1) * P], ln_source(k, g, b),
                                                       mv[:, k, b, 0:1], rstd[:, k, b:b + 1], ALU.subtract,
                                                       ALU.mult)
                    last.then_inc(ln_done[k], 1)
                elif ev[:2] == ("read", "proj_s"):
                    name, g = ev[1:]
                    dve.wait_ge(bank_filled[name], g + 1)
                    if not isinstance(g, int) or g > 0:
                        dve.wait_ge(bank_filled["yt_s"], g)
                    for b in range(GB):
                        nb = bass.ds(g * GB + b, 1)
                        last = nc.vector.tensor_scalar(YT[0][:, b * P:(b + 1) * P],
                                                       GROUP_BANK[:, b * P:(b + 1) * P], mod[:, 2, nb],
                                                       gba[:, nb], ALU.mult, ALU.add)
                    last.then_inc(bank_read[name], 1)
                elif name == "read" and ev[1] in ("yt_s", "yt_c"):
                    name, g = ev[1:]
                    x = X[:, bass.ds(g * GT, GT)]
                    dve.wait_ge(bank_filled[name], g + 1)
                    nc.vector.tensor_tensor(x, GROUP_BANK[:, :], x, ALU.add).then_inc(bank_read[name], 1)

            attention_loop(dve, body)

        @block.tensor
        def _(pe):
            pe.wait_ge(load_small, 48)
            pe.wait_ge(load_w, 16)
            nc.tensor.transpose(PS[0][:, 0:B], condr[:, :], ident[0:B, 0:B]).then_inc(setup_pe, 1)
            pe.wait_ge(setup_act, 1)
            for k in range(6):
                nc.tensor.matmul(PS[1][:, k * B:(k + 1) * B], w("mod", k * P, P), condS[:, :], start=True, stop=True)
            nc.tensor.matmul(PS[1][:, 6 * B:6 * B + 1], w("proj"), vec("bv"), start=True, stop=True)
            nc.tensor.matmul(PS[1][:, 6 * B + 1:6 * B + 2], w("cproj"), vec("bvc"), start=True, stop=True)\
                .then_inc(setup_pe, 1)
            pe.wait_ge(setup_dve, 3)
            pe.wait_ge(consts, 32)

            def body(ev):
                name = ev[0]
                if name == "score":
                    _, c, u = ev
                    e, lo = u // 2, (u % 2) * 4
                    if u == 0 and c.b == 0:
                        pe.wait_ge(stacked[c.kind], STACK_DMAS * (c.group + 1))
                    if not isinstance(c.n, int) or 4 * c.n + u > 1:
                        pe.wait_ge(max_done, 4 * c.n + (u - 1))
                    for j in range(4):
                        rows, cols = slice(64 * e, 64 * e + 64), slice(c.b * P, (c.b + 1) * P)
                        last = nc.tensor.matmul(S_BANK[u % 2][:, j * P:(j + 1) * P], Qs[c.kind][rows, lo + j, cols],
                                                Ks[c.kind][rows, lo + j, cols], start=True, stop=True)
                    last.then_inc(score_done, 1)
                elif name == "shifted":
                    _, c, u = ev
                    e, lo = u // 2, (u % 2) * 4
                    if u == 0:
                        pe.wait_ge(max_rows, 16 * (c.n + 1))
                    if not isinstance(c.n, int) or 4 * c.n + u > 1:
                        pe.wait_ge(exp_done, 4 * c.n + (u - 1))
                    for j in range(4):
                        rows, cols = slice(64 * e, 64 * e + 64), slice(c.b * P, (c.b + 1) * P)
                        last = nc.tensor.matmul(T_BANK[u % 2][:, j * P:(j + 1) * P], Ks[c.kind][rows, lo + j, cols],
                                                Qs[c.kind][rows, lo + j, cols], start=True, stop=True)
                    last.then_inc(shifted_done, 1)
                elif name == "value":
                    _, c, u = ev
                    pe.wait_ge(exp_done, 4 * c.n + (u + 1))
                    if u == 0:
                        if not isinstance(c.n, int) or c.n > 0:
                            pe.wait_ge(o_copied, c.n)
                        if c.b == 0:
                            pe.wait_ge(bank_read["v_s" if c.kind == 0 else "v_c"], c.group + 1)
                    for j in range(4):
                        last = nc.tensor.matmul(O_BANK[32 * j:32 * j + 32, u * P:(u + 1) * P],
                                                Va[c.kind][:, c.b, 4 * u + j, :], PR[:, u, j * P:(j + 1) * P],
                                                start=True, stop=True)
                    last.then_inc(value_done, 1)
                elif name == "max_turn":
                    _, c, stored = ev
                    pe.wait_ge(max_parts, c.n + 1)
                    if not isinstance(c.n, int) or stored > 0:
                        pe.wait_ge(o_stored, stored)
                    if isinstance(c.n, int) and c.n > 0:
                        pe.wait_ge(max_copied, c.n)
                    nc.tensor.transpose(SMALL_BANK[0:32, 0:P // 2].bitcast(BF16),
                                        M2[:, c.mod % 2, :, :, :].rearrange("p e t j -> p (e t j)"), identb[:, :])\
                        .then_inc(max_turned, 1)
                elif name == "o_turn":
                    c = ev[1]
                    pe.wait_ge(o_copied, c.n + 1)
                    if not isinstance(c.n, int) or c.n > 0:
                        pe.wait_ge(o_normed, c.n)
                    for u in range(4):
                        last = nc.tensor.transpose(TURN_BANK[:, u * P:(u + 1) * P], OTs[:, u * P:(u + 1) * P],
                                                   ident[:, :])
                    last.then_inc(o_turned, 1)
                elif name == "o_back":
                    _, c, copied = ev
                    pe.wait_ge(o_normed, c.n + 1)
                    pe.wait_ge(max_copied, copied)
                    if isinstance(c.n, int) and c.n > 0:
                        pe.wait_ge(o_stored, c.n)
                    nc.tensor.transpose(SMALL_BANK[:, 0:P], On[:, c.mod % 2, :], ident[:, :]).then_inc(o_backed, 1)
                elif name == "fill":
                    _, name, g, before, last_core = ev
                    if before is not None:
                        pe.wait_ge(bank_read[before[0]], before[1] + 1)
                    if name in ("xt_s", "xt_x", "xt_c"):
                        k = LN_KIND[name]
                        pe.wait_ge(ln_done[k], g + 1)
                        for b in range(GB):
                            last = nc.tensor.transpose(GROUP_BANK[:, b * P:(b + 1) * P], XN[k][:, b * P:(b + 1) * P],
                                                       ident[:, :])
                    elif name in PARTS:
                        last = nc.tensor.matmul(GROUP_BANK[:, :], w(WEIGHT[name]), XT[SOURCE[name]][:, :],
                                                start=True, stop=True)
                    elif name in ("v_s", "v_c"):
                        for b in range(GB):
                            last = nc.tensor.matmul(GROUP_BANK[:, b * P:(b + 1) * P],
                                                    XT[SOURCE[name]][:, b * P:(b + 1) * P], w(WEIGHT[name]),
                                                    start=True, stop=True)
                    elif name in ("proj_s", "proj_c"):
                        pe.wait_ge(o_stored, last_core.n + 1)
                        last = nc.tensor.matmul(GROUP_BANK[:, :], w(WEIGHT[name]), OgT[KIND[name]][:, :],
                                                start=True, stop=True)
                    else:
                        for b in range(GB):
                            last = nc.tensor.transpose(GROUP_BANK[:, b * P:(b + 1) * P],
                                                       YT[KIND[name]][:, b * P:(b + 1) * P], ident[:, :])
                    last.then_inc(bank_filled[name], 1)

            attention_loop(pe, body)

        attention_memory.close()
        mlp_and_router(nc, stack, X, ctxin, w, vec, rows1, condT, mod, gbm, half, ident, PS, load_w2, out)


MLP_STEPS = (
    ("stats", 2, 0), ("xt", 1, 0),
    ("second", -1, 0), ("first", 0, 0), ("second", -1, 1), ("first", 0, 1),
    ("turn_back", -2, 0), ("norm", 2, 0), ("first", 0, 2), ("first", 0, 3), ("xt_read", 1, 0),
    ("second", -1, 2), ("gelu", 0, 2), ("second", -1, 3), ("gelu", 0, 3), ("gate", -1, 0),
)
ROUTER_STEPS = (
    ("hidden", 0, 0), ("ctx_turn", 1, 0),
    ("hidden", 0, 1), ("keys", 1, 0),
    ("hidden", 0, 2), ("nx_turn", 1, 0),
    ("hidden", 0, 3), ("scores", 1, 0),
    ("hidden", 0, 4), ("exp", 1, 0), ("probs", 0, 0), ("weigh", 1, 0),
    ("hidden", 0, 5), ("hidden", 0, 6),
    ("expert", 0, 0), ("gate", 0, 0), ("w_turn", 1, 0),
    ("expert", 0, 1), ("evidence", 1, 0),
    ("expert", 0, 2), ("load", 2, 0), ("stats", 2, 0),
    ("expert", 0, 3), ("logits", 1, 0), ("norm", 2, 0), ("finish", 0, 0),
)
NE = 3
NHC = 7
EH = 2 * NE


def over_groups(eng, steps, body):
    lags = [lag for _, lag, _ in steps]
    steady = range(1 - min(lags), NG - max(lags))

    def iteration(i, all_valid):
        for name, lag, k in steps:
            if all_valid or 0 <= i + lag < NG:
                body(name, i + lag, k)

    for i in range(-max(lags), steady.start):
        iteration(i, False)
    with eng.Fori(steady.start, steady.stop) as i:
        iteration(i, True)
    for i in range(steady.stop, NG - min(lags)):
        iteration(i, False)


def later(g):
    return not isinstance(g, int) or g > 0


def mlp_and_router(nc, stack, X, ctxin, w, vec, rows1, condT, mod, gbm, half, ident, PS, load_w2, out):
    def sb(name, shape, dt=F32):
        return stack.enter_context(nc.sbuf_tensor(name, shape, dt))

    def sem(name):
        return stack.enter_context(nc.semaphore(name))

    seen = sb("seen2", [P, 1])
    XN = sb("m_XN", [P, GT])
    XT = sb("m_XT", [P, GT])
    H = sb("m_H", [P, 4, GT])
    YT = sb("m_YT", [P, GT])
    stat = sb("m_stat", [P, 2, GB, 6])
    mv = sb("m_mv", [P, 2, GB, 2])
    eps = sb("m_eps", [P, 2, GB])
    veps = sb("m_veps", [P, 2, GB])
    rstd = sb("m_rstd", [P, 2, GB])
    ones = sb("ones", [B, P])
    A = sb("A", [P, P])
    KEYS = sb("KEYS", [P, GT])
    REV = sb("REV", [P, NE])
    U = sb("U", [P, NHC * P])
    WO = sb("WO", [P, EH * P])
    ANC = sb("ANC", [P, NHC, B])
    BO = sb("BO", [P, GT])
    LOG32 = sb("LOG32", [B, NE])
    MASKED = sb("MASKED", [B, B, NE])
    RA = sb("RA", [P, B, NE])
    CTX = sb("r_CTX", [P, GB, P])
    CTXT = sb("r_CTXT", [P, GT])
    RXN = sb("r_XN", [P, GT])
    NXA = sb("r_NXA", [P, GT])
    NXH = sb("r_NXH", [P, GT])
    nothing = sb("nothing", [P, GT])
    E = sb("r_E", [P, GB, P])
    WN = sb("r_WN", [P, GB, P])
    WT = sb("r_WT", [P, GT])
    EV = sb("r_EV", [P, GT])
    HID = sb("r_HID", [P, NHC, GT])
    nmax = sb("r_nmax", [P, GB])
    nbias = sb("r_nbias", [P, GB])
    esum = sb("r_esum", [P, GB])
    rsum = sb("r_rsum", [P, GB])
    LG = sb("r_LG", [P, GB, NE])
    lmax = sb("r_lmax", [P, GB])
    LS = sb("r_LS", [P, GB, NE])
    LE = sb("r_LE", [P, GB, NE])
    lsum = sb("r_lsum", [P, GB])
    lrec = sb("r_lrec", [P, GB])
    RP = sb("r_RP", [P, GB, NE])
    T = sb("r_T", [P, 2, NE * P])
    R = sb("r_R", [P, GB, P])
    GS = sb("r_GS", [P, GT])
    GTH = sb("r_GTH", [P, GT])
    D = sb("r_D", [P, GT])

    XT_BANK, FIRST_BANK, SECOND_BANK, BACK_BANK = PS[0], PS[1:5], PS[5], PS[6]
    HIDDEN_BANK, EXPERT_BANK, GATE_BANK, EVIDENCE_BANK, SCORE_BANK = PS[0:2], PS[2:4], PS[4], PS[5], PS[6:8]

    fills = sem("fills")
    d_stat = [sem(f"{k}_stat") for k in "mr"]
    d_mv = [sem(f"{k}_mv") for k in "mr"]
    d_var = [sem(f"{k}_var") for k in "mr"]
    d_rstd = [sem(f"{k}_rstd") for k in "mr"]
    d_norm = [sem(f"{k}_norm") for k in "mr"]
    xt_turned = sem("xt_turned")
    xt_read = sem("xt_read")
    first_done = sem("first_done")
    gelu_done = sem("gelu_done")
    second_done = sem("second_done")
    gated = sem("gated")
    turned_back = sem("turned_back")
    x_added = sem("x_added")
    derived_pe = sem("derived_pe")
    derived_act = sem("derived_act")
    derived_dve = sem("derived_dve")
    ctx_in = sem("ctx_in")
    ctx_turned = sem("ctx_turned")
    ctx_read = sem("ctx_read")
    keys_done = sem("keys_done")
    keys_read = sem("keys_read")
    nx_turned = sem("nx_turned")
    nx_read = sem("nx_read")
    nx_kept = sem("nx_kept")
    scores_done = sem("scores_done")
    nmax_done = sem("nmax_done")
    nbias_done = sem("nbias_done")
    exps_done = sem("exps_done")
    rsum_done = sem("rsum_done")
    weights_done = sem("weights_done")
    w_turned = sem("w_turned")
    w_read = sem("w_read")
    evidence_done = sem("evidence_done")
    evidence_read = sem("evidence_read")
    logits_done = sem("logits_done")
    logits_read = sem("logits_read")
    lmax_done = sem("lmax_done")
    lshift_done = sem("lshift_done")
    lexp_done = sem("lexp_done")
    lsum_done = sem("lsum_done")
    lrec_done = sem("lrec_done")
    probs_done = sem("probs_done")
    hidden_done = sem("hidden_done")
    silu_done = sem("silu_done")
    expert_done = sem("expert_done")
    expert_read = sem("expert_read")
    routed = sem("routed")
    gate_done = sem("gate_done")
    gate_read = sem("gate_read")
    gate_tanh = sem("gate_tanh")
    delta_done = sem("delta_done")
    finished = sem("finished")
    out_done = sem("out_done")

    def x_batch(g, b):
        return X[:, bass.ds(g * GT + b * P, P)]

    def score_view(h):
        return SCORE_BANK[h][:, 0:2 * P].rearrange("p (b k) -> p b k", b=2)

    def logit_view(h):
        return SCORE_BANK[h][:, 2 * P:2 * P + 2 * NE].rearrange("p (b e) -> p b e", b=2)

    block = stack.enter_context(nc.Block())

    @block.sync
    def _(sp):
        def body(name, g, k):
            if name == "load":
                if later(g):
                    sp.wait_ge(evidence_done, g)
                sp.dma_start(CTX[:, :, :], ctxin[bass.ds(g * GB, GB)].rearrange("b p h -> p b h"))\
                    .then_inc(ctx_in, 16)
            elif name == "finish":
                sp.wait_ge(finished, g + 1)
                sp.dma_start(out[bass.ds(g * GB, GB)].rearrange("b p h -> p b h"),
                             X[:, bass.ds(g * GT, GT)].rearrange("p (b h) -> p b h", b=GB)).then_inc(out_done, 16)

        over_groups(sp, ROUTER_STEPS, body)
        sp.wait_ge(out_done, 16 * NG)

    @block.gpsimd
    def _(pool):
        nc.gpsimd.memset(ones[:, :], 1.0)
        nc.gpsimd.memset(eps[:, 0, :], 1e-6)
        nc.gpsimd.memset(eps[:, 1, :], 1e-5)
        nc.gpsimd.memset(nothing[:, :], 0.0).then_inc(fills, 1)
        pool.wait_ge(fills, 1)

        def inverse_deviation(s, g):
            pool.wait_ge(d_mv[s], g + 1)
            nc.gpsimd.tensor_tensor(veps[:, s, :], mv[:, s, :, 1], eps[:, s, :], ALU.add).then_inc(d_var[s], 1)
            pool.wait_ge(d_var[s], g + 1)
            nc.gpsimd.tensor_tensor(rstd[:, s, :], veps[:, s, :], half[:, :], ALU.pow).then_inc(d_rstd[s], 1)

        def mlp(name, g, k):
            if name == "stats":
                inverse_deviation(0, g)

        def router(name, g, k):
            if name == "stats":
                inverse_deviation(1, g)
            elif name == "w_turn":
                pool.wait_ge(nx_read, g + 1)
                if later(g):
                    pool.wait_ge(hidden_done, NHC * g)
                nc.gpsimd.tensor_tensor(NXH[:, :], NXA[:, :], nothing[:, :], ALU.add).then_inc(nx_kept, 1)

        over_groups(pool, MLP_STEPS, mlp)
        over_groups(pool, ROUTER_STEPS, router)

    @block.scalar
    def _(act):
        act.wait_ge(derived_pe, 2)
        for c in range(NHC):
            bias = vec("be1", c) if c < EH else vec("bg1")
            last = nc.scalar.activation(ANC[:, c, :], PS[5][:, c * B:(c + 1) * B], ACT.Identity, bias=bias)
        nc.scalar.activation(U[:, 0:GT], PS[1][:, :], ACT.Copy)
        nc.scalar.activation(U[:, GT:NHC * P], PS[2][:, 0:NHC * P - GT], ACT.Copy).then_inc(derived_act, 1)

        def gelu(g, k):
            act.wait_ge(first_done, 4 * g + (k + 1))
            if later(g):
                act.wait_ge(second_done, 4 * g + (k - 3))
            nc.scalar.activation(H[:, k, :], FIRST_BANK[k][:, :], ACT.Gelu_apprx_tanh, bias=vec("bmlp1", k))\
                .then_inc(gelu_done, 1)

        def mlp(name, g, k):
            if name == "first" and k < 2 or name == "gelu":
                gelu(g, k)
            elif name == "xt_read":
                act.wait_ge(xt_turned, g + 1)
                if later(g):
                    act.wait_ge(first_done, 4 * g)
                for b in range(GB):
                    nb = bass.ds(g * GB + b, 1)
                    last = nc.scalar.activation(XT[:, b * P:(b + 1) * P], XT_BANK[:, b * P:(b + 1) * P],
                                                ACT.Identity, scale=mod[:, 4, nb], bias=mod[:, 3, nb])
                last.then_inc(xt_read, 1)

        def router(name, g, k):
            if name == "hidden":
                act.wait_ge(hidden_done, NHC * g + (k + 1))
                for b in range(GB):
                    last = nc.scalar.activation(HID[:, k, b * P:(b + 1) * P], HIDDEN_BANK[k % 2][:, b * P:(b + 1) * P],
                                                ACT.Silu, bias=ANC[:, k, bass.ds(g * GB + b, 1)])
                last.then_inc(silu_done, 1)
            elif name == "ctx_turn":
                act.wait_ge(ctx_turned, g + 1)
                nc.scalar.activation(CTXT[:, :], EVIDENCE_BANK[:, :], ACT.Copy).then_inc(ctx_read, 1)
            elif name == "nx_turn":
                act.wait_ge(nx_turned, g + 1)
                if later(g):
                    act.wait_ge(nx_kept, g)
                nc.scalar.activation(NXA[:, :], EVIDENCE_BANK[:, :], ACT.Identity, scale=vec("gamma"),
                                     bias=vec("beta")).then_inc(nx_read, 1)
            elif name == "exp":
                act.wait_ge(nbias_done, g + 1)
                if later(g):
                    act.wait_ge(weights_done, g)
                for b in range(GB):
                    last = nc.scalar.activation(E[:, b, :], score_view(b // 2)[:, b % 2, :], ACT.Exp,
                                                scale=SCALE1, bias=nbias[:, b:b + 1], accum_out=esum[:, b:b + 1])
                last.then_inc(exps_done, 1)
            elif name == "probs":
                act.wait_ge(lshift_done, g + 1)
                if later(g):
                    act.wait_ge(probs_done, g)
                nc.scalar.activation(LE[:, :, :], LS[:, :, :], ACT.Exp).then_inc(lexp_done, 1)
            elif name == "w_turn":
                act.wait_ge(w_turned, g + 1)
                nc.scalar.activation(WT[:, :], EVIDENCE_BANK[:, :], ACT.Copy).then_inc(w_read, 1)
            elif name == "gate":
                act.wait_ge(gate_read, g + 1)
                if later(g):
                    act.wait_ge(delta_done, g)
                nc.scalar.activation(GTH[:, :], GS[:, :], ACT.Tanh, scale=0.5).then_inc(gate_tanh, 1)

        over_groups(act, MLP_STEPS, mlp)
        over_groups(act, ROUTER_STEPS, router)

    @block.vector
    def _(dve):
        dve.wait_ge(derived_pe, 1)
        nc.vector.tensor_copy(LOG32[:, :], PS[0][0:B, 2 * P:2 * P + NE]).then_inc(derived_dve, 1)
        dve.wait_ge(derived_dve, 1)
        nc.vector.tensor_tensor(MASKED[:, :, :], ident[0:B, 0:B].unsqueeze(2).to_broadcast([B, B, NE]),
                                LOG32[:, :].unsqueeze(1).to_broadcast([B, B, NE]), ALU.mult).then_inc(derived_dve, 1)
        nc.vector.tensor_copy(A[:, :], PS[0][:, 0:P])
        nc.vector.tensor_copy(REV[:, :], PS[0][:, P:P + NE])
        dve.wait_ge(derived_pe, 2)
        nc.vector.tensor_copy(WO[:, 0:GT], PS[3][:, :])
        nc.vector.tensor_copy(WO[:, GT:EH * P], PS[4][:, 0:EH * P - GT])
        nc.vector.tensor_copy(BO[:, :], PS[6][:, :])
        dve.wait_ge(derived_pe, 3)
        nc.vector.tensor_copy(RA[:, :, :], PS[7][:, 0:NE * B].rearrange("p (b e) -> p b e", e=NE))\
            .then_inc(derived_dve, 1)

        def statistics(s, g):
            for b in range(GB):
                last = nc.vector.bn_stats(stat[:, s, b, :], x_batch(g, b))
            last.then_inc(d_stat[s], 1)
            dve.wait_ge(d_stat[s], g + 1)
            nc.vector.tensor_copy(seen[:, :], stat[:, s, GB - 1, 0:1])
            for b in range(GB):
                last = nc.vector.bn_aggr(mv[:, s, b, :], stat[:, s, b, :])
            last.then_inc(d_mv[s], 1)

        def normalise(s, g, to, turned):
            dve.wait_ge(d_rstd[s], g + 1)
            if later(g):
                dve.wait_ge(turned, g)
            for b in range(GB):
                last = nc.vector.tensor_scalar(to[:, b * P:(b + 1) * P], x_batch(g, b), mv[:, s, b, 0:1],
                                               rstd[:, s, b:b + 1], ALU.subtract, ALU.mult)
            last.then_inc(d_norm[s], 1)

        def mlp(name, g, k):
            if name == "stats":
                statistics(0, g)
            elif name == "norm":
                normalise(0, g, XN, xt_turned)
            elif name == "gate":
                dve.wait_ge(second_done, 4 * g + 4)
                if later(g):
                    dve.wait_ge(turned_back, g)
                for b in range(GB):
                    nb = bass.ds(g * GB + b, 1)
                    last = nc.vector.tensor_scalar(YT[:, b * P:(b + 1) * P], SECOND_BANK[:, b * P:(b + 1) * P],
                                                   mod[:, 5, nb], gbm[:, nb], ALU.mult, ALU.add)
                last.then_inc(gated, 1)
            elif name == "turn_back":
                x = X[:, bass.ds(g * GT, GT)]
                dve.wait_ge(turned_back, g + 1)
                nc.vector.tensor_tensor(x, BACK_BANK[:, :], x, ALU.add).then_inc(x_added, 1)

        def router(name, g, k):
            if name == "stats":
                statistics(1, g)
            elif name == "norm":
                normalise(1, g, RXN, nx_turned)
            elif name == "keys":
                dve.wait_ge(keys_done, g + 1)
                nc.vector.tensor_copy(KEYS[:, :], EVIDENCE_BANK[:, :]).then_inc(keys_read, 1)
            elif name == "scores":
                dve.wait_ge(scores_done, g + 1)
                for h in range(2):
                    last = nc.vector.tensor_reduce(out=nmax[:, 2 * h:2 * h + 2], in_=score_view(h),
                                                   axis=AX.X, op=ALU.max, negate=True)
                last.then_inc(nmax_done, 1)
                dve.wait_ge(nmax_done, g + 1)
                nc.vector.tensor_scalar(nbias[:, :], nmax[:, :], SCALE1, None, ALU.mult).then_inc(nbias_done, 1)
            elif name == "probs":
                dve.wait_ge(lexp_done, g + 1)
                nc.vector.tensor_reduce(out=lsum[:, :], in_=LE[:, :, :], axis=AX.X, op=ALU.add)\
                    .then_inc(lsum_done, 1)
                dve.wait_ge(lsum_done, g + 1)
                nc.vector.reciprocal(lrec[:, :], lsum[:, :]).then_inc(lrec_done, 1)
                dve.wait_ge(lrec_done, g + 1)
                nc.vector.scalar_tensor_tensor(RP[:, :, :], LE[:, :, :], 0.5,
                                               lrec[:, :].unsqueeze(2).to_broadcast([P, GB, NE]), ALU.mult,
                                               ALU.mult).then_inc(probs_done, 1)
                dve.wait_ge(probs_done, g + 1)
            elif name == "weigh":
                dve.wait_ge(exps_done, g + 1)
                nc.vector.reciprocal(rsum[:, :], esum[:, :]).then_inc(rsum_done, 1)
                dve.wait_ge(rsum_done, g + 1)
                nc.vector.tensor_tensor(WN[:, :, :], E[:, :, :], rsum[:, :].unsqueeze(2).to_broadcast([P, GB, P]),
                                        ALU.mult).then_inc(weights_done, 1)
            elif name == "evidence":
                dve.wait_ge(evidence_done, g + 1)
                nc.vector.tensor_copy(EV[:, :], EVIDENCE_BANK[:, :]).then_inc(evidence_read, 1)
            elif name == "logits":
                dve.wait_ge(logits_done, g + 1)
                for h in range(2):
                    last = nc.vector.tensor_tensor(LG[:, 2 * h:2 * h + 2, :], logit_view(h),
                                                   RA[:, bass.ds(g * GB + 2 * h, 2), :], ALU.add)
                last.then_inc(logits_read, 1)
                dve.wait_ge(logits_read, g + 1)
                nc.vector.tensor_reduce(out=lmax[:, :], in_=LG[:, :, :], axis=AX.X, op=ALU.max)\
                    .then_inc(lmax_done, 1)
                dve.wait_ge(lmax_done, g + 1)
                nc.vector.tensor_tensor(LS[:, :, :], LG[:, :, :], lmax[:, :].unsqueeze(2).to_broadcast([P, GB, NE]),
                                        ALU.subtract).then_inc(lshift_done, 1)
            elif name == "gate":
                dve.wait_ge(gate_done, g + 1)
                if later(g):
                    dve.wait_ge(gate_tanh, g)
                gate_bias = BO[:, NE * P:GT].unsqueeze(1).to_broadcast([P, GB, P])
                nc.vector.tensor_tensor(GS[:, :].rearrange("p (b c) -> p b c", b=GB),
                                        GATE_BANK[:, :].rearrange("p (b c) -> p b c", b=GB), gate_bias, ALU.add)\
                    .then_inc(gate_read, 1)
            elif name == "expert":
                b, t = k, T[:, k % 2, :]
                dve.wait_ge(expert_done, GB * g + (b + 1))
                nc.vector.tensor_tensor(t, EXPERT_BANK[b % 2][:, 0:NE * P], BO[:, 0:NE * P], ALU.add)\
                    .then_inc(expert_read, 1)
                dve.wait_ge(expert_read, GB * g + (b + 1))
                nc.vector.tensor_scalar(R[:, b, :], t[:, 0:P], RP[:, b, 0:1], None, ALU.mult).then_inc(routed, 1)
                for e in range(1, NE):
                    dve.wait_ge(routed, NE * GB * g + (NE * b + e))
                    nc.vector.scalar_tensor_tensor(R[:, b, :], t[:, e * P:(e + 1) * P], RP[:, b, e:e + 1], R[:, b, :],
                                                   ALU.mult, ALU.add).then_inc(routed, 1)
            elif name == "finish":
                x = X[:, bass.ds(g * GT, GT)]
                dve.wait_ge(routed, NE * GB * g + NE * GB)
                dve.wait_ge(gate_tanh, g + 1)
                nc.vector.scalar_tensor_tensor(D[:, :], GTH[:, :], 1.0, R[:, :, :].rearrange("p b c -> p (b c)"),
                                               ALU.add, ALU.mult).then_inc(delta_done, 1)
                dve.wait_ge(delta_done, g + 1)
                nc.vector.tensor_tensor(x, D[:, :], x, ALU.add).then_inc(finished, 1)

        over_groups(dve, MLP_STEPS, mlp)
        dve.wait_ge(x_added, NG)
        over_groups(dve, ROUTER_STEPS, router)

    @block.tensor
    def _(pe):
        def product(to, lhsT, rhs, start=True, stop=True):
            return nc.tensor.matmul(to, lhsT, rhs, start=start, stop=stop)

        pe.wait_ge(load_w2, 32)
        pe.wait_ge(fills, 1)
        product(PS[0][:, 0:P], w("wkT"), w("wqT"))
        product(PS[0][:, P:P + NE], w("wvT"), w("r_ev"))
        product(PS[0][0:B, 2 * P:2 * P + NE], condT[:, :], w("r_an"), stop=False)
        product(PS[0][0:B, 2 * P:2 * P + NE], ones[0:1, 0:B], rows1[0:1, 2 * P:2 * P + NE], start=False)\
            .then_inc(derived_pe, 1)
        product(PS[1][:, :], w("wvT"), w("e_ev", 0, GT))
        product(PS[2][:, 0:EH * P - GT], w("wvT"), w("e_ev", GT, EH * P - GT))
        product(PS[2][:, EH * P - GT:NHC * P - GT], w("wvT"), w("g_ev"))
        for c in range(NHC):
            product(PS[5][:, c * B:(c + 1) * B], w("e_an", c * P, P) if c < EH else w("g_an"), condT[:, :])
        for c in range(EH):
            product(PS[3 + c // 4][:, (c % 4) * P:(c % 4 + 1) * P], w("e2T", c * P, P), w("outw"))
        for e in range(NE):
            product(PS[6][:, e * P:(e + 1) * P], vec("be2", e).to_broadcast([P, P]), w("outw"), stop=False)
            product(PS[6][:, e * P:(e + 1) * P], ones[0:1, :], rows1[0:1, 0:P], start=False)
        product(PS[6][:, NE * P:GT], ones[0:1, :], rows1[0:1, P:2 * P]).then_inc(derived_pe, 1)
        pe.wait_ge(derived_dve, 2)
        product(PS[7][:, 0:NE * B], ones[:, :], MASKED[:, :, :].rearrange("p b e -> p (b e)"))\
            .then_inc(derived_pe, 1)
        pe.wait_ge(derived_act, 1)
        pe.wait_ge(derived_dve, 3)

        def turn(bank, source):
            for b in range(GB):
                last = nc.tensor.transpose(bank[:, b * P:(b + 1) * P], source(b), ident[:, :])
            return last

        def mlp(name, g, k):
            if name == "xt":
                pe.wait_ge(d_norm[0], g + 1)
                if later(g):
                    pe.wait_ge(xt_read, g)
                turn(XT_BANK, lambda b: XN[:, b * P:(b + 1) * P]).then_inc(xt_turned, 1)
            elif name == "first":
                if k == 0:
                    pe.wait_ge(xt_read, g + 1)
                if later(g):
                    pe.wait_ge(gelu_done, 4 * g + (k - 3))
                product(FIRST_BANK[k][:, :], w("mlp1", k * P, P), XT[:, :]).then_inc(first_done, 1)
            elif name == "second":
                if k == 0 and later(g):
                    pe.wait_ge(gated, g)
                pe.wait_ge(gelu_done, 4 * g + (k + 1))
                product(SECOND_BANK[:, :], w("mlp2", k * P, P), H[:, k, :], start=k == 0, stop=k == 3)\
                    .then_inc(second_done, 1)
            elif name == "turn_back":
                pe.wait_ge(gated, g + 1)
                if later(g):
                    pe.wait_ge(x_added, g)
                turn(BACK_BANK, lambda b: YT[:, b * P:(b + 1) * P]).then_inc(turned_back, 1)

        def router(name, g, k):
            if name == "ctx_turn":
                pe.wait_ge(ctx_in, 16 * (g + 1))
                if later(g):
                    pe.wait_ge(evidence_read, g)
                turn(EVIDENCE_BANK, lambda b: CTX[:, b, :]).then_inc(ctx_turned, 1)
            elif name == "keys":
                pe.wait_ge(ctx_read, g + 1)
                product(EVIDENCE_BANK[:, :], A[:, :], CTXT[:, :]).then_inc(keys_done, 1)
            elif name == "nx_turn":
                pe.wait_ge(d_norm[1], g + 1)
                pe.wait_ge(keys_read, g + 1)
                turn(EVIDENCE_BANK, lambda b: RXN[:, b * P:(b + 1) * P]).then_inc(nx_turned, 1)
            elif name == "scores":
                pe.wait_ge(nx_read, g + 1)
                if later(g):
                    pe.wait_ge(logits_read, g)
                for b in range(GB):
                    last = product(score_view(b // 2)[:, b % 2, :], NXA[:, b * P:(b + 1) * P],
                                   KEYS[:, b * P:(b + 1) * P])
                last.then_inc(scores_done, 1)
            elif name == "w_turn":
                pe.wait_ge(weights_done, g + 1)
                turn(EVIDENCE_BANK, lambda b: WN[:, b, :]).then_inc(w_turned, 1)
            elif name == "evidence":
                pe.wait_ge(w_read, g + 1)
                for b in range(GB):
                    last = product(EVIDENCE_BANK[:, b * P:(b + 1) * P], CTX[:, b, :], WT[:, b * P:(b + 1) * P])
                last.then_inc(evidence_done, 1)
            elif name == "logits":
                pe.wait_ge(evidence_read, g + 1)
                for b in range(GB):
                    to, batch = logit_view(b // 2)[:, b % 2, :], slice(b * P, (b + 1) * P)
                    product(to, NXA[:, batch], w("r_nx"), stop=False)
                    last = product(to, EV[:, batch], REV[:, :], start=False)
                last.then_inc(logits_done, 1)
            elif name == "hidden":
                if k == 0:
                    pe.wait_ge(nx_kept, g + 1)
                    pe.wait_ge(evidence_read, g + 1)
                if k > 1:
                    pe.wait_ge(silu_done, NHC * g + (k - 1))
                elif later(g):
                    pe.wait_ge(silu_done, NHC * g)
                nx = w("e_nx", k * P, P) if k < EH else w("g_nx")
                product(HIDDEN_BANK[k % 2][:, :], nx, NXH[:, :], stop=False)
                product(HIDDEN_BANK[k % 2][:, :], U[:, k * P:(k + 1) * P], EV[:, :], start=False)\
                    .then_inc(hidden_done, 1)
            elif name == "expert":
                b = k
                if b == 0:
                    pe.wait_ge(silu_done, NHC * g + EH)
                if b > 1 or later(g):
                    pe.wait_ge(expert_read, GB * g + (b - 1))
                for e in range(NE):
                    for c in range(2):
                        last = product(EXPERT_BANK[b % 2][:, e * P:(e + 1) * P],
                                       HID[:, 2 * e + c, b * P:(b + 1) * P],
                                       WO[:, (2 * e + c) * P:(2 * e + c + 1) * P], start=c == 0, stop=c == 1)
                last.then_inc(expert_done, 1)
            elif name == "gate":
                pe.wait_ge(silu_done, NHC * g + NHC)
                if later(g):
                    pe.wait_ge(gate_read, g)
                for b in range(GB):
                    last = product(GATE_BANK[:, b * P:(b + 1) * P], HID[:, EH, b * P:(b + 1) * P], w("gate2"))
                last.then_inc(gate_done, 1)

        over_groups(pe, MLP_STEPS, mlp)
        pe.wait_ge(gelu_done, 4 * NG)
        pe.wait_ge(x_added, NG)
        over_groups(pe, ROUTER_STEPS, router)


_OUT = ((B, P, P), "float32")


def head_channel_last_to_stack(a):
    n = a.shape[0]
    return a.reshape(n, 2, NJ, HD).transpose(0, 1, 3, 2).reshape(n, P)


def rows_of_chunks(a):
    k, n = a.shape[0] // P, a.shape[1]
    return a.reshape(k, P, n).transpose(1, 0, 2).reshape(P, k * n)


def pack(inputs):
    import numpy as np
    a = {k: np.asarray(v) for k, v in inputs.items()}
    l0 = {k[9:]: v for k, v in a.items() if k.startswith("L0_")}
    l1 = {k[9:]: v for k, v in a.items() if k.startswith("L1_")}
    qkv, kvc = l0["W_qkv"], l0["W_kvc"]
    ew1, gw1, rw = l1["e_w1"], l1["gate_w1"], l1["router_W"]

    def experts(lo):
        return ew1[:, lo:lo + P, :].transpose(1, 0, 2).reshape(P, -1)

    w = {
        "mod": l0["W_mod"],
        "q": head_channel_last_to_stack(qkv[:, 0:P]), "k": head_channel_last_to_stack(qkv[:, P:2 * P]),
        "v": qkv[:, 2 * P:], "proj": l0["W_proj"],
        "qc": head_channel_last_to_stack(l0["W_qc"]), "kc": head_channel_last_to_stack(kvc[:, 0:P]),
        "vc": kvc[:, P:], "cproj": l0["W_cproj"],
        "mlp1": l0["W_mlp1"], "mlp2": rows_of_chunks(l0["W_mlp2"]),
        "wqT": l1["Wq"].T, "wkT": l1["Wk"].T, "wvT": l1["Wv"].T,
        "r_nx": rw[0:P], "r_ev": rw[P:2 * P], "r_an": rw[2 * P:],
        "e_nx": experts(0), "g_nx": gw1[0:P], "e_ev": experts(P), "g_ev": gw1[P:2 * P],
        "e_an": experts(2 * P), "g_an": gw1[2 * P:], "gate2": l1["gate_w2"],
        "e2T": l1["e_w2"].transpose(2, 0, 1).reshape(P, -1), "outw": l1["out_w"],
    }
    bq = l0["b_qkv"]
    v = {
        "bmod": l0["b_mod"].reshape(6, P).T,
        "bq": head_channel_last_to_stack(bq[None, 0:P]).T, "bk": head_channel_last_to_stack(bq[None, P:2 * P]).T,
        "bv": bq[2 * P:, None], "bproj": l0["b_proj"][:, None],
        "bqc": head_channel_last_to_stack(l0["b_qc"][None]).T,
        "bkc": head_channel_last_to_stack(l0["b_kvc"][None, 0:P]).T, "bvc": l0["b_kvc"][P:, None],
        "bcproj": l0["b_cproj"][:, None], "bmlp1": l0["b_mlp1"].reshape(4, P).T, "bmlp2": l0["b_mlp2"][:, None],
        "gamma": l1["ln_gamma"][:, None], "beta": l1["ln_beta"][:, None],
        "be1": l1["e_b1"].reshape(6, P).T, "bg1": l1["gate_b1"][:, None], "be2": l1["e_b2"].T,
    }
    rows = np.concatenate([l1["out_b"], l1["gate_b2"], l1["router_b"]])[None]
    return {
        "x": a["x"], "cond": a["cond_1024"], "ctx": a["ctx_1024"],
        "weights": np.ascontiguousarray(np.concatenate([w[k] for k in W_COLS], axis=1)),
        "vectors": np.ascontiguousarray(np.concatenate([v[k] for k in V_COLS], axis=1)),
        "ident": np.eye(P, dtype=np.float32), "rows": np.ascontiguousarray(rows),
    }


def kernel(**inputs):
    import concourse.bacc as bacc
    from concourse.bass_utils import run_bass_kernel_spmd

    nc = bacc.Bacc("TRN2", target_bir_lowering=False, num_devices=1)
    arrays, args = {}, []
    for name, a in pack(inputs).items():
        arrays[f"in_{name}"] = a
        args.append(nc.dram_tensor(f"in_{name}", a.shape, mybir.dt.from_np(a.dtype), kind="ExternalInput").ap())
    args.append(nc.dram_tensor("out", _OUT[0], F32, kind="ExternalOutput").ap())
    build_block(nc, *args)
    r = run_bass_kernel_spmd(nc, [arrays], core_ids=[0])
    return r.results[0]["out"]
```

```python
import concourse.bass as bass
from concourse import mybir
from contextlib import ExitStack

F32 = mybir.dt.float32
BF16 = mybir.dt.bfloat16
ALU = mybir.AluOpType
ACT = mybir.ActivationFunctionType
AX = mybir.AxisListType

P = 128
B = 32
GB = 4
NG = B // GB
GT = GB * P
NH = 16
HD = P // NH
NJ = NH // 2
VW = 32
NCORE = 2 * B
SCALE = float(HD) ** -0.5
SCALE1 = float(P) ** -0.5
Q_PART = (0, 1, 2, 0, 1, 0)
K_PART = (0, 0, 0, 1, 1, 2)
Q_ROWS, K_ROWS = (sorted(range(6), key=lambda r: part[r]) for part in (Q_PART, K_PART))
MAX_ROW = 6
HALF_DMAS = 16 * (len(Q_PART) + len(K_PART) + 1)

W_COLS = {}
_at = 0
for _name, _n in (("mod", 6 * P), ("q", P), ("k", P), ("v", P), ("proj", P), ("qc", P), ("kc", P), ("vc", P),
                  ("cproj", P), ("mlp1", 4 * P), ("mlp2", 4 * P), ("wqT", P), ("wkT", P), ("wvT", P),
                  ("r_nx", 3), ("r_ev", 3), ("r_an", 3), ("e_nx", 6 * P), ("g_nx", P), ("e_ev", 6 * P), ("g_ev", P),
                  ("e_an", 6 * P), ("g_an", P), ("gate2", P), ("e2T", 6 * P), ("outw", P)):
    W_COLS[_name] = (_at, _n)
    _at += _n
W_TOTAL = _at
V_COLS = {}
_at = 0
for _name, _n in (("bmod", 6), ("bq", 1), ("bk", 1), ("bv", 1), ("bproj", 1), ("bqc", 1), ("bkc", 1), ("bvc", 1),
                  ("bcproj", 1), ("bmlp1", 4), ("bmlp2", 1), ("gamma", 1), ("beta", 1), ("be1", 6), ("bg1", 1),
                  ("be2", 3)):
    V_COLS[_name] = (_at, _n)
    _at += _n
V_TOTAL = _at


class Core:

    def __init__(self, n, mod, pairs, kind, group, b):
        self.n, self.mod, self.pairs, self.kind, self.group, self.b = n, mod, pairs, kind, group, b


def core_at(i, s, steady):
    kind, b = (0, s) if s < GB else (1, s - GB)
    g = i - kind
    if steady:
        return Core(8 * i + (s - GB), (s + GB) % 8, 4 * i + (s - GB) // 2, kind, g, b)
    if not 0 <= g < NG:
        return None
    n = s if i == 0 else NCORE - GB + b if i == NG else 8 * i + (s - GB)
    return Core(n, n % 8, n // 2, kind, g, b)


GROUP_STEPS = sorted([
    (0.9, "load", "ln_c", 0, 0),
    (0.5, "stats", "ln_s", 1, 0), (1.5, "stats", "ln_s", 1, 1),
    (3.5, "norm", "ln_s", 1, 0), (4.0, "norm", "ln_s", 1, 1), (4.5, "norm", "ln_s", 1, 2), (5.0, "norm", "ln_s", 1, 3),
    (1.9, "fill", "v_c", -1, 0), (2.0, "read", "v_c", -1, 1),
    (6.9, "fill", "xt_s", 1, 0), (7.0, "read", "xt_s", 1, 0), (7.5, "read", "xt_s", 1, 1),
    (8.9, "fill", "q_s", 1, 0), (9.0, "read", "q_s", 1, 0), (9.4, "read", "q_s", 1, 1),
    (8.6, "stats", "ln_c", 0, 0), (9.6, "stats", "ln_c", 0, 1),
    (10.9, "fill", "k_s", 1, 0), (11.0, "read", "k_s", 1, 0), (11.4, "read", "k_s", 1, 1),
    (12.9, "fill", "proj_c", -2, 0), (13.0, "read", "proj_c", -2, 1),
    (14.9, "fill", "yt_c", -2, 0), (15.0, "read", "yt_c", -2, 1),
    (13.0, "norm", "ln_c", 0, 0), (13.5, "norm", "ln_c", 0, 1), (14.0, "norm", "ln_c", 0, 2),
    (14.5, "norm", "ln_c", 0, 3),
    (16.9, "fill", "xt_c", 0, 0), (17.0, "read", "xt_c", 0, 1),
    (18.9, "fill", "k_c", 0, 0), (19.0, "read", "k_c", 0, 0), (19.4, "read", "k_c", 0, 1),
    (20.9, "fill", "v_s", 1, 0), (21.0, "read", "v_s", 1, 1),
    (22.9, "fill", "proj_s", 0, 0), (23.0, "read", "proj_s", 0, 0), (23.5, "read", "proj_s", 0, 1),
    (24.6, "fill", "yt_s", 0, 0), (25.0, "read", "yt_s", 0, 1),
    (25.4, "stats", "ln_x", 0, 0), (25.6, "stats", "ln_x", 0, 1),
    (26.5, "norm", "ln_x", 0, 0), (27.0, "norm", "ln_x", 0, 1), (27.4, "norm", "ln_x", 0, 2),
    (27.8, "norm", "ln_x", 0, 3),
    (28.9, "fill", "xt_x", 0, 0), (29.0, "read", "xt_x", 0, 1),
    (29.9, "fill", "q_c", 0, 0), (30.0, "read", "q_c", 0, 0), (30.4, "read", "q_c", 0, 1),
])
BANK_ORDER = [name for _, step, name, _, _ in GROUP_STEPS if step == "fill"]
BANK_LAG = {name: lag for _, step, name, lag, _ in GROUP_STEPS if step == "fill"}


def stack_steps():
    def moves(what, h):
        return [(what, r, h) for r in {"zero": [0], "Q": Q_ROWS, "K": K_ROWS}[what]]

    own = moves("zero", 0) + moves("Q", 0) + moves("K", 0) + moves("zero", 1) + moves("Q", 1) + moves("K", 1)
    steps = [(12 + k // 2, 0, 1, *m, (1, 3)[m[2]]) for k, m in enumerate(own)]
    steps += [(26 + k // 2, 1, 0, *m, 5) for k, m in enumerate(moves("zero", 0) + moves("K", 0))]
    q, k = moves("Q", 0), moves("K", 1)
    rest = q[0:3] + moves("zero", 1) + q[3:6] + k + moves("Q", 1)
    steps += [(k // 2, 1, -1, *m, (-3, -1)[m[2]]) for k, m in enumerate(rest)]
    return steps


STACK_STEPS = stack_steps()


def attention_events(i, steady=False):
    def valid(g):
        return steady or 0 <= g < NG

    def before(name):
        at, it = BANK_ORDER.index(name), i
        while True:
            at -= 1
            if at < 0:
                at, it = len(BANK_ORDER) - 1, it - 1
                if not steady and it < -1:
                    return None
            g = it + BANK_LAG[BANK_ORDER[at]]
            if valid(g):
                return BANK_ORDER[at], g

    def group_steps(start, end):
        for t, step, name, lag, part in GROUP_STEPS:
            if start <= t < end and valid(i + lag):
                if step == "fill":
                    last = {"proj_s": core_at(i, 3, steady), "proj_c": core_at(i - 1, 7, steady)}.get(name)
                    yield (step, name, i + lag, before(name), last)
                else:
                    yield (step, name, i + lag, part)

    for s in range(8):
        here = core_at(i, s, steady)
        back1 = core_at(i, s - 1, steady) if s else core_at(i - 1, 7, steady)
        back2 = core_at(i, s - 2, steady) if s > 1 else core_at(i - 1, s + 6, steady)
        ahead1 = core_at(i, s + 1, steady) if s < 7 else core_at(i + 1, 0, steady)
        ahead2 = core_at(i, s + 2, steady) if s < 6 else core_at(i + 1, s - 6, steady)
        ahead3 = core_at(i, s + 3, steady) if s < 5 else core_at(i + 1, s - 5, steady)
        for u in range(4):
            for t, kind, lag, what, r, h, slot in STACK_STEPS:
                if t == 4 * s + u and valid(i + lag):
                    last = core_at(i, slot, steady) if slot >= 0 else core_at(i - 1, slot + 8, steady)
                    yield ("stack", kind, i + lag, last, what, r, h)
            if u == 3 and back1:
                yield ("o_turn", back1)
            if u == 2 and ahead2:
                yield ("max_parts", ahead2)
            if u == 2 and back2:
                yield ("o_back", back2, back2.n + 1 + bool(back1) + bool(here) + bool(ahead1))
            yield from group_steps(4 * s + u, 4 * s + u + 0.5)
            scored = ahead2 if u < 2 else ahead3
            if scored:
                yield ("score", scored, (u + 2) % 4)
            if here:
                yield ("shifted", here, u)
            if u > 1 and here:
                yield ("value", here, u - 2)
            if u < 2 and back1:
                yield ("value", back1, u + 2)
            if u == 3 and back1:
                yield ("o_norm", back1)
            if u == 3 and ahead2:
                yield ("max_turn", ahead2, ahead2.n - bool(ahead1) - bool(here) - bool(back1))
            yield from group_steps(4 * s + u + 0.5, 4 * s + u + 1)


def build_block(nc, xin, cond, ctxin, weights, vectors, ident_in, rowb, out):
    stack = ExitStack()
    with stack:
        def sb(name, shape, dt=F32):
            return stack.enter_context(nc.sbuf_tensor(name, shape, dt))

        def sem(name):
            return stack.enter_context(nc.semaphore(name))

        attention_memory = ExitStack()

        def asb(name, shape, dt=F32):
            return attention_memory.enter_context(nc.sbuf_tensor(name, shape, dt))

        X = sb("X", [P, B * P])
        W = sb("W", [P, W_TOTAL])
        V = sb("V", [P, V_TOTAL])
        ident = sb("ident", [P, P])
        identb = sb("identb", [P, P], BF16)

        def w(name, lo=0, n=None):
            at, size = W_COLS[name]
            return W[:, at + lo:at + lo + (size if n is None else n)]

        def vec(name, k=0):
            return V[:, V_COLS[name][0] + k:V_COLS[name][0] + k + 1]

        condr = sb("condr", [B, P])
        rows1 = sb("rows1", [1, 2 * P + 3])
        condT = sb("condT", [P, B])
        condS = sb("condS", [P, B])
        mod = sb("mod", [P, 6, B])
        gba = sb("gba", [P, B])
        gbm = sb("gbm", [P, B])
        bpr = sb("bpr", [P, 2])
        half = sb("half", [P, GB])
        eps = sb("eps", [P, GB])
        seen = sb("seen", [P, 1])
        zeros = sb("zeros", [P, GT])
        XN = [asb(f"XN{k}", [P, GT]) for k in range(3)]
        XT = [asb(f"XT{k}", [P, GT]) for k in range(3)]
        CTXG = asb("CTXG", [P, GB, P])
        stat = asb("stat", [P, 3, GB, 6])
        mv = asb("mv", [P, 3, GB, 2])
        veps = asb("veps", [P, 3, GB])
        rstd = asb("rstd", [P, 3, GB])
        Qp = [asb(f"Qp{k}", [P, 3, GT], BF16) for k in range(2)]
        Kp = [asb(f"Kp{k}", [P, 3, GT], BF16) for k in range(2)]
        rest = asb("rest", [P, 2, GT])
        Qs = [asb(f"Qs{k}", [P, NJ, GT], BF16) for k in range(2)]
        Ks = [asb(f"Ks{k}", [P, NJ, GT], BF16) for k in range(2)]
        zrow = asb("zrow", [32, GT], BF16)
        orow = asb("orow", [32, GT], BF16)
        Va = [asb(f"Va{k}", [P, GB, NH, VW]) for k in range(2)]
        NM = asb("NM", [P, 2, NH])
        M2 = asb("M2", [P, 2, 2, 2, NJ], BF16)
        MT = asb("MT", [32, 2, P], BF16)
        PR = asb("PR", [P, 4, 4 * P])
        OTs = asb("OTs", [P, 4 * P])
        rden = asb("rden", [P, NH])
        On = asb("On", [P, 2, P])
        OgT = [asb(f"OgT{k}", [P, GT]) for k in range(2)]
        YT = [asb(f"YT{k}", [P, GT]) for k in range(2)]

        PS = [stack.enter_context(nc.psum_tensor(f"PS{k}", [P, 512], F32)) for k in range(8)]
        S_BANK, T_BANK, O_BANK, GROUP_BANK, SMALL_BANK = PS[0:2], PS[2:4], PS[4:6], PS[6], PS[7]

        load_small = sem("load_small")
        load_w = sem("load_w")
        load_w2 = sem("load_w2")
        load_x = [sem(f"load_x{g}") for g in range(NG)]
        consts = sem("consts")
        stack_init = sem("stack_init")
        setup_pe = sem("setup_pe")
        setup_act = sem("setup_act")
        setup_dve = sem("setup_dve")

        kinds = ("s", "x", "c")
        ln_stat = [sem(f"ln_stat_{k}") for k in kinds]
        ln_mv = [sem(f"ln_mv_{k}") for k in kinds]
        ln_var = [sem(f"ln_var_{k}") for k in kinds]
        ln_rstd = [sem(f"ln_rstd_{k}") for k in kinds]
        ln_done = [sem(f"ln_done_{k}") for k in kinds]
        bank_filled = {e: sem(f"filled_{e}") for e in BANK_ORDER}
        bank_read = {e: sem(f"read_{e}") for e in BANK_ORDER}
        high_ready = {e: sem(f"high_{e}") for e in ("q_s", "k_s", "q_c", "k_c")}
        middle_ready = {e: sem(f"middle_{e}") for e in ("q_s", "k_s", "q_c", "k_c")}
        low_ready = {e: sem(f"low_{e}") for e in ("q_s", "k_s", "q_c", "k_c")}
        stacked = [[sem(f"stacked_{k}_{h}") for h in range(2)] for k in ("self", "cross")]
        ctx_loaded = sem("ctx_loaded")
        score_done = sem("score_done")
        max_done = sem("max_done")
        max_high = sem("max_high")
        max_parts = sem("max_parts")
        max_turned = sem("max_turned")
        max_copied = sem("max_copied")
        max_rows = [sem(f"max_rows{k}") for k in range(2)]
        shifted_done = sem("shifted_done")
        exp_done = sem("exp_done")
        value_done = sem("value_done")
        o_copied = sem("o_copied")
        o_turned = sem("o_turned")
        den_done = sem("den_done")
        o_normed = sem("o_normed")
        o_backed = sem("o_backed")
        o_stored = sem("o_stored")

        LN_KIND = {"ln_s": 0, "ln_x": 1, "ln_c": 2, "xt_s": 0, "xt_x": 1, "xt_c": 2}
        WEIGHT = {"q_s": "q", "k_s": "k", "q_c": "qc", "k_c": "kc", "v_s": "v", "v_c": "vc", "proj_s": "proj",
                  "proj_c": "cproj"}
        SOURCE = {"q_s": 0, "k_s": 0, "v_s": 0, "q_c": 1, "k_c": 2, "v_c": 2}
        BIAS = {"q_s": "bq", "k_s": "bk", "q_c": "bqc", "k_c": "bkc"}
        PARTS = {"q_s": Qp[0], "k_s": Kp[0], "q_c": Qp[1], "k_c": Kp[1]}
        REST = {"q_s": 0, "k_s": 1, "q_c": 0, "k_c": 1}
        KIND = {"q_s": 0, "k_s": 0, "q_c": 1, "k_c": 1, "v_s": 0, "v_c": 1, "proj_s": 0, "proj_c": 1, "yt_s": 0,
                "yt_c": 1}

        def attention_loop(eng, body):
            for i in range(-1, 3):
                for ev in attention_events(i):
                    body(ev)
            with eng.Fori(3, 7) as i:
                for ev in attention_events(i, steady=True):
                    body(ev)
            for i in range(7, 10):
                for ev in attention_events(i):
                    body(ev)

        block = attention_memory.enter_context(nc.Block())

        @block.sync
        def _(sp):
            sp.dma_start(ident[:, :], ident_in).then_inc(load_small, 16)
            sp.dma_start(condr[:, :], cond).then_inc(load_small, 16)
            sp.dma_start(V[:, :], vectors).then_inc(load_small, 16)
            sp.dma_start(rows1[:, :], rowb).then_inc(load_w2, 16)
            sp.dma_start(W[:, 0:W_COLS["mlp1"][0]], weights[:, 0:W_COLS["mlp1"][0]]).then_inc(load_w, 16)
            for g in range(NG):
                sp.dma_start(X[:, g * GT:(g + 1) * GT].rearrange("p (b h) -> p b h", b=GB),
                             xin[g * GB:(g + 1) * GB].rearrange("b p h -> p b h")).then_inc(load_x[g], 16)
            sp.dma_start(W[:, W_COLS["mlp1"][0]:], weights[:, W_COLS["mlp1"][0]:]).then_inc(load_w2, 16)
            sp.wait_ge(stack_init, 1)
            for k in range(2):
                sp.dma_start(Ks[k][MAX_ROW::32, :, :], orow[:, :]).then_inc(consts, 16)

            def body(ev):
                name = ev[0]
                if name == "stack":
                    _, kind, g, last, what, r, h = ev
                    half_group = slice(2 * h * P, 2 * (h + 1) * P)
                    if what == "zero":
                        if last is not None:
                            sp.wait_ge(shifted_done, 4 * last.n + 4)
                        to, source = Qs[kind][MAX_ROW::32, :, half_group], zrow[:, half_group]
                    else:
                        name, parts, of, to = \
                            (("k_s", "k_c")[kind], Kp[kind], K_PART, Ks[kind]) if what == "K" else \
                            (("q_s", "q_c")[kind], Qp[kind], Q_PART, Qs[kind])
                        sp.wait_ge((high_ready, middle_ready, low_ready)[of[r]][name], g + 1)
                        to, source = to[r::8, :, half_group], parts[:, of[r], half_group]
                    sp.dma_start(to, source).then_inc(stacked[kind][h], 16)
                elif name == "max_turn":
                    c = ev[1]
                    sp.wait_ge(max_copied, c.n + 1)
                    sp.dma_start(Qs[c.kind][MAX_ROW::32, :, c.b * P:(c.b + 1) * P],
                                 MT[:, c.mod % 2, :]).then_inc(max_rows[c.mod % 2], 16)
                elif name == "load":
                    g = ev[2]
                    if not isinstance(g, int) or g > 0:
                        sp.wait_ge(ln_done[2], g)
                    sp.dma_start(CTXG[:, :, :], ctxin[bass.ds(g * GB, GB)].rearrange("b p h -> p b h"))\
                        .then_inc(ctx_loaded, 16)

            attention_loop(sp, body)

        @block.gpsimd
        def _(pool):
            nc.gpsimd.memset(zrow[:, :], 0.0)
            nc.gpsimd.memset(orow[:, :], 1.0)
            nc.gpsimd.memset(half[:, :], -0.5)
            nc.gpsimd.memset(eps[:, :], 1e-6)
            nc.gpsimd.memset(zeros[:, :], 0.0)
            for k in range(2):
                nc.gpsimd.memset(Qs[k][:, :, :].bitcast(F32), 0.0)
                last = nc.gpsimd.memset(Ks[k][:, :, :].bitcast(F32), 0.0)
            last.then_inc(stack_init, 1)
            pool.wait_ge(stack_init, 1)

            def body(ev):
                name = ev[0]
                if name == "stats" and ev[3] == 1:
                    g, k = ev[2], LN_KIND[ev[1]]
                    pool.wait_ge(ln_mv[k], g + 1)
                    nc.gpsimd.tensor_tensor(veps[:, k, :], mv[:, k, :, 1], eps[:, :], ALU.add)\
                        .then_inc(ln_var[k], 1)
                    pool.wait_ge(ln_var[k], g + 1)
                    nc.gpsimd.tensor_tensor(rstd[:, k, :], veps[:, k, :], half[:, :], ALU.pow)\
                        .then_inc(ln_rstd[k], 1)
                elif name == "read" and ev[1] in PARTS and ev[3] == 1:
                    name, g = ev[1:3]
                    parts, left = PARTS[name], rest[:, REST[name], :]
                    pool.wait_ge(bank_read[name], g + 1)
                    nc.gpsimd.tensor_tensor(parts[:, 1, :], left, zeros[:, :], ALU.add)\
                        .then_inc(middle_ready[name], 1)
                    pool.wait_ge(middle_ready[name], g + 1)
                    nc.gpsimd.tensor_tensor(parts[:, 2, :], left, parts[:, 1, :], ALU.subtract)\
                        .then_inc(low_ready[name], 1)

            attention_loop(pool, body)

        @block.scalar
        def _(act):
            act.wait_ge(setup_pe, 1)
            nc.scalar.activation(condS[:, :], PS[0][:, 0:B], ACT.Silu).then_inc(setup_act, 1)
            act.wait_ge(setup_pe, 2)
            for k in range(6):
                nc.scalar.activation(mod[:, k, :], PS[1][:, k * B:(k + 1) * B], ACT.Identity,
                                     bias=vec("bmod", k))
            nc.scalar.activation(bpr[:, 0:1], PS[1][:, 6 * B:6 * B + 1], ACT.Identity, bias=vec("bproj"))
            nc.scalar.activation(bpr[:, 1:2], PS[1][:, 6 * B + 1:6 * B + 2], ACT.Identity,
                                 bias=vec("bcproj")).then_inc(setup_act, 1)
            act.wait_ge(setup_dve, 3)

            def body(ev):
                name = ev[0]
                if name == "shifted":
                    _, c, u = ev
                    act.wait_ge(shifted_done, 4 * c.n + (u + 1))
                    if not isinstance(c.n, int) or c.n > 0:
                        act.wait_ge(value_done, 4 * c.n + (u - 3))
                    nc.scalar.activation(PR[:, u, :], T_BANK[u % 2][:, :], ACT.Exp, scale=SCALE)\
                        .then_inc(exp_done, 1)
                elif name == "value" and ev[2] == 3:
                    c = ev[1]
                    act.wait_ge(value_done, 4 * c.n + 4)
                    if not isinstance(c.n, int) or c.n > 0:
                        act.wait_ge(o_turned, c.n)
                    nc.scalar.activation(OTs[:, :], O_BANK[c.mod % 2][:, :], ACT.Copy).then_inc(o_copied, 1)
                elif name == "max_turn":
                    c = ev[1]
                    act.wait_ge(max_turned, c.n + 1)
                    if not isinstance(c.n, int) or c.n > 1:
                        act.wait_ge(max_rows[c.mod % 2], 16 * c.pairs)
                    nc.scalar.activation(MT[:, c.mod % 2, :], SMALL_BANK[0:32, 0:P // 2].bitcast(BF16), ACT.Copy)\
                        .then_inc(max_copied, 1)
                elif name == "o_back":
                    c = ev[1]
                    act.wait_ge(o_backed, c.n + 1)
                    e = "proj_s" if c.kind == 0 else "proj_c"
                    if not isinstance(c.group, int) or c.group > 0:
                        act.wait_ge(bank_filled[e], c.group)
                    nc.scalar.activation(OgT[c.kind][:, c.b * P:(c.b + 1) * P], SMALL_BANK[:, 0:P], ACT.Copy)\
                        .then_inc(o_stored, 1)
                elif ev[:2] == ("read", "xt_s"):
                    _, name, g, part = ev
                    act.wait_ge(bank_filled[name], g + 1)
                    for b in range(2 * part, 2 * part + 2):
                        nb = bass.ds(g * GB + b, 1)
                        last = nc.scalar.activation(XT[0][:, b * P:(b + 1) * P], GROUP_BANK[:, b * P:(b + 1) * P],
                                                    ACT.Identity, scale=mod[:, 1, nb], bias=mod[:, 0, nb])
                    if part == 1:
                        last.then_inc(bank_read[name], 1)
                elif name == "read" and ev[1] in ("xt_x", "xt_c"):
                    name, g = ev[1:3]
                    act.wait_ge(bank_filled[name], g + 1)
                    nc.scalar.activation(XT[LN_KIND[name]][:, :], GROUP_BANK[:, :], ACT.Copy)\
                        .then_inc(bank_read[name], 1)
                elif name == "read" and ev[1] in PARTS and ev[3] == 0:
                    name, g = ev[1:3]
                    act.wait_ge(bank_filled[name], g + 1)
                    if not isinstance(g, int) or g > 0:
                        for h in range(2):
                            act.wait_ge(stacked[KIND[name]][h], HALF_DMAS * g)
                    nc.scalar.activation(PARTS[name][:, 0, :], GROUP_BANK[:, :], ACT.Identity,
                                         bias=vec(BIAS[name])).then_inc(high_ready[name], 1)
                elif name == "read" and ev[1] in ("v_s", "v_c"):
                    name, g = ev[1:3]
                    kind = KIND[name]
                    act.wait_ge(bank_filled[name], g + 1)
                    nc.scalar.activation(Va[kind][:, :, :, 0:HD].rearrange("p b h d -> p (b h) d"),
                                         GROUP_BANK[:, :].rearrange("p (n d) -> p n d", d=HD), ACT.Copy)\
                        .then_inc(bank_read[name], 1)
                elif ev[:2] == ("read", "proj_c"):
                    name, g = ev[1:3]
                    act.wait_ge(bank_filled[name], g + 1)
                    if not isinstance(g, int) or g > 0:
                        act.wait_ge(bank_filled["yt_c"], g)
                    nc.scalar.activation(YT[1][:, :], GROUP_BANK[:, :], ACT.Identity, bias=bpr[:, 1:2])\
                        .then_inc(bank_read[name], 1)

            attention_loop(act, body)

        @block.vector
        def _(dve):
            for k in range(2):
                nc.vector.memset(Va[k][:, :, :, :], 0.0)
            dve.drain()
            for k in range(2):
                nc.vector.memset(Va[k][:, :, :, HD:HD + 1], 1.0)
            dve.wait_ge(load_small, 48)
            nc.vector.tensor_copy(identb[:, :], ident[:, :]).then_inc(setup_dve, 1)
            dve.wait_ge(setup_pe, 1)
            dve.wait_ge(setup_act, 2)
            nc.vector.tensor_copy(condT[:, :], PS[0][:, 0:B])
            nc.vector.tensor_scalar(mod[:, 1, :], mod[:, 1, :], 1.0, None, ALU.add)
            nc.vector.tensor_scalar(mod[:, 4, :], mod[:, 4, :], 1.0, None, ALU.add).then_inc(setup_dve, 1)
            nc.vector.tensor_scalar(gba[:, :], mod[:, 2, :], bpr[:, 0:1], None, ALU.mult)
            nc.vector.tensor_scalar(gbm[:, :], mod[:, 5, :], vec("bmlp2"), None, ALU.mult).then_inc(setup_dve, 1)
            dve.wait_ge(setup_dve, 3)

            def ln_source(k, g, b):
                return CTXG[:, b, :] if k == 2 else X[:, bass.ds(g * GT + b * P, P)]

            def body(ev):
                name = ev[0]
                if name == "score":
                    _, c, u = ev
                    r = c.mod % 2
                    dve.wait_ge(score_done, 4 * c.n + (u + 1))
                    nc.vector.tensor_reduce(out=NM[:, r, 4 * u:4 * u + 4],
                                            in_=S_BANK[u % 2][:, :].rearrange("p (h k) -> p h k", k=P),
                                            axis=AX.X, op=ALU.max, negate=True).then_inc(max_done, 1)
                elif name == "max_parts":
                    c = ev[1]
                    r = c.mod % 2
                    nm = NM[:, r, :].rearrange("p (e j) -> p e j", e=2)
                    dve.wait_ge(max_done, 4 * c.n + 4)
                    if not isinstance(c.n, int) or c.n > 1:
                        dve.wait_ge(max_turned, c.n - 1)
                    nc.vector.tensor_copy(M2[:, r, :, 0, :], nm).then_inc(max_high, 1)
                    dve.wait_ge(max_high, c.n + 1)
                    nc.vector.tensor_tensor(M2[:, r, :, 1, :], nm, M2[:, r, :, 0, :], ALU.subtract)\
                        .then_inc(max_parts, 1)
                elif name == "o_norm":
                    c = ev[1]
                    r = c.mod % 2
                    turned = O_BANK[c.mod % 2][:, :].rearrange("p (h d) -> p h d", d=VW)
                    dve.wait_ge(o_turned, c.n + 1)
                    nc.vector.reciprocal(rden[:, :].unsqueeze(2), turned[:, :, HD:HD + 1]).then_inc(den_done, 1)
                    dve.wait_ge(den_done, c.n + 1)
                    if not isinstance(c.n, int) or c.n > 1:
                        dve.wait_ge(o_backed, c.n - 1)
                    nc.vector.tensor_tensor(On[:, r, :].rearrange("p (h d) -> p h d", d=HD), turned[:, :, 0:HD],
                                            rden[:, :].unsqueeze(2).to_broadcast([P, NH, HD]), ALU.mult)\
                        .then_inc(o_normed, 1)
                elif name == "stats":
                    g, k, part = ev[2], LN_KIND[ev[1]], ev[3]
                    if k == 0 and part == 0 and isinstance(g, int):
                        dve.wait_ge(load_x[g], 16)
                    elif k == 0 and part == 0:
                        for q in range(NG):
                            dve.wait_ge(load_x[q], 16)
                    if k > 0 and part == 0:
                        if k == 1:
                            dve.wait_ge(bank_read["yt_s"], g + 1)
                        else:
                            dve.wait_ge(ctx_loaded, 16 * (g + 1))
                        nc.vector.tensor_copy(seen[:, :], half[:, 0:1])
                    for b in range(2 * part, 2 * part + 2):
                        last = nc.vector.bn_stats(stat[:, k, b, :], ln_source(k, g, b))
                    if part == 1:
                        last.then_inc(ln_stat[k], 1)
                        dve.wait_ge(ln_stat[k], g + 1)
                        nc.vector.tensor_copy(seen[:, :], stat[:, k, GB - 1, 0:1])
                        for b in range(GB):
                            last = nc.vector.bn_aggr(mv[:, k, b, :], stat[:, k, b, :])
                        last.then_inc(ln_mv[k], 1)
                elif name == "norm":
                    g, k, b = ev[2], LN_KIND[ev[1]], ev[3]
                    if b == 0:
                        dve.wait_ge(ln_rstd[k], g + 1)
                        if not isinstance(g, int) or g > 0:
                            dve.wait_ge(bank_filled[("xt_s", "xt_x", "xt_c")[k]], g)
                    last = nc.vector.tensor_scalar(XN[k][:, b * P:(b + 1) * P], ln_source(k, g, b),
                                                   mv[:, k, b, 0:1], rstd[:, k, b:b + 1], ALU.subtract, ALU.mult)
                    if b == GB - 1:
                        last.then_inc(ln_done[k], 1)
                elif ev[:2] == ("read", "proj_s"):
                    _, name, g, part = ev
                    if part == 0:
                        dve.wait_ge(bank_filled[name], g + 1)
                        if not isinstance(g, int) or g > 0:
                            dve.wait_ge(bank_filled["yt_s"], g)
                    for b in range(2 * part, 2 * part + 2):
                        nb = bass.ds(g * GB + b, 1)
                        last = nc.vector.tensor_scalar(YT[0][:, b * P:(b + 1) * P],
                                                       GROUP_BANK[:, b * P:(b + 1) * P], mod[:, 2, nb],
                                                       gba[:, nb], ALU.mult, ALU.add)
                    if part == 1:
                        last.then_inc(bank_read[name], 1)
                elif name == "read" and ev[1] in PARTS and ev[3] == 1:
                    name, g = ev[1:3]
                    before = {"q_s": g - 1, "k_s": g - 1, "q_c": g + 2, "k_c": g + 2}[name]
                    other = {"q_s": "q_c", "k_s": "k_c", "q_c": "q_s", "k_c": "k_s"}[name]
                    if isinstance(before, int):
                        before = min(before, NG)
                    if not isinstance(before, int) or before > 0:
                        dve.wait_ge(low_ready[other], before)
                    dve.wait_ge(high_ready[name], g + 1)
                    nc.vector.scalar_tensor_tensor(rest[:, REST[name], :], GROUP_BANK[:, :], vec(BIAS[name]),
                                                   PARTS[name][:, 0, :], ALU.add, ALU.subtract)\
                        .then_inc(bank_read[name], 1)
                elif name == "read" and ev[1] in ("yt_s", "yt_c"):
                    name, g = ev[1:3]
                    x = X[:, bass.ds(g * GT, GT)]
                    dve.wait_ge(bank_filled[name], g + 1)
                    nc.vector.tensor_tensor(x, GROUP_BANK[:, :], x, ALU.add).then_inc(bank_read[name], 1)

            attention_loop(dve, body)

        @block.tensor
        def _(pe):
            pe.wait_ge(load_small, 48)
            pe.wait_ge(load_w, 16)
            nc.tensor.transpose(PS[0][:, 0:B], condr[:, :], ident[0:B, 0:B]).then_inc(setup_pe, 1)
            pe.wait_ge(setup_act, 1)
            for k in range(6):
                nc.tensor.matmul(PS[1][:, k * B:(k + 1) * B], w("mod", k * P, P), condS[:, :], start=True, stop=True)
            nc.tensor.matmul(PS[1][:, 6 * B:6 * B + 1], w("proj"), vec("bv"), start=True, stop=True)
            nc.tensor.matmul(PS[1][:, 6 * B + 1:6 * B + 2], w("cproj"), vec("bvc"), start=True, stop=True)\
                .then_inc(setup_pe, 1)
            pe.wait_ge(setup_dve, 3)
            pe.wait_ge(consts, 32)

            def body(ev):
                name = ev[0]
                if name == "score":
                    _, c, u = ev
                    e, lo = u // 2, (u % 2) * 4
                    if u == 0 and c.b % 2 == 0:
                        pe.wait_ge(stacked[c.kind][c.b // 2], HALF_DMAS * (c.group + 1))
                    if not isinstance(c.n, int) or 4 * c.n + u > 1:
                        pe.wait_ge(max_done, 4 * c.n + (u - 1))
                    for j in range(4):
                        rows, cols = slice(64 * e, 64 * e + 64), slice(c.b * P, (c.b + 1) * P)
                        last = nc.tensor.matmul(S_BANK[u % 2][:, j * P:(j + 1) * P], Qs[c.kind][rows, lo + j, cols],
                                                Ks[c.kind][rows, lo + j, cols], start=True, stop=True)
                    last.then_inc(score_done, 1)
                elif name == "shifted":
                    _, c, u = ev
                    e, lo = u // 2, (u % 2) * 4
                    if u == 0:
                        pe.wait_ge(max_rows[c.mod % 2], 16 * (c.pairs + 1))
                    if not isinstance(c.n, int) or 4 * c.n + u > 1:
                        pe.wait_ge(exp_done, 4 * c.n + (u - 1))
                    for j in range(4):
                        rows, cols = slice(64 * e, 64 * e + 64), slice(c.b * P, (c.b + 1) * P)
                        last = nc.tensor.matmul(T_BANK[u % 2][:, j * P:(j + 1) * P], Ks[c.kind][rows, lo + j, cols],
                                                Qs[c.kind][rows, lo + j, cols], start=True, stop=True)
                    last.then_inc(shifted_done, 1)
                elif name == "value":
                    _, c, u = ev
                    pe.wait_ge(exp_done, 4 * c.n + (u + 1))
                    if u == 0:
                        if not isinstance(c.n, int) or c.n > 1:
                            pe.wait_ge(o_normed, c.n - 1)
                        if c.b == 0:
                            pe.wait_ge(bank_read["v_s" if c.kind == 0 else "v_c"], c.group + 1)
                    for j in range(4):
                        last = nc.tensor.matmul(O_BANK[c.mod % 2][32 * j:32 * j + 32, u * P:(u + 1) * P],
                                                Va[c.kind][:, c.b, 4 * u + j, :], PR[:, u, j * P:(j + 1) * P],
                                                start=True, stop=True)
                    last.then_inc(value_done, 1)
                elif name == "max_turn":
                    _, c, stored = ev
                    pe.wait_ge(max_parts, c.n + 1)
                    if not isinstance(c.n, int) or stored > 0:
                        pe.wait_ge(o_stored, stored)
                    if isinstance(c.n, int) and c.n > 0:
                        pe.wait_ge(max_copied, c.n)
                    nc.tensor.transpose(SMALL_BANK[0:32, 0:P // 2].bitcast(BF16),
                                        M2[:, c.mod % 2, :, :, :].rearrange("p e t j -> p (e t j)"), identb[:, :])\
                        .then_inc(max_turned, 1)
                elif name == "o_turn":
                    c = ev[1]
                    pe.wait_ge(o_copied, c.n + 1)
                    for u in range(4):
                        last = nc.tensor.transpose(O_BANK[c.mod % 2][:, u * P:(u + 1) * P], OTs[:, u * P:(u + 1) * P],
                                                   ident[:, :])
                    last.then_inc(o_turned, 1)
                elif name == "o_back":
                    _, c, copied = ev
                    pe.wait_ge(o_normed, c.n + 1)
                    pe.wait_ge(max_copied, copied)
                    if isinstance(c.n, int) and c.n > 0:
                        pe.wait_ge(o_stored, c.n)
                    nc.tensor.transpose(SMALL_BANK[:, 0:P], On[:, c.mod % 2, :], ident[:, :]).then_inc(o_backed, 1)
                elif name == "fill":
                    _, name, g, before, last_core = ev
                    if before is not None:
                        pe.wait_ge(bank_read[before[0]], before[1] + 1)
                    if name in ("xt_s", "xt_x", "xt_c"):
                        k = LN_KIND[name]
                        pe.wait_ge(ln_done[k], g + 1)
                        for b in range(GB):
                            last = nc.tensor.transpose(GROUP_BANK[:, b * P:(b + 1) * P], XN[k][:, b * P:(b + 1) * P],
                                                       ident[:, :])
                    elif name in PARTS:
                        last = nc.tensor.matmul(GROUP_BANK[:, :], w(WEIGHT[name]), XT[SOURCE[name]][:, :],
                                                start=True, stop=True)
                    elif name in ("v_s", "v_c"):
                        for b in range(GB):
                            last = nc.tensor.matmul(GROUP_BANK[:, b * P:(b + 1) * P],
                                                    XT[SOURCE[name]][:, b * P:(b + 1) * P], w(WEIGHT[name]),
                                                    start=True, stop=True)
                    elif name in ("proj_s", "proj_c"):
                        pe.wait_ge(o_stored, last_core.n + 1)
                        last = nc.tensor.matmul(GROUP_BANK[:, :], w(WEIGHT[name]), OgT[KIND[name]][:, :],
                                                start=True, stop=True)
                    else:
                        for b in range(GB):
                            last = nc.tensor.transpose(GROUP_BANK[:, b * P:(b + 1) * P],
                                                       YT[KIND[name]][:, b * P:(b + 1) * P], ident[:, :])
                    last.then_inc(bank_filled[name], 1)

            attention_loop(pe, body)

        attention_memory.close()
        mlp_and_router(nc, stack, X, ctxin, w, vec, rows1, condT, mod, gbm, half, ident, PS, load_w2, out)


MLP_STEPS = (
    ("stats", 2, 0), ("xt", 1, 0),
    ("second", -1, 0), ("first", 0, 0), ("second", -1, 1), ("first", 0, 1),
    ("turn_back", -2, 0), ("norm", 2, 0), ("first", 0, 2), ("first", 0, 3), ("xt_read", 1, 0),
    ("second", -1, 2), ("gelu", 0, 2), ("second", -1, 3), ("gelu", 0, 3), ("gate", -1, 0),
)
ROUTER_STEPS = (
    ("probs", 0, 0), ("weigh", 1, 0),
    ("hidden", 0, 0), ("stats", 2, 0),
    ("hidden", 0, 1), ("ctx_turn", 2, 0),
    ("hidden", 0, 2), ("keys", 2, 0), ("norm", 2, 0),
    ("hidden", 0, 3), ("w_turn", 1, 0),
    ("hidden", 0, 4), ("evidence", 1, 0),
    ("load", 3, 0), ("hidden", 0, 5), ("nx_turn", 2, 0), ("logits", 1, 0),
    ("hidden", 0, 6), ("nx_read", 2, 0),
    ("expert", 0, 0), ("scores", 2, 0), ("gate", 0, 0), ("exp", 2, 0), ("exp_logits", 1, 0),
    ("expert", 0, 1), ("expert", 0, 2), ("expert", 0, 3), ("finish", 0, 0),
)
NE = 3
NHC = 7
EH = 2 * NE


def over_groups(eng, steps, body):
    lags = [lag for _, lag, _ in steps]
    start = 1 - min(lags)
    pairs = (NG - max(lags) - start) // 2

    def iteration(j, t, in_loop):
        for name, lag, k in steps:
            g = t + lag if j is None else 2 * j + (t + lag)
            if in_loop or 0 <= g < NG:
                pair = (t + lag) // 2 if j is None else j + (t + lag) // 2
                body(name, g, k, (t + lag) % 2, pair)

    for i in range(-max(lags), start):
        iteration(None, i, False)
    with eng.Fori(0, pairs) as j:
        for t in range(start, start + 2):
            iteration(j, t, True)
    for i in range(start + 2 * pairs, NG - min(lags)):
        iteration(None, i, False)


def later(g):
    return not isinstance(g, int) or g > 0


def mlp_and_router(nc, stack, X, ctxin, w, vec, rows1, condT, mod, gbm, half, ident, PS, load_w2, out):
    def sb(name, shape, dt=F32):
        return stack.enter_context(nc.sbuf_tensor(name, shape, dt))

    def sem(name):
        return stack.enter_context(nc.semaphore(name))

    seen = sb("seen2", [P, 1])
    warm = sb("warm", [P, 1])
    XN = sb("m_XN", [P, GT])
    XT = sb("m_XT", [P, GT])
    H = sb("m_H", [P, 4, GT])
    YT = sb("m_YT", [P, GT])
    stat = sb("m_stat", [P, 2, GB, 6])
    mv = sb("m_mv", [P, 2, GB, 2])
    eps = sb("m_eps", [P, 2, GB])
    veps = sb("m_veps", [P, 2, GB])
    rstd = sb("m_rstd", [P, 2, GB])
    ones = sb("ones", [B, P])
    A = sb("A", [P, P])
    KEYS = sb("KEYS", [P, GT])
    REV = sb("REV", [P, NE])
    U = sb("U", [P, NHC * P])
    WO = sb("WO", [P, EH * P])
    ANC = sb("ANC", [P, NHC, B])
    BO = sb("BO", [P, GT])
    LOG32 = sb("LOG32", [B, NE])
    MASKED = sb("MASKED", [B, B, NE])
    RA = sb("RA", [P, B, NE])
    CTX = [sb(f"r_CTX{k}", [P, GB, P]) for k in range(2)]
    CTXT = sb("r_CTXT", [P, GT])
    RXN = sb("r_XN", [P, GT])
    NX = [sb(f"r_NX{k}", [P, GT]) for k in range(2)]
    E = sb("r_E", [P, GB, P])
    WN = sb("r_WN", [P, GB, P])
    WT = sb("r_WT", [P, GT])
    EV = [sb(f"r_EV{k}", [P, GT]) for k in range(2)]
    HID = sb("r_HID", [P, NHC, GT])
    nmax = sb("r_nmax", [P, GB])
    nbias = sb("r_nbias", [P, GB])
    esum = sb("r_esum", [P, GB])
    rsum = sb("r_rsum", [P, GB])
    LG = sb("r_LG", [P, GB, NE])
    lmax = sb("r_lmax", [P, GB])
    LS = sb("r_LS", [P, GB, NE])
    LE = sb("r_LE", [P, GB, NE])
    lsum = sb("r_lsum", [P, GB])
    lrec = sb("r_lrec", [P, GB])
    RP = sb("r_RP", [P, GB, NE])
    T = sb("r_T", [P, 2, NE * P])
    R = sb("r_R", [P, GB, P])
    GS = sb("r_GS", [P, GT])
    GTH = sb("r_GTH", [P, GT])
    D = sb("r_D", [P, GT])

    XT_BANK, FIRST_BANK, SECOND_BANK, BACK_BANK = PS[0], PS[1:5], PS[5], PS[6]
    HIDDEN_BANK, EXPERT_BANK, GATE_BANK, EVIDENCE_BANK, SCORE_BANK = PS[0:2], PS[2:4], PS[4], PS[5], PS[6:8]

    fills = sem("fills")
    d_stat = [sem(f"{k}_stat") for k in "mr"]
    d_mv = [sem(f"{k}_mv") for k in "mr"]
    d_var = [sem(f"{k}_var") for k in "mr"]
    d_rstd = [sem(f"{k}_rstd") for k in "mr"]
    d_norm = [sem(f"{k}_norm") for k in "mr"]
    xt_turned = sem("xt_turned")
    xt_read = sem("xt_read")
    first_done = sem("first_done")
    gelu_done = sem("gelu_done")
    second_done = sem("second_done")
    gated = sem("gated")
    turned_back = sem("turned_back")
    x_added = sem("x_added")
    derived_pe = sem("derived_pe")
    derived_act = sem("derived_act")
    derived_dve = sem("derived_dve")
    ctx_in = [sem(f"ctx_in{k}") for k in range(2)]
    ctx_turned = sem("ctx_turned")
    ctx_read = sem("ctx_read")
    keys_done = sem("keys_done")
    keys_read = sem("keys_read")
    nx_turned = sem("nx_turned")
    nx_read = sem("nx_read")
    scores_done = sem("scores_done")
    nmax_done = sem("nmax_done")
    nbias_done = sem("nbias_done")
    exps_done = sem("exps_done")
    rsum_done = sem("rsum_done")
    weights_done = sem("weights_done")
    w_turned = sem("w_turned")
    w_read = sem("w_read")
    evidence_done = sem("evidence_done")
    evidence_read = sem("evidence_read")
    logits_done = sem("logits_done")
    logits_read = sem("logits_read")
    lmax_done = sem("lmax_done")
    lshift_done = sem("lshift_done")
    lexp_done = sem("lexp_done")
    lsum_done = sem("lsum_done")
    lrec_done = sem("lrec_done")
    probs_done = sem("probs_done")
    hidden_done = sem("hidden_done")
    silu_done = sem("silu_done")
    expert_done = sem("expert_done")
    expert_read = sem("expert_read")
    routed = sem("routed")
    gate_done = sem("gate_done")
    gate_read = sem("gate_read")
    gate_tanh = sem("gate_tanh")
    delta_done = sem("delta_done")
    finished = sem("finished")
    out_done = sem("out_done")

    def x_batch(g, b):
        return X[:, bass.ds(g * GT + b * P, P)]

    def score_view(h):
        return SCORE_BANK[h][:, 0:2 * P].rearrange("p (b k) -> p b k", b=2)

    def logit_view(h):
        return SCORE_BANK[h][:, 2 * P:2 * P + 2 * NE].rearrange("p (b e) -> p b e", b=2)

    block = stack.enter_context(nc.Block())

    @block.sync
    def _(sp):
        def body(name, g, k, par, pair):
            if name == "load":
                if not isinstance(g, int) or g > 1:
                    sp.wait_ge(evidence_done, g - 1)
                sp.dma_start(CTX[par][:, :, :], ctxin[bass.ds(g * GB, GB)].rearrange("b p h -> p b h"))\
                    .then_inc(ctx_in[par], 16)
            elif name == "finish":
                sp.wait_ge(finished, g + 1)
                sp.dma_start(out[bass.ds(g * GB, GB)].rearrange("b p h -> p b h"),
                             X[:, bass.ds(g * GT, GT)].rearrange("p (b h) -> p b h", b=GB)).then_inc(out_done, 16)

        over_groups(sp, ROUTER_STEPS, body)
        sp.wait_ge(out_done, 16 * NG)

    @block.gpsimd
    def _(pool):
        nc.gpsimd.memset(ones[:, :], 1.0)
        nc.gpsimd.memset(eps[:, 0, :], 1e-6)
        nc.gpsimd.memset(eps[:, 1, :], 1e-5).then_inc(fills, 1)
        pool.wait_ge(fills, 1)

        def inverse_deviation(s, g):
            pool.wait_ge(d_mv[s], g + 1)
            nc.gpsimd.tensor_tensor(veps[:, s, :], mv[:, s, :, 1], eps[:, s, :], ALU.add).then_inc(d_var[s], 1)
            pool.wait_ge(d_var[s], g + 1)
            nc.gpsimd.tensor_tensor(rstd[:, s, :], veps[:, s, :], half[:, :], ALU.pow).then_inc(d_rstd[s], 1)

        def mlp(name, g, k, par, pair):
            if name == "stats":
                inverse_deviation(0, g)

        def router(name, g, k, par, pair):
            if name == "stats":
                inverse_deviation(1, g)

        over_groups(pool, MLP_STEPS, mlp)
        over_groups(pool, ROUTER_STEPS, router)

    @block.scalar
    def _(act):
        act.wait_ge(derived_pe, 2)
        for c in range(NHC):
            bias = vec("be1", c) if c < EH else vec("bg1")
            last = nc.scalar.activation(ANC[:, c, :], PS[5][:, c * B:(c + 1) * B], ACT.Identity, bias=bias)
        nc.scalar.activation(U[:, 0:GT], PS[1][:, :], ACT.Copy)
        nc.scalar.activation(U[:, GT:NHC * P], PS[2][:, 0:NHC * P - GT], ACT.Copy).then_inc(derived_act, 1)

        def gelu(g, k):
            act.wait_ge(first_done, 4 * g + (k + 1))
            if later(g):
                act.wait_ge(second_done, 4 * g + (k - 3))
            nc.scalar.activation(H[:, k, :], FIRST_BANK[k][:, :], ACT.Gelu_apprx_tanh, bias=vec("bmlp1", k))\
                .then_inc(gelu_done, 1)

        def mlp(name, g, k, par, pair):
            if name == "first" and k < 2 or name == "gelu":
                gelu(g, k)
            elif name == "xt_read":
                act.wait_ge(xt_turned, g + 1)
                if later(g):
                    act.wait_ge(first_done, 4 * g)
                for b in range(GB):
                    nb = bass.ds(g * GB + b, 1)
                    last = nc.scalar.activation(XT[:, b * P:(b + 1) * P], XT_BANK[:, b * P:(b + 1) * P],
                                                ACT.Identity, scale=mod[:, 4, nb], bias=mod[:, 3, nb])
                last.then_inc(xt_read, 1)

        def router(name, g, k, par, pair):
            if name == "hidden":
                act.wait_ge(hidden_done, NHC * g + (k + 1))
                for b in range(GB):
                    last = nc.scalar.activation(HID[:, k, b * P:(b + 1) * P], HIDDEN_BANK[k % 2][:, b * P:(b + 1) * P],
                                                ACT.Silu, bias=ANC[:, k, bass.ds(g * GB + b, 1)])
                last.then_inc(silu_done, 1)
            elif name == "ctx_turn":
                act.wait_ge(ctx_turned, g + 1)
                nc.scalar.activation(CTXT[:, :], EVIDENCE_BANK[:, :], ACT.Copy).then_inc(ctx_read, 1)
            elif name == "exp":
                act.wait_ge(nbias_done, g + 1)
                if later(g):
                    act.wait_ge(weights_done, g)
                for b in range(GB):
                    last = nc.scalar.activation(E[:, b, :], score_view(b // 2)[:, b % 2, :], ACT.Exp,
                                                scale=SCALE1, bias=nbias[:, b:b + 1], accum_out=esum[:, b:b + 1])
                last.then_inc(exps_done, 1)
            elif name == "exp_logits":
                act.wait_ge(lshift_done, g + 1)
                if later(g):
                    act.wait_ge(probs_done, g)
                nc.scalar.activation(LE[:, :, :], LS[:, :, :], ACT.Exp).then_inc(lexp_done, 1)
                nc.scalar.activation(warm[:, :], half[:, 0:1], ACT.Silu)
            elif name == "w_turn":
                act.wait_ge(w_turned, g + 1)
                nc.scalar.activation(WT[:, :], EVIDENCE_BANK[:, :], ACT.Copy).then_inc(w_read, 1)
            elif name == "gate":
                act.wait_ge(gate_read, g + 1)
                if later(g):
                    act.wait_ge(delta_done, g)
                nc.scalar.activation(GTH[:, :], GS[:, :], ACT.Tanh, scale=0.5).then_inc(gate_tanh, 1)

        over_groups(act, MLP_STEPS, mlp)
        over_groups(act, ROUTER_STEPS, router)

    @block.vector
    def _(dve):
        dve.wait_ge(derived_pe, 1)
        nc.vector.tensor_copy(LOG32[:, :], PS[0][0:B, 2 * P:2 * P + NE]).then_inc(derived_dve, 1)
        dve.wait_ge(derived_dve, 1)
        nc.vector.tensor_tensor(MASKED[:, :, :], ident[0:B, 0:B].unsqueeze(2).to_broadcast([B, B, NE]),
                                LOG32[:, :].unsqueeze(1).to_broadcast([B, B, NE]), ALU.mult).then_inc(derived_dve, 1)
        nc.vector.tensor_copy(A[:, :], PS[0][:, 0:P])
        nc.vector.tensor_copy(REV[:, :], PS[0][:, P:P + NE])
        dve.wait_ge(derived_pe, 2)
        nc.vector.tensor_copy(WO[:, 0:GT], PS[3][:, :])
        nc.vector.tensor_copy(WO[:, GT:EH * P], PS[4][:, 0:EH * P - GT])
        nc.vector.tensor_copy(BO[:, :], PS[6][:, :])
        dve.wait_ge(derived_pe, 3)
        nc.vector.tensor_copy(RA[:, :, :], PS[7][:, 0:NE * B].rearrange("p (b e) -> p b e", e=NE))\
            .then_inc(derived_dve, 1)

        def statistics(s, g):
            for b in range(GB):
                last = nc.vector.bn_stats(stat[:, s, b, :], x_batch(g, b))
            last.then_inc(d_stat[s], 1)
            dve.wait_ge(d_stat[s], g + 1)
            nc.vector.tensor_copy(seen[:, :], stat[:, s, GB - 1, 0:1])
            for b in range(GB):
                last = nc.vector.bn_aggr(mv[:, s, b, :], stat[:, s, b, :])
            last.then_inc(d_mv[s], 1)

        def normalise(s, g, to, turned):
            dve.wait_ge(d_rstd[s], g + 1)
            if later(g):
                dve.wait_ge(turned, g)
            for b in range(GB):
                last = nc.vector.tensor_scalar(to[:, b * P:(b + 1) * P], x_batch(g, b), mv[:, s, b, 0:1],
                                               rstd[:, s, b:b + 1], ALU.subtract, ALU.mult)
            last.then_inc(d_norm[s], 1)

        def mlp(name, g, k, par, pair):
            if name == "stats":
                statistics(0, g)
            elif name == "norm":
                normalise(0, g, XN, xt_turned)
            elif name == "gate":
                dve.wait_ge(second_done, 4 * g + 4)
                if later(g):
                    dve.wait_ge(turned_back, g)
                for b in range(GB):
                    nb = bass.ds(g * GB + b, 1)
                    last = nc.vector.tensor_scalar(YT[:, b * P:(b + 1) * P], SECOND_BANK[:, b * P:(b + 1) * P],
                                                   mod[:, 5, nb], gbm[:, nb], ALU.mult, ALU.add)
                last.then_inc(gated, 1)
            elif name == "turn_back":
                x = X[:, bass.ds(g * GT, GT)]
                dve.wait_ge(turned_back, g + 1)
                nc.vector.tensor_tensor(x, BACK_BANK[:, :], x, ALU.add).then_inc(x_added, 1)

        def router(name, g, k, par, pair):
            if name == "stats":
                statistics(1, g)
            elif name == "norm":
                normalise(1, g, RXN, nx_turned)
            elif name == "keys":
                dve.wait_ge(keys_done, g + 1)
                nc.vector.tensor_copy(KEYS[:, :], EVIDENCE_BANK[:, :]).then_inc(keys_read, 1)
            elif name == "nx_read":
                if not isinstance(g, int) or g > 1:
                    dve.wait_ge(hidden_done, NHC * (g - 1))
                dve.wait_ge(nx_turned, g + 1)
                nc.vector.tensor_scalar(NX[par][:, :], EVIDENCE_BANK[:, :], vec("gamma"), vec("beta"), ALU.mult,
                                        ALU.add).then_inc(nx_read, 1)
            elif name == "scores":
                dve.wait_ge(scores_done, g + 1)
                for h in range(2):
                    last = nc.vector.tensor_reduce(out=nmax[:, 2 * h:2 * h + 2], in_=score_view(h),
                                                   axis=AX.X, op=ALU.max, negate=True)
                last.then_inc(nmax_done, 1)
                dve.wait_ge(nmax_done, g + 1)
                nc.vector.tensor_scalar(nbias[:, :], nmax[:, :], SCALE1, None, ALU.mult).then_inc(nbias_done, 1)
            elif name == "probs":
                dve.wait_ge(lexp_done, g + 1)
                nc.vector.tensor_reduce(out=lsum[:, :], in_=LE[:, :, :], axis=AX.X, op=ALU.add)\
                    .then_inc(lsum_done, 1)
                dve.wait_ge(lsum_done, g + 1)
                nc.vector.reciprocal(lrec[:, :], lsum[:, :]).then_inc(lrec_done, 1)
                dve.wait_ge(lrec_done, g + 1)
                nc.vector.scalar_tensor_tensor(RP[:, :, :], LE[:, :, :], 0.5,
                                               lrec[:, :].unsqueeze(2).to_broadcast([P, GB, NE]), ALU.mult,
                                               ALU.mult).then_inc(probs_done, 1)
                dve.wait_ge(probs_done, g + 1)
            elif name == "weigh":
                dve.wait_ge(exps_done, g + 1)
                nc.vector.reciprocal(rsum[:, :], esum[:, :]).then_inc(rsum_done, 1)
                dve.wait_ge(rsum_done, g + 1)
                nc.vector.tensor_tensor(WN[:, :, :], E[:, :, :], rsum[:, :].unsqueeze(2).to_broadcast([P, GB, P]),
                                        ALU.mult).then_inc(weights_done, 1)
            elif name == "evidence":
                dve.wait_ge(evidence_done, g + 1)
                nc.vector.tensor_copy(EV[par][:, :], EVIDENCE_BANK[:, :]).then_inc(evidence_read, 1)
            elif name == "logits":
                dve.wait_ge(logits_done, g + 1)
                for h in range(2):
                    last = nc.vector.tensor_tensor(LG[:, 2 * h:2 * h + 2, :], logit_view(h),
                                                   RA[:, bass.ds(g * GB + 2 * h, 2), :], ALU.add)
                last.then_inc(logits_read, 1)
                dve.wait_ge(logits_read, g + 1)
                nc.vector.tensor_reduce(out=lmax[:, :], in_=LG[:, :, :], axis=AX.X, op=ALU.max)\
                    .then_inc(lmax_done, 1)
                dve.wait_ge(lmax_done, g + 1)
                nc.vector.tensor_tensor(LS[:, :, :], LG[:, :, :], lmax[:, :].unsqueeze(2).to_broadcast([P, GB, NE]),
                                        ALU.subtract).then_inc(lshift_done, 1)
            elif name == "gate":
                dve.wait_ge(gate_done, g + 1)
                if later(g):
                    dve.wait_ge(gate_tanh, g)
                gate_bias = BO[:, NE * P:GT].unsqueeze(1).to_broadcast([P, GB, P])
                nc.vector.tensor_tensor(GS[:, :].rearrange("p (b c) -> p b c", b=GB),
                                        GATE_BANK[:, :].rearrange("p (b c) -> p b c", b=GB), gate_bias, ALU.add)\
                    .then_inc(gate_read, 1)
            elif name == "expert":
                b, t = k, T[:, k % 2, :]
                dve.wait_ge(expert_done, GB * g + (b + 1))
                nc.vector.tensor_tensor(t, EXPERT_BANK[b % 2][:, 0:NE * P], BO[:, 0:NE * P], ALU.add)\
                    .then_inc(expert_read, 1)
                dve.wait_ge(expert_read, GB * g + (b + 1))
                nc.vector.tensor_scalar(R[:, b, :], t[:, 0:P], RP[:, b, 0:1], None, ALU.mult).then_inc(routed, 1)
                for e in range(1, NE):
                    dve.wait_ge(routed, NE * GB * g + (NE * b + e))
                    nc.vector.scalar_tensor_tensor(R[:, b, :], t[:, e * P:(e + 1) * P], RP[:, b, e:e + 1], R[:, b, :],
                                                   ALU.mult, ALU.add).then_inc(routed, 1)
            elif name == "finish":
                x = X[:, bass.ds(g * GT, GT)]
                dve.wait_ge(routed, NE * GB * g + NE * GB)
                dve.wait_ge(gate_tanh, g + 1)
                nc.vector.scalar_tensor_tensor(D[:, :], GTH[:, :], 1.0, R[:, :, :].rearrange("p b c -> p (b c)"),
                                               ALU.add, ALU.mult).then_inc(delta_done, 1)
                dve.wait_ge(delta_done, g + 1)
                nc.vector.tensor_tensor(x, D[:, :], x, ALU.add).then_inc(finished, 1)

        over_groups(dve, MLP_STEPS, mlp)
        dve.wait_ge(x_added, NG)
        over_groups(dve, ROUTER_STEPS, router)

    @block.tensor
    def _(pe):
        def product(to, lhsT, rhs, start=True, stop=True):
            return nc.tensor.matmul(to, lhsT, rhs, start=start, stop=stop)

        pe.wait_ge(load_w2, 32)
        pe.wait_ge(fills, 1)
        product(PS[0][:, 0:P], w("wkT"), w("wqT"))
        product(PS[0][:, P:P + NE], w("wvT"), w("r_ev"))
        product(PS[0][0:B, 2 * P:2 * P + NE], condT[:, :], w("r_an"), stop=False)
        product(PS[0][0:B, 2 * P:2 * P + NE], ones[0:1, 0:B], rows1[0:1, 2 * P:2 * P + NE], start=False)\
            .then_inc(derived_pe, 1)
        product(PS[1][:, :], w("wvT"), w("e_ev", 0, GT))
        product(PS[2][:, 0:EH * P - GT], w("wvT"), w("e_ev", GT, EH * P - GT))
        product(PS[2][:, EH * P - GT:NHC * P - GT], w("wvT"), w("g_ev"))
        for c in range(NHC):
            product(PS[5][:, c * B:(c + 1) * B], w("e_an", c * P, P) if c < EH else w("g_an"), condT[:, :])
        for c in range(EH):
            product(PS[3 + c // 4][:, (c % 4) * P:(c % 4 + 1) * P], w("e2T", c * P, P), w("outw"))
        for e in range(NE):
            product(PS[6][:, e * P:(e + 1) * P], vec("be2", e).to_broadcast([P, P]), w("outw"), stop=False)
            product(PS[6][:, e * P:(e + 1) * P], ones[0:1, :], rows1[0:1, 0:P], start=False)
        product(PS[6][:, NE * P:GT], ones[0:1, :], rows1[0:1, P:2 * P]).then_inc(derived_pe, 1)
        pe.wait_ge(derived_dve, 2)
        product(PS[7][:, 0:NE * B], ones[:, :], MASKED[:, :, :].rearrange("p b e -> p (b e)"))\
            .then_inc(derived_pe, 1)
        pe.wait_ge(derived_act, 1)
        pe.wait_ge(derived_dve, 3)

        def turn(bank, source):
            for b in range(GB):
                last = nc.tensor.transpose(bank[:, b * P:(b + 1) * P], source(b), ident[:, :])
            return last

        def mlp(name, g, k, par, pair):
            if name == "xt":
                pe.wait_ge(d_norm[0], g + 1)
                if later(g):
                    pe.wait_ge(xt_read, g)
                turn(XT_BANK, lambda b: XN[:, b * P:(b + 1) * P]).then_inc(xt_turned, 1)
            elif name == "first":
                if k == 0:
                    pe.wait_ge(xt_read, g + 1)
                if later(g):
                    pe.wait_ge(gelu_done, 4 * g + (k - 3))
                product(FIRST_BANK[k][:, :], w("mlp1", k * P, P), XT[:, :]).then_inc(first_done, 1)
            elif name == "second":
                if k == 0 and later(g):
                    pe.wait_ge(gated, g)
                pe.wait_ge(gelu_done, 4 * g + (k + 1))
                product(SECOND_BANK[:, :], w("mlp2", k * P, P), H[:, k, :], start=k == 0, stop=k == 3)\
                    .then_inc(second_done, 1)
            elif name == "turn_back":
                pe.wait_ge(gated, g + 1)
                if later(g):
                    pe.wait_ge(x_added, g)
                turn(BACK_BANK, lambda b: YT[:, b * P:(b + 1) * P]).then_inc(turned_back, 1)

        def router(name, g, k, par, pair):
            if name == "ctx_turn":
                pe.wait_ge(ctx_in[par], 16 * (pair + 1))
                if later(g):
                    pe.wait_ge(nx_read, g)
                turn(EVIDENCE_BANK, lambda b: CTX[par][:, b, :]).then_inc(ctx_turned, 1)
            elif name == "keys":
                pe.wait_ge(ctx_read, g + 1)
                product(EVIDENCE_BANK[:, :], A[:, :], CTXT[:, :]).then_inc(keys_done, 1)
            elif name == "nx_turn":
                pe.wait_ge(d_norm[1], g + 1)
                pe.wait_ge(keys_read, g + 1)
                if later(g):
                    pe.wait_ge(evidence_read, g)
                turn(EVIDENCE_BANK, lambda b: RXN[:, b * P:(b + 1) * P]).then_inc(nx_turned, 1)
            elif name == "scores":
                pe.wait_ge(nx_read, g + 1)
                if later(g):
                    pe.wait_ge(logits_read, g)
                for b in range(GB):
                    last = product(score_view(b // 2)[:, b % 2, :], NX[par][:, b * P:(b + 1) * P],
                                   KEYS[:, b * P:(b + 1) * P])
                last.then_inc(scores_done, 1)
            elif name == "w_turn":
                pe.wait_ge(weights_done, g + 1)
                if not isinstance(g, int) or g + 1 < NG:
                    pe.wait_ge(keys_read, g + 2)
                else:
                    pe.wait_ge(nx_read, NG)
                turn(EVIDENCE_BANK, lambda b: WN[:, b, :]).then_inc(w_turned, 1)
            elif name == "evidence":
                pe.wait_ge(w_read, g + 1)
                for b in range(GB):
                    last = product(EVIDENCE_BANK[:, b * P:(b + 1) * P], CTX[par][:, b, :], WT[:, b * P:(b + 1) * P])
                last.then_inc(evidence_done, 1)
            elif name == "logits":
                pe.wait_ge(evidence_read, g + 1)
                for b in range(GB):
                    to, batch = logit_view(b // 2)[:, b % 2, :], slice(b * P, (b + 1) * P)
                    product(to, NX[par][:, batch], w("r_nx"), stop=False)
                    last = product(to, EV[par][:, batch], REV[:, :], start=False)
                last.then_inc(logits_done, 1)
            elif name == "hidden":
                if k == 0:
                    pe.wait_ge(nx_read, g + 1)
                    pe.wait_ge(evidence_read, g + 1)
                if k > 1:
                    pe.wait_ge(silu_done, NHC * g + (k - 1))
                elif later(g):
                    pe.wait_ge(silu_done, NHC * g)
                nx = w("e_nx", k * P, P) if k < EH else w("g_nx")
                product(HIDDEN_BANK[k % 2][:, :], nx, NX[par][:, :], stop=False)
                product(HIDDEN_BANK[k % 2][:, :], U[:, k * P:(k + 1) * P], EV[par][:, :], start=False)\
                    .then_inc(hidden_done, 1)
            elif name == "expert":
                b = k
                if b == 0:
                    pe.wait_ge(silu_done, NHC * g + EH)
                if b > 1 or later(g):
                    pe.wait_ge(expert_read, GB * g + (b - 1))
                for e in range(NE):
                    for c in range(2):
                        last = product(EXPERT_BANK[b % 2][:, e * P:(e + 1) * P],
                                       HID[:, 2 * e + c, b * P:(b + 1) * P],
                                       WO[:, (2 * e + c) * P:(2 * e + c + 1) * P], start=c == 0, stop=c == 1)
                last.then_inc(expert_done, 1)
            elif name == "gate":
                pe.wait_ge(silu_done, NHC * g + NHC)
                if later(g):
                    pe.wait_ge(gate_read, g)
                for b in range(GB):
                    last = product(GATE_BANK[:, b * P:(b + 1) * P], HID[:, EH, b * P:(b + 1) * P], w("gate2"))
                last.then_inc(gate_done, 1)

        over_groups(pe, MLP_STEPS, mlp)
        pe.wait_ge(gelu_done, 4 * NG)
        pe.wait_ge(x_added, NG)
        over_groups(pe, ROUTER_STEPS, router)


_OUT = ((B, P, P), "float32")


def head_channel_last_to_stack(a):
    n = a.shape[0]
    return a.reshape(n, 2, NJ, HD).transpose(0, 1, 3, 2).reshape(n, P)


def rows_of_chunks(a):
    k, n = a.shape[0] // P, a.shape[1]
    return a.reshape(k, P, n).transpose(1, 0, 2).reshape(P, k * n)


def pack(inputs):
    import numpy as np
    a = {k: np.asarray(v) for k, v in inputs.items()}
    l0 = {k[9:]: v for k, v in a.items() if k.startswith("L0_")}
    l1 = {k[9:]: v for k, v in a.items() if k.startswith("L1_")}
    qkv, kvc = l0["W_qkv"], l0["W_kvc"]
    ew1, gw1, rw = l1["e_w1"], l1["gate_w1"], l1["router_W"]

    def experts(lo):
        return ew1[:, lo:lo + P, :].transpose(1, 0, 2).reshape(P, -1)

    w = {
        "mod": l0["W_mod"],
        "q": head_channel_last_to_stack(qkv[:, 0:P]), "k": head_channel_last_to_stack(qkv[:, P:2 * P]),
        "v": qkv[:, 2 * P:], "proj": l0["W_proj"],
        "qc": head_channel_last_to_stack(l0["W_qc"]), "kc": head_channel_last_to_stack(kvc[:, 0:P]),
        "vc": kvc[:, P:], "cproj": l0["W_cproj"],
        "mlp1": l0["W_mlp1"], "mlp2": rows_of_chunks(l0["W_mlp2"]),
        "wqT": l1["Wq"].T, "wkT": l1["Wk"].T, "wvT": l1["Wv"].T,
        "r_nx": rw[0:P], "r_ev": rw[P:2 * P], "r_an": rw[2 * P:],
        "e_nx": experts(0), "g_nx": gw1[0:P], "e_ev": experts(P), "g_ev": gw1[P:2 * P],
        "e_an": experts(2 * P), "g_an": gw1[2 * P:], "gate2": l1["gate_w2"],
        "e2T": l1["e_w2"].transpose(2, 0, 1).reshape(P, -1), "outw": l1["out_w"],
    }
    bq = l0["b_qkv"]
    v = {
        "bmod": l0["b_mod"].reshape(6, P).T,
        "bq": head_channel_last_to_stack(bq[None, 0:P]).T, "bk": head_channel_last_to_stack(bq[None, P:2 * P]).T,
        "bv": bq[2 * P:, None], "bproj": l0["b_proj"][:, None],
        "bqc": head_channel_last_to_stack(l0["b_qc"][None]).T,
        "bkc": head_channel_last_to_stack(l0["b_kvc"][None, 0:P]).T, "bvc": l0["b_kvc"][P:, None],
        "bcproj": l0["b_cproj"][:, None], "bmlp1": l0["b_mlp1"].reshape(4, P).T, "bmlp2": l0["b_mlp2"][:, None],
        "gamma": l1["ln_gamma"][:, None], "beta": l1["ln_beta"][:, None],
        "be1": l1["e_b1"].reshape(6, P).T, "bg1": l1["gate_b1"][:, None], "be2": l1["e_b2"].T,
    }
    rows = np.concatenate([l1["out_b"], l1["gate_b2"], l1["router_b"]])[None]
    return {
        "x": a["x"], "cond": a["cond_1024"], "ctx": a["ctx_1024"],
        "weights": np.ascontiguousarray(np.concatenate([w[k] for k in W_COLS], axis=1)),
        "vectors": np.ascontiguousarray(np.concatenate([v[k] for k in V_COLS], axis=1)),
        "ident": np.eye(P, dtype=np.float32), "rows": np.ascontiguousarray(rows),
    }


def kernel(**inputs):
    import concourse.bacc as bacc
    from concourse.bass_utils import run_bass_kernel_spmd

    nc = bacc.Bacc("TRN2", target_bir_lowering=False, num_devices=1)
    arrays, args = {}, []
    for name, a in pack(inputs).items():
        arrays[f"in_{name}"] = a
        args.append(nc.dram_tensor(f"in_{name}", a.shape, mybir.dt.from_np(a.dtype), kind="ExternalInput").ap())
    args.append(nc.dram_tensor("out", _OUT[0], F32, kind="ExternalOutput").ap())
    build_block(nc, *args)
    r = run_bass_kernel_spmd(nc, [arrays], core_ids=[0])
    return r.results[0]["out"]
```

```python
import concourse.bass as bass
from concourse import mybir
from contextlib import ExitStack

F32 = mybir.dt.float32
BF16 = mybir.dt.bfloat16
F32R = mybir.dt.float32r
ALU = mybir.AluOpType
ACT = mybir.ActivationFunctionType
AX = mybir.AxisListType

P = 128
B = 32
GB = 4
NG = B // GB
GT = GB * P
NH = 16
HD = P // NH
NJ = NH // 2
VW = 32
NCORE = 2 * B
SCALE = float(HD) ** -0.5
SCALE1 = float(P) ** -0.5
Q_PART = (0, 1, 2, 0, 1, 0)
K_PART = (0, 0, 0, 1, 1, 2)
Q_ROWS, K_ROWS = (sorted(range(6), key=lambda r: part[r]) for part in (Q_PART, K_PART))
MAX_ROW = 6
HALF_DMAS = 16 * (len(Q_PART) + len(K_PART) + 1)

W_COLS = {}
_at = 0
for _name, _n in (("mod", 6 * P), ("q", P), ("k", P), ("v", P), ("proj", P), ("qc", P), ("kc", P), ("vc", P),
                  ("cproj", P), ("mlp1", 4 * P), ("mlp2", 4 * P), ("wqT", P), ("wkT", P), ("wvT", P),
                  ("r_nx", 3), ("r_ev", 3), ("r_an", 3), ("e_nx", 6 * P), ("g_nx", P), ("e_ev", 6 * P), ("g_ev", P),
                  ("e_an", 6 * P), ("g_an", P), ("gate2", P), ("e2T", 6 * P), ("outw", P)):
    W_COLS[_name] = (_at, _n)
    _at += _n
W_TOTAL = _at
V_COLS = {}
_at = 0
for _name, _n in (("bmod", 6), ("bq", 1), ("bk", 1), ("bv", 1), ("bproj", 1), ("bqc", 1), ("bkc", 1), ("bvc", 1),
                  ("bcproj", 1), ("bmlp1", 4), ("bmlp2", 1), ("gamma", 1), ("beta", 1), ("be1", 6), ("bg1", 1),
                  ("be2", 3)):
    V_COLS[_name] = (_at, _n)
    _at += _n
V_TOTAL = _at


class Core:

    def __init__(self, n, mod, pairs, kind, group, b):
        self.n, self.mod, self.pairs, self.kind, self.group, self.b = n, mod, pairs, kind, group, b


def core_at(i, s, steady):
    kind, b = (0, s) if s < GB else (1, s - GB)
    g = i - kind
    if steady:
        return Core(8 * i + (s - GB), (s + GB) % 8, 4 * i + (s - GB) // 2, kind, g, b)
    if not 0 <= g < NG:
        return None
    n = s if i == 0 else NCORE - GB + b if i == NG else 8 * i + (s - GB)
    return Core(n, n % 8, n // 2, kind, g, b)


GROUP_STEPS = sorted([
    (0.9, "load", "ln_c", 0, 0),
    (0.5, "stats", "ln_s", 1, 0), (1.5, "stats", "ln_s", 1, 1),
    (3.0, "norm", "ln_s", 1, 0),
    (1.9, "fill", "v_c", -1, 0), (2.0, "read", "v_c", -1, 1),
    (6.4, "fill", "xt_s", 1, 0), (6.5, "read", "xt_s", 1, 0), (6.6, "read", "xt_s", 1, 1),
    (8.9, "fill", "q_s", 1, 0), (9.0, "read", "q_s", 1, 0), (9.4, "read", "q_s", 1, 1),
    (8.6, "stats", "ln_c", 0, 0), (9.6, "stats", "ln_c", 0, 1),
    (10.9, "fill", "k_s", 1, 0), (11.0, "read", "k_s", 1, 0), (11.4, "read", "k_s", 1, 1),
    (12.9, "fill", "proj_c", -2, 0), (13.0, "read", "proj_c", -2, 1),
    (14.9, "fill", "yt_c", -2, 0), (15.0, "read", "yt_c", -2, 1),
    (13.0, "norm", "ln_c", 0, 0),
    (16.9, "fill", "xt_c", 0, 0), (17.0, "read", "xt_c", 0, 1),
    (18.9, "fill", "k_c", 0, 0), (19.0, "read", "k_c", 0, 0), (19.4, "read", "k_c", 0, 1),
    (20.9, "fill", "v_s", 1, 0), (21.0, "read", "v_s", 1, 1),
    (22.5, "fill", "proj_s", 0, 0), (23.0, "read", "proj_s", 0, 0), (23.1, "read", "proj_s", 0, 1),
    (24.0, "fill", "yt_s", 0, 0), (24.4, "read", "yt_s", 0, 1),
    (25.0, "stats", "ln_x", 0, 0), (25.1, "stats", "ln_x", 0, 1),
    (26.5, "norm", "ln_x", 0, 0), (26.6, "norm", "ln_x", 0, 1), (26.7, "norm", "ln_x", 0, 2),
    (26.8, "norm", "ln_x", 0, 3),
    (28.5, "fill", "xt_x", 0, 0), (28.9, "read", "xt_x", 0, 1),
    (29.5, "fill", "q_c", 0, 0), (30.0, "read", "q_c", 0, 0), (30.1, "read", "q_c", 0, 1),
])
BANK_ORDER = [name for _, step, name, _, _ in GROUP_STEPS if step == "fill"]
BANK_LAG = {name: lag for _, step, name, lag, _ in GROUP_STEPS if step == "fill"}


def stack_steps():
    def moves(what, h):
        return [(what, r, h) for r in {"zero": [0], "Q": Q_ROWS, "K": K_ROWS}[what]]

    own = moves("zero", 0) + moves("Q", 0) + moves("K", 0) + moves("zero", 1) + moves("Q", 1) + moves("K", 1)
    steps = [(12 + k // 2, 0, 1, *m, (1, 3)[m[2]]) for k, m in enumerate(own)]
    steps += [(26 + k // 2, 1, 0, *m, 5) for k, m in enumerate(moves("zero", 0) + moves("K", 0))]
    q, k = moves("Q", 0), moves("K", 1)
    rest = q[0:3] + moves("zero", 1) + q[3:6] + k + moves("Q", 1)
    steps += [(k // 2, 1, -1, *m, (-3, -1)[m[2]]) for k, m in enumerate(rest)]
    return steps


STACK_STEPS = stack_steps()


def attention_events(i, steady=False):
    def valid(g):
        return steady or 0 <= g < NG

    def before(name):
        at, it = BANK_ORDER.index(name), i
        while True:
            at -= 1
            if at < 0:
                at, it = len(BANK_ORDER) - 1, it - 1
                if not steady and it < -1:
                    return None
            g = it + BANK_LAG[BANK_ORDER[at]]
            if valid(g):
                return BANK_ORDER[at], g

    def group_steps(start, end):
        for t, step, name, lag, part in GROUP_STEPS:
            if start <= t < end and valid(i + lag):
                if step == "fill":
                    last = {"proj_s": core_at(i, 3, steady), "proj_c": core_at(i - 1, 7, steady)}.get(name)
                    yield (step, name, i + lag, before(name), last)
                else:
                    yield (step, name, i + lag, part)

    for s in range(8):
        here = core_at(i, s, steady)
        back1 = core_at(i, s - 1, steady) if s else core_at(i - 1, 7, steady)
        back2 = core_at(i, s - 2, steady) if s > 1 else core_at(i - 1, s + 6, steady)
        ahead1 = core_at(i, s + 1, steady) if s < 7 else core_at(i + 1, 0, steady)
        ahead2 = core_at(i, s + 2, steady) if s < 6 else core_at(i + 1, s - 6, steady)
        ahead3 = core_at(i, s + 3, steady) if s < 5 else core_at(i + 1, s - 5, steady)
        for u in range(4):
            if not steady and (i, s, u) == (NG, 1, 0):
                yield ("between",)
            if not steady and (i, s, u) == (0, 0, 0):
                yield ("load_rest",)
            if not steady and (i, s, u) == (NG - 1, 7, 0):
                yield ("start",)
            if not steady and (i, s, u) == (-1, 5, 1):
                yield ("derive",)
            if not steady and (i, s, u) == (NG + 1, 2, 0):
                yield ("behind",)
            for t, kind, lag, what, r, h, slot in STACK_STEPS:
                if t == 4 * s + u and valid(i + lag):
                    last = core_at(i, slot, steady) if slot >= 0 else core_at(i - 1, slot + 8, steady)
                    yield ("stack", kind, i + lag, last, what, r, h)
            if u == 3 and back1:
                yield ("o_turn", back1)
            if u == 2 and ahead2:
                yield ("max_parts", ahead2)
            if u == 2 and back2:
                yield ("o_back", back2, back2.n + 1 + bool(back1) + bool(here) + bool(ahead1))
            yield from group_steps(4 * s + u, 4 * s + u + 0.5)
            scored = ahead2 if u < 2 else ahead3
            if scored:
                yield ("score", scored, (u + 2) % 4)
            if here:
                yield ("shifted", here, u)
            if u > 1 and here:
                yield ("value", here, u - 2)
            if u < 2 and back1:
                yield ("value", back1, u + 2)
            if u == 3 and back1:
                yield ("o_norm", back1)
            if u == 3 and ahead2:
                yield ("max_turn", ahead2, ahead2.n - bool(ahead1) - bool(here) - bool(back1))
            yield from group_steps(4 * s + u + 0.5, 4 * s + u + 1)


MLP_STEPS = (
    ("stats", 2, 0), ("xt", 1, 0),
    ("first", 0, 0), ("second", -1, 0), ("first", 0, 1), ("second", -1, 1),
    ("turn_back", -2, 0), ("norm", 2, 0), ("first", 0, 2), ("first", 0, 3), ("xt_read", 1, 0),
    ("second", -1, 2), ("gelu", 0, 2), ("second", -1, 3), ("gelu", 0, 3), ("gate", -1, 0),
)
ROUTER_STEPS = (
    ("probs", 0, 0), ("weigh", 1, 0),
    ("hidden", 0, 0), ("stats", 2, 0),
    ("hidden", 0, 1), ("ctx_turn", 2, 0),
    ("hidden", 0, 2), ("keys", 2, 0), ("norm", 2, 0),
    ("hidden", 0, 3), ("w_turn", 1, 0),
    ("hidden", 0, 4), ("evidence", 1, 0),
    ("load", 3, 0), ("hidden", 0, 5), ("nx_turn", 2, 0), ("logits", 1, 0),
    ("hidden", 0, 6), ("nx_read", 2, 0),
    ("expert", 0, 0), ("scores", 2, 0), ("gate", 0, 0), ("exp", 2, 0), ("exp_logits", 1, 0),
    ("expert", 0, 1), ("expert", 0, 2), ("expert", 0, 3), ("finish", 0, 0),
)
NE = 3
NHC = 7
EH = 2 * NE


def valid_steps(steps, i):
    return [(name, i + lag, k, (i + lag) % 2, (i + lag) // 2) for name, lag, k in steps if 0 <= i + lag < NG]


def start_mlp(body):
    for step in valid_steps(MLP_STEPS, -2):
        body(*step)


def between_cores(body):
    for i in range(-1, 2):
        for step in valid_steps(MLP_STEPS, i):
            body(*step)


def behind_cores(body):
    for step in valid_steps(MLP_STEPS, 2):
        body(*step)


def rest_of_groups(eng, mlp, router, before_router, before_shared=lambda: None):
    with eng.Fori(3, NG - 2) as i:
        for name, lag, k in MLP_STEPS:
            mlp(name, i + lag, k, 0, 0)
    before_shared()
    for i in range(NG - 2, NG + 2):
        a, b = valid_steps(MLP_STEPS, i), valid_steps(ROUTER_STEPS, i - NG - 1) if i < NG + 1 else []
        for at in range(max(len(a), len(b))):
            if at < len(a):
                mlp(*a[at])
            for step in b[len(b) * at // max(len(a), len(b)):len(b) * (at + 1) // max(len(a), len(b))]:
                router(*step)
    before_router()
    pairs = (NG - 3 - 1) // 2
    for step in valid_steps(ROUTER_STEPS, 0):
        router(*step)
    with eng.Fori(0, pairs) as j:
        for t in range(1, 3):
            for name, lag, k in ROUTER_STEPS:
                router(name, 2 * j + (t + lag), k, (t + lag) % 2, j + (t + lag) // 2)
    for i in range(1 + 2 * pairs, NG):
        for step in valid_steps(ROUTER_STEPS, i):
            router(*step)


def later(g):
    return not isinstance(g, int) or g > 0


def mlp_and_router(nc, stack, X, ctxin, w, vec, rows1, condT, mod, gbm, half, zeros, ident, PS, load_w2, out,
                   attended, max_done, exp_done, o_normed, o_stored):
    def sb(name, shape, dt=F32):
        return stack.enter_context(nc.sbuf_tensor(name, shape, dt))

    def sem(name):
        return stack.enter_context(nc.semaphore(name))

    reused = ExitStack()

    def rb(name, shape, dt=F32):
        return reused.enter_context(nc.sbuf_tensor(name, shape, dt))

    seen = sb("seen2", [P, 1])
    warm = sb("warm", [P, 1])
    XN = sb("m_XN", [P, GT])
    XT = sb("m_XT", [P, GT])
    H = sb("m_H", [P, 4, GT])
    YT = sb("m_YT", [P, GT])
    stat = sb("m_stat", [P, 2, GB, 6])
    mv = sb("m_mv", [P, 2, GB, 2])
    eps = sb("m_eps", [P, 2, GB])
    veps = sb("m_veps", [P, 2, GB])
    rstd = sb("m_rstd", [P, 2, GB])
    ones = sb("ones", [B, P])
    A = sb("A", [P, P])
    KEYS = sb("KEYS", [P, GT])
    REV = sb("REV", [P, NE])
    U = sb("U", [P, NHC * P])
    WO = sb("WO", [P, EH * P])
    ANC = sb("ANC", [P, NHC, B])
    BO = sb("BO", [P, GT])
    LOG32 = sb("LOG32", [B, NE])
    MASKED = sb("MASKED", [B, B, NE])
    RA = sb("RA", [P, B, NE])
    CTX = [rb(f"r_CTX{k}", [P, GB, P]) for k in range(2)]
    CTXT = rb("r_CTXT", [P, GT])
    RXN = rb("r_XN", [P, GT])
    NX = [rb(f"r_NX{k}", [P, GT]) for k in range(2)]
    E = rb("r_E", [P, GB, P])
    WN = rb("r_WN", [P, GB, P])
    WT = rb("r_WT", [P, GT])
    EV = [rb(f"r_EV{k}", [P, GT]) for k in range(2)]
    HID = rb("r_HID", [P, NHC, GT])
    NXS = [rb(f"r_NXS{k}", [P, 2, GT], F32R) for k in range(2)]
    EVS = [rb(f"r_EVS{k}", [P, 2, GT], F32R) for k in range(2)]
    WNS = rb("r_WNS", [P, 2, NHC * P], F32R)
    US = rb("r_US", [P, 2, NHC * P], F32R)
    nmax = rb("r_nmax", [P, GB])
    nbias = rb("r_nbias", [P, GB])
    esum = rb("r_esum", [P, GB])
    rsum = rb("r_rsum", [P, GB])
    LG = rb("r_LG", [P, GB, NE])
    lmax = rb("r_lmax", [P, GB])
    LS = rb("r_LS", [P, GB, NE])
    LE = rb("r_LE", [P, GB, NE])
    lsum = rb("r_lsum", [P, GB])
    lrec = rb("r_lrec", [P, GB])
    RP = rb("r_RP", [P, GB, NE])
    T = rb("r_T", [P, 2, NE * P])
    R = rb("r_R", [P, GB, P])
    GS = rb("r_GS", [P, GT])
    GTH = rb("r_GTH", [P, GT])
    D = rb("r_D", [P, GT])

    reused.close()
    XT_BANK, FIRST_BANK, SECOND_BANK, BACK_BANK = PS[0], PS[1:3], PS[3], PS[4]
    HIDDEN_BANK, EXPERT_BANK, GATE_BANK, EVIDENCE_BANK, SCORE_BANK = PS[0:2], PS[2:4], PS[4], PS[5], PS[6:8]

    fills = sem("fills")
    d_stat = [sem(f"{k}_stat") for k in "mr"]
    d_mv = [sem(f"{k}_mv") for k in "mr"]
    d_var = [sem(f"{k}_var") for k in "mr"]
    d_rstd = [sem(f"{k}_rstd") for k in "mr"]
    d_norm = [sem(f"{k}_norm") for k in "mr"]
    xt_turned = sem("xt_turned")
    xt_read = sem("xt_read")
    first_done = sem("first_done")
    gelu_done = sem("gelu_done")
    second_done = sem("second_done")
    gated = sem("gated")
    turned_back = sem("turned_back")
    x_added = sem("x_added")
    derived_pe = sem("derived_pe")
    derived_act = sem("derived_act")
    derived_dve = sem("derived_dve")
    ctx_in = [sem(f"ctx_in{k}") for k in range(2)]
    ctx_turned = sem("ctx_turned")
    ctx_read = sem("ctx_read")
    keys_done = sem("keys_done")
    keys_read = sem("keys_read")
    nx_turned = sem("nx_turned")
    nx_read = sem("nx_read")
    nx_high = sem("nx_high")
    nx_split = sem("nx_split")
    ev_high = sem("ev_high")
    ev_split = sem("ev_split")
    weights_high = sem("weights_high")
    weights_split = sem("weights_split")
    scores_done = sem("scores_done")
    nmax_done = sem("nmax_done")
    nbias_done = sem("nbias_done")
    exps_done = sem("exps_done")
    rsum_done = sem("rsum_done")
    weights_done = sem("weights_done")
    w_turned = sem("w_turned")
    w_read = sem("w_read")
    evidence_done = sem("evidence_done")
    evidence_read = sem("evidence_read")
    logits_done = sem("logits_done")
    logits_read = sem("logits_read")
    lmax_done = sem("lmax_done")
    lshift_done = sem("lshift_done")
    lexp_done = sem("lexp_done")
    lsum_done = sem("lsum_done")
    lrec_done = sem("lrec_done")
    probs_done = sem("probs_done")
    hidden_done = sem("hidden_done")
    silu_done = sem("silu_done")
    expert_done = sem("expert_done")
    expert_read = sem("expert_read")
    routed = sem("routed")
    gate_done = sem("gate_done")
    gate_read = sem("gate_read")
    gate_tanh = sem("gate_tanh")
    delta_done = sem("delta_done")
    finished = sem("finished")
    out_done = sem("out_done")

    def x_batch(g, b):
        return X[:, bass.ds(g * GT + b * P, P)]

    def score_view(h):
        return SCORE_BANK[h][:, 0:2 * P].rearrange("p (b k) -> p b k", b=2)

    def logit_view(h):
        return SCORE_BANK[h][:, 2 * P:2 * P + 2 * NE].rearrange("p (b e) -> p b e", b=2)

    def nothing():
        pass

    def sync_programs(sp):
        def body(name, g, k, par, pair):
            if name == "load":
                if not isinstance(g, int) or g > 1:
                    sp.wait_ge(evidence_done, g - 1)
                sp.dma_start(CTX[par][:, :, :], ctxin[bass.ds(g * GB, GB)].rearrange("b p h -> p b h"))\
                    .then_inc(ctx_in[par], 16)
            elif name == "finish":
                sp.wait_ge(finished, g + 1)
                sp.dma_start(out[bass.ds(g * GB, GB)].rearrange("b p h -> p b h"),
                             X[:, bass.ds(g * GT, GT)].rearrange("p (b h) -> p b h", b=GB)).then_inc(out_done, 16)

        def rest():
            sp.wait_ge(attended, NG)
            rest_of_groups(sp, lambda *step: None, body, nothing)
            sp.wait_ge(out_done, 16 * NG)

        return {}, rest

    def gpsimd_programs(pool):
        nc.gpsimd.memset(ones[:, :], 1.0)
        nc.gpsimd.memset(eps[:, 0, :], 1e-6)
        nc.gpsimd.memset(eps[:, 1, :], 1e-5).then_inc(fills, 1)
        pool.wait_ge(fills, 1)

        def inverse_deviation(s, g):
            pool.wait_ge(d_mv[s], g + 1)
            nc.gpsimd.tensor_tensor(veps[:, s, :], mv[:, s, :, 1], eps[:, s, :], ALU.add).then_inc(d_var[s], 1)
            pool.wait_ge(d_var[s], g + 1)
            nc.gpsimd.tensor_tensor(rstd[:, s, :], veps[:, s, :], half[:, :], ALU.pow).then_inc(d_rstd[s], 1)

        def mlp(name, g, k, par, pair):
            if name == "stats":
                inverse_deviation(0, g)

        def split(to, source, high, done):
            count = source.shape[-1]
            nc.gpsimd.tensor_tensor(to[:, 0, :], source, zeros[:, 0:count], ALU.add).then_inc(high[0], 1)
            pool.wait_ge(*high)
            nc.gpsimd.tensor_tensor(to[:, 1, :], source, to[:, 0, :], ALU.subtract).then_inc(done, 1)

        def router(name, g, k, par, pair):
            if name == "stats":
                inverse_deviation(1, g)
            elif name == "nx_read":
                pool.wait_ge(nx_read, g + 1)
                if not isinstance(g, int) or g > 1:
                    pool.wait_ge(hidden_done, NHC * (g - 1))
                split(NXS[par], NX[par][:, :], (nx_high, g + 1), nx_split)
            elif name == "evidence":
                pool.wait_ge(evidence_read, g + 1)
                if not isinstance(g, int) or g > 1:
                    pool.wait_ge(hidden_done, NHC * (g - 1))
                split(EVS[par], EV[par][:, :], (ev_high, g + 1), ev_split)

        def split_weights():
            pool.wait_ge(attended, NG)
            pool.wait_ge(derived_act, 1)
            count = 0
            for lo in range(0, NHC * P, GT):
                for to, source in ((WNS, w("e_nx", lo, min(GT, NHC * P - lo))), (US, U[:, lo:min(lo + GT, NHC * P)])):
                    count += 1
                    split(to[:, :, lo:min(lo + GT, NHC * P)], source, (weights_high, count), weights_split)

        return {"start": lambda: start_mlp(mlp), "between": lambda: between_cores(mlp),
                "behind": lambda: behind_cores(mlp)}, \
            lambda: rest_of_groups(pool, mlp, router, nothing, split_weights)

    def scalar_programs(act):
        def derive():
            act.wait_ge(derived_pe, 2)
            for c in range(NHC):
                bias = vec("be1", c) if c < EH else vec("bg1")
                nc.scalar.activation(ANC[:, c, :], PS[4][:, 2 * P + c * B:2 * P + (c + 1) * B], ACT.Identity, bias=bias)
            nc.scalar.activation(WO[:, GT:EH * P], PS[4][:, 0:EH * P - GT], ACT.Copy)
            nc.scalar.activation(U[:, 0:GT], PS[1][:, :], ACT.Copy)
            nc.scalar.activation(U[:, GT:NHC * P], PS[2][:, 0:NHC * P - GT], ACT.Copy).then_inc(derived_act, 1)

        def gelu(g, k):
            act.wait_ge(first_done, 4 * g + (k + 1))
            if later(g):
                act.wait_ge(second_done, 4 * g + (k - 3))
            nc.scalar.activation(H[:, k, :], FIRST_BANK[k % 2][:, :], ACT.Gelu_apprx_tanh, bias=vec("bmlp1", k))\
                .then_inc(gelu_done, 1)

        def mlp(name, g, k, par, pair):
            if name == "first" and k < 2 or name == "gelu":
                gelu(g, k)
            elif name == "xt_read":
                act.wait_ge(xt_turned, g + 1)
                if later(g):
                    act.wait_ge(first_done, 4 * g)
                for b in range(GB):
                    nb = bass.ds(g * GB + b, 1)
                    last = nc.scalar.activation(XT[:, b * P:(b + 1) * P], XT_BANK[:, b * P:(b + 1) * P],
                                                ACT.Identity, scale=mod[:, 4, nb], bias=mod[:, 3, nb])
                last.then_inc(xt_read, 1)

        def router(name, g, k, par, pair):
            if name == "hidden":
                act.wait_ge(hidden_done, NHC * g + (k + 1))
                for b in range(GB):
                    last = nc.scalar.activation(HID[:, k, b * P:(b + 1) * P], HIDDEN_BANK[k % 2][:, b * P:(b + 1) * P],
                                                ACT.Silu, bias=ANC[:, k, bass.ds(g * GB + b, 1)])
                last.then_inc(silu_done, 1)
            elif name == "ctx_turn":
                act.wait_ge(ctx_turned, g + 1)
                nc.scalar.activation(CTXT[:, :], EVIDENCE_BANK[:, :], ACT.Copy).then_inc(ctx_read, 1)
            elif name == "exp":
                act.wait_ge(nbias_done, g + 1)
                if later(g):
                    act.wait_ge(weights_done, g)
                for b in range(GB):
                    last = nc.scalar.activation(E[:, b, :], score_view(b // 2)[:, b % 2, :], ACT.Exp,
                                                scale=SCALE1, bias=nbias[:, b:b + 1], accum_out=esum[:, b:b + 1])
                last.then_inc(exps_done, 1)
            elif name == "exp_logits":
                act.wait_ge(lshift_done, g + 1)
                if later(g):
                    act.wait_ge(probs_done, g)
                nc.scalar.activation(LE[:, :, :], LS[:, :, :], ACT.Exp).then_inc(lexp_done, 1)
                nc.scalar.activation(warm[:, :], half[:, 0:1], ACT.Silu)
            elif name == "w_turn":
                act.wait_ge(w_turned, g + 1)
                nc.scalar.activation(WT[:, :], EVIDENCE_BANK[:, :], ACT.Copy).then_inc(w_read, 1)
            elif name == "gate":
                act.wait_ge(gate_read, g + 1)
                if later(g):
                    act.wait_ge(delta_done, g)
                nc.scalar.activation(GTH[:, :], GS[:, :], ACT.Tanh, scale=0.5).then_inc(gate_tanh, 1)

        return {"derive": derive, "between": lambda: between_cores(mlp), "behind": lambda: behind_cores(mlp)}, \
            lambda: rest_of_groups(act, mlp, router, nothing)

    def vector_programs(dve):
        def derive():
            dve.wait_ge(derived_pe, 1)
            nc.vector.tensor_copy(A[:, :], PS[0][:, 0:P])
            nc.vector.tensor_copy(REV[:, :], PS[0][:, P:P + NE])
            nc.vector.tensor_copy(LOG32[:, :], PS[0][0:B, 2 * P:2 * P + NE]).then_inc(derived_dve, 1)
            dve.wait_ge(derived_dve, 1)
            nc.vector.tensor_tensor(MASKED[:, :, :], ident[0:B, 0:B].unsqueeze(2).to_broadcast([B, B, NE]),
                                    LOG32[:, :].unsqueeze(1).to_broadcast([B, B, NE]), ALU.mult)\
                .then_inc(derived_dve, 1)
            dve.wait_ge(derived_pe, 2)
            nc.vector.tensor_copy(WO[:, 0:GT], PS[3][:, :])
            nc.vector.tensor_copy(BO[:, :], PS[5][:, :])
            dve.wait_ge(derived_pe, 3)
            nc.vector.tensor_copy(RA[:, :, :], PS[0][:, 3 * P:3 * P + NE * B].rearrange("p (b e) -> p b e", e=NE))\
                .then_inc(derived_dve, 1)

        def statistics(s, g):
            if isinstance(g, int):
                dve.wait_ge((attended, x_added)[s], g + 1)
            for b in range(GB):
                last = nc.vector.bn_stats(stat[:, s, b, :], x_batch(g, b))
            last.then_inc(d_stat[s], 1)
            dve.wait_ge(d_stat[s], g + 1)
            nc.vector.tensor_copy(seen[:, :], stat[:, s, GB - 1, 0:1])
            for b in range(GB):
                last = nc.vector.bn_aggr(mv[:, s, b, :], stat[:, s, b, :])
            last.then_inc(d_mv[s], 1)

        def normalise(s, g, to, turned):
            dve.wait_ge(d_rstd[s], g + 1)
            if later(g):
                dve.wait_ge(turned, g)
            for b in range(GB):
                last = nc.vector.tensor_scalar(to[:, b * P:(b + 1) * P], x_batch(g, b), mv[:, s, b, 0:1],
                                               rstd[:, s, b:b + 1], ALU.subtract, ALU.mult)
            last.then_inc(d_norm[s], 1)

        def mlp(name, g, k, par, pair):
            if name == "stats":
                statistics(0, g)
            elif name == "norm":
                normalise(0, g, XN, xt_turned)
            elif name == "gate":
                dve.wait_ge(second_done, 4 * g + 4)
                if later(g):
                    dve.wait_ge(turned_back, g)
                for b in range(GB):
                    nb = bass.ds(g * GB + b, 1)
                    last = nc.vector.tensor_scalar(YT[:, b * P:(b + 1) * P], SECOND_BANK[:, b * P:(b + 1) * P],
                                                   mod[:, 5, nb], gbm[:, nb], ALU.mult, ALU.add)
                last.then_inc(gated, 1)
            elif name == "turn_back":
                x = X[:, bass.ds(g * GT, GT)]
                dve.wait_ge(turned_back, g + 1)
                nc.vector.tensor_tensor(x, BACK_BANK[:, :], x, ALU.add).then_inc(x_added, 1)

        def router(name, g, k, par, pair):
            if name == "stats":
                statistics(1, g)
            elif name == "norm":
                normalise(1, g, RXN, nx_turned)
            elif name == "keys":
                dve.wait_ge(keys_done, g + 1)
                nc.vector.tensor_copy(KEYS[:, :], EVIDENCE_BANK[:, :]).then_inc(keys_read, 1)
            elif name == "nx_read":
                dve.wait_ge(nx_turned, g + 1)
                nc.vector.tensor_scalar(NX[par][:, :], EVIDENCE_BANK[:, :], vec("gamma"), vec("beta"), ALU.mult,
                                        ALU.add).then_inc(nx_read, 1)
            elif name == "scores":
                dve.wait_ge(scores_done, g + 1)
                for h in range(2):
                    last = nc.vector.tensor_reduce(out=nmax[:, 2 * h:2 * h + 2], in_=score_view(h),
                                                   axis=AX.X, op=ALU.max, negate=True)
                last.then_inc(nmax_done, 1)
                dve.wait_ge(nmax_done, g + 1)
                nc.vector.tensor_scalar(nbias[:, :], nmax[:, :], SCALE1, None, ALU.mult).then_inc(nbias_done, 1)
            elif name == "probs":
                dve.wait_ge(lexp_done, g + 1)
                nc.vector.tensor_reduce(out=lsum[:, :], in_=LE[:, :, :], axis=AX.X, op=ALU.add)\
                    .then_inc(lsum_done, 1)
                dve.wait_ge(lsum_done, g + 1)
                nc.vector.reciprocal(lrec[:, :], lsum[:, :]).then_inc(lrec_done, 1)
                dve.wait_ge(lrec_done, g + 1)
                nc.vector.scalar_tensor_tensor(RP[:, :, :], LE[:, :, :], 0.5,
                                               lrec[:, :].unsqueeze(2).to_broadcast([P, GB, NE]), ALU.mult,
                                               ALU.mult).then_inc(probs_done, 1)
                dve.wait_ge(probs_done, g + 1)
            elif name == "weigh":
                dve.wait_ge(exps_done, g + 1)
                nc.vector.reciprocal(rsum[:, :], esum[:, :]).then_inc(rsum_done, 1)
                dve.wait_ge(rsum_done, g + 1)
                nc.vector.tensor_tensor(WN[:, :, :], E[:, :, :], rsum[:, :].unsqueeze(2).to_broadcast([P, GB, P]),
                                        ALU.mult).then_inc(weights_done, 1)
            elif name == "evidence":
                dve.wait_ge(evidence_done, g + 1)
                nc.vector.tensor_copy(EV[par][:, :], EVIDENCE_BANK[:, :]).then_inc(evidence_read, 1)
            elif name == "logits":
                dve.wait_ge(logits_done, g + 1)
                for h in range(2):
                    last = nc.vector.tensor_tensor(LG[:, 2 * h:2 * h + 2, :], logit_view(h),
                                                   RA[:, bass.ds(g * GB + 2 * h, 2), :], ALU.add)
                last.then_inc(logits_read, 1)
                dve.wait_ge(logits_read, g + 1)
                nc.vector.tensor_reduce(out=lmax[:, :], in_=LG[:, :, :], axis=AX.X, op=ALU.max)\
                    .then_inc(lmax_done, 1)
                dve.wait_ge(lmax_done, g + 1)
                nc.vector.tensor_tensor(LS[:, :, :], LG[:, :, :], lmax[:, :].unsqueeze(2).to_broadcast([P, GB, NE]),
                                        ALU.subtract).then_inc(lshift_done, 1)
            elif name == "gate":
                dve.wait_ge(gate_done, g + 1)
                if later(g):
                    dve.wait_ge(gate_tanh, g)
                gate_bias = BO[:, NE * P:GT].unsqueeze(1).to_broadcast([P, GB, P])
                nc.vector.tensor_tensor(GS[:, :].rearrange("p (b c) -> p b c", b=GB),
                                        GATE_BANK[:, :].rearrange("p (b c) -> p b c", b=GB), gate_bias, ALU.add)\
                    .then_inc(gate_read, 1)
            elif name == "expert":
                b, t = k, T[:, k % 2, :]
                dve.wait_ge(expert_done, GB * g + (b + 1))
                nc.vector.tensor_tensor(t, EXPERT_BANK[b % 2][:, 0:NE * P], BO[:, 0:NE * P], ALU.add)\
                    .then_inc(expert_read, 1)
                dve.wait_ge(expert_read, GB * g + (b + 1))
                nc.vector.tensor_scalar(R[:, b, :], t[:, 0:P], RP[:, b, 0:1], None, ALU.mult).then_inc(routed, 1)
                for e in range(1, NE):
                    dve.wait_ge(routed, NE * GB * g + (NE * b + e))
                    nc.vector.scalar_tensor_tensor(R[:, b, :], t[:, e * P:(e + 1) * P], RP[:, b, e:e + 1], R[:, b, :],
                                                   ALU.mult, ALU.add).then_inc(routed, 1)
            elif name == "finish":
                x = X[:, bass.ds(g * GT, GT)]
                dve.wait_ge(routed, NE * GB * g + NE * GB)
                dve.wait_ge(gate_tanh, g + 1)
                nc.vector.scalar_tensor_tensor(D[:, :], GTH[:, :], 1.0, R[:, :, :].rearrange("p b c -> p (b c)"),
                                               ALU.add, ALU.mult).then_inc(delta_done, 1)
                dve.wait_ge(delta_done, g + 1)
                nc.vector.tensor_tensor(x, D[:, :], x, ALU.add).then_inc(finished, 1)

        def rest():
            dve.wait_ge(attended, NG)
            rest_of_groups(dve, mlp, router, lambda: dve.wait_ge(x_added, NG))

        return {"derive": derive, "start": lambda: start_mlp(mlp), "between": lambda: between_cores(mlp),
                "behind": lambda: behind_cores(mlp)}, rest

    def tensor_programs(pe):
        def product(to, lhsT, rhs, start=True, stop=True):
            return nc.tensor.matmul(to, lhsT, rhs, start=start, stop=stop)

        def derive():
            pe.wait_ge(load_w2, 32)
            pe.wait_ge(fills, 1)
            product(PS[0][:, 0:P], w("wkT"), w("wqT"))
            product(PS[0][:, P:P + NE], w("wvT"), w("r_ev"))
            product(PS[0][0:B, 2 * P:2 * P + NE], condT[:, :], w("r_an"), stop=False)
            product(PS[0][0:B, 2 * P:2 * P + NE], ones[0:1, 0:B], rows1[0:1, 2 * P:2 * P + NE], start=False)\
                .then_inc(derived_pe, 1)
            product(PS[1][:, :], w("wvT"), w("e_ev", 0, GT))
            product(PS[2][:, 0:EH * P - GT], w("wvT"), w("e_ev", GT, EH * P - GT))
            product(PS[2][:, EH * P - GT:NHC * P - GT], w("wvT"), w("g_ev"))
            for c in range(NHC):
                product(PS[4][:, 2 * P + c * B:2 * P + (c + 1) * B], w("e_an", c * P, P) if c < EH else w("g_an"), condT[:, :])
            for c in range(EH):
                product(PS[3 + c // 4][:, (c % 4) * P:(c % 4 + 1) * P], w("e2T", c * P, P), w("outw"))
            for e in range(NE):
                product(PS[5][:, e * P:(e + 1) * P], vec("be2", e).to_broadcast([P, P]), w("outw"), stop=False)
                product(PS[5][:, e * P:(e + 1) * P], ones[0:1, :], rows1[0:1, 0:P], start=False)
            product(PS[5][:, NE * P:GT], ones[0:1, :], rows1[0:1, P:2 * P]).then_inc(derived_pe, 1)
            pe.wait_ge(derived_dve, 2)
            product(PS[0][:, 3 * P:3 * P + NE * B], ones[:, :], MASKED[:, :, :].rearrange("p b e -> p (b e)"))\
                .then_inc(derived_pe, 1)
            pe.wait_ge(derived_act, 1)
            pe.wait_ge(derived_dve, 3)

        def turn(bank, source):
            for b in range(GB):
                last = nc.tensor.transpose(bank[:, b * P:(b + 1) * P], source(b), ident[:, :])
            return last

        def mlp(name, g, k, par, pair):
            if name == "xt":
                pe.wait_ge(d_norm[0], g + 1)
                if later(g):
                    pe.wait_ge(xt_read, g)
                turn(XT_BANK, lambda b: XN[:, b * P:(b + 1) * P]).then_inc(xt_turned, 1)
            elif name == "first":
                if k == 0:
                    pe.wait_ge(xt_read, g + 1)
                if k > 1 or later(g):
                    pe.wait_ge(gelu_done, 4 * g + (k - 1))
                product(FIRST_BANK[k % 2][:, :], w("mlp1", k * P, P), XT[:, :]).then_inc(first_done, 1)
            elif name == "second":
                if k == 0 and later(g):
                    pe.wait_ge(gated, g)
                pe.wait_ge(gelu_done, 4 * g + (k + 1))
                product(SECOND_BANK[:, :], w("mlp2", k * P, P), H[:, k, :], start=k == 0, stop=k == 3)\
                    .then_inc(second_done, 1)
            elif name == "turn_back":
                pe.wait_ge(gated, g + 1)
                if later(g):
                    pe.wait_ge(x_added, g)
                turn(BACK_BANK, lambda b: YT[:, b * P:(b + 1) * P]).then_inc(turned_back, 1)

        def router(name, g, k, par, pair):
            if name == "ctx_turn":
                pe.wait_ge(ctx_in[par], 16 * (pair + 1))
                if later(g):
                    pe.wait_ge(nx_read, g)
                turn(EVIDENCE_BANK, lambda b: CTX[par][:, b, :]).then_inc(ctx_turned, 1)
            elif name == "keys":
                pe.wait_ge(ctx_read, g + 1)
                product(EVIDENCE_BANK[:, :], A[:, :], CTXT[:, :]).then_inc(keys_done, 1)
            elif name == "nx_turn":
                pe.wait_ge(d_norm[1], g + 1)
                pe.wait_ge(keys_read, g + 1)
                if later(g):
                    pe.wait_ge(evidence_read, g)
                turn(EVIDENCE_BANK, lambda b: RXN[:, b * P:(b + 1) * P]).then_inc(nx_turned, 1)
            elif name == "scores":
                pe.wait_ge(nx_read, g + 1)
                if later(g):
                    pe.wait_ge(logits_read, g)
                for b in range(GB):
                    last = product(score_view(b // 2)[:, b % 2, :], NX[par][:, b * P:(b + 1) * P],
                                   KEYS[:, b * P:(b + 1) * P])
                last.then_inc(scores_done, 1)
            elif name == "w_turn":
                pe.wait_ge(weights_done, g + 1)
                if not isinstance(g, int) or g + 1 < NG:
                    pe.wait_ge(keys_read, g + 2)
                else:
                    pe.wait_ge(nx_read, NG)
                turn(EVIDENCE_BANK, lambda b: WN[:, b, :]).then_inc(w_turned, 1)
            elif name == "evidence":
                pe.wait_ge(w_read, g + 1)
                for b in range(GB):
                    last = product(EVIDENCE_BANK[:, b * P:(b + 1) * P], CTX[par][:, b, :], WT[:, b * P:(b + 1) * P])
                last.then_inc(evidence_done, 1)
            elif name == "logits":
                pe.wait_ge(evidence_read, g + 1)
                for b in range(GB):
                    to, batch = logit_view(b // 2)[:, b % 2, :], slice(b * P, (b + 1) * P)
                    product(to, NX[par][:, batch], w("r_nx"), stop=False)
                    last = product(to, EV[par][:, batch], REV[:, :], start=False)
                last.then_inc(logits_done, 1)
            elif name == "hidden":
                if k == 0:
                    pe.wait_ge(nx_split, g + 1)
                    pe.wait_ge(ev_split, g + 1)
                if k > 1:
                    pe.wait_ge(silu_done, NHC * g + (k - 1))
                elif later(g):
                    pe.wait_ge(silu_done, NHC * g)
                chunk = slice(k * P, (k + 1) * P)
                for weights, data in ((WNS, NXS[par]), (US, EVS[par])):
                    product(HIDDEN_BANK[k % 2][:, :], weights[:, 0, chunk], data[:, 0, :], weights is WNS, False)
                    product(HIDDEN_BANK[k % 2][:, :], weights[:, 0, chunk], data[:, 1, :], False, False)
                    last = product(HIDDEN_BANK[k % 2][:, :], weights[:, 1, chunk], data[:, 0, :], False,
                                   weights is US)
                last.then_inc(hidden_done, 1)
            elif name == "expert":
                b = k
                if b == 0:
                    pe.wait_ge(silu_done, NHC * g + EH)
                if b > 1 or later(g):
                    pe.wait_ge(expert_read, GB * g + (b - 1))
                for e in range(NE):
                    for c in range(2):
                        last = product(EXPERT_BANK[b % 2][:, e * P:(e + 1) * P],
                                       HID[:, 2 * e + c, b * P:(b + 1) * P],
                                       WO[:, (2 * e + c) * P:(2 * e + c + 1) * P], start=c == 0, stop=c == 1)
                last.then_inc(expert_done, 1)
            elif name == "gate":
                pe.wait_ge(silu_done, NHC * g + NHC)
                if later(g):
                    pe.wait_ge(gate_read, g)
                for b in range(GB):
                    last = product(GATE_BANK[:, b * P:(b + 1) * P], HID[:, EH, b * P:(b + 1) * P], w("gate2"))
                last.then_inc(gate_done, 1)

        def between():
            pe.wait_ge(max_done, 4 * (NCORE - GB))
            pe.wait_ge(exp_done, 4 * (NCORE - GB))
            pe.wait_ge(o_normed, NCORE - GB)
            between_cores(mlp)
            pe.wait_ge(xt_read, 3)
            pe.wait_ge(gelu_done, 4 * 2)
            pe.wait_ge(gated, 1)

        def behind():
            pe.wait_ge(max_done, 4 * NCORE)
            pe.wait_ge(exp_done, 4 * NCORE)
            pe.wait_ge(o_normed, NCORE)
            behind_cores(mlp)

        def before_router():
            pe.wait_ge(weights_split, 2 * -(-NHC * P // GT))
            pe.wait_ge(xt_read, NG)
            pe.wait_ge(gelu_done, 4 * NG)
            pe.wait_ge(x_added, NG)

        def rest():
            pe.wait_ge(attended, NG)
            pe.wait_ge(o_stored, NCORE)
            rest_of_groups(pe, mlp, router, before_router)

        return {"derive": derive, "between": between, "behind": behind}, rest

    return sync_programs, gpsimd_programs, scalar_programs, vector_programs, tensor_programs


def build_block(nc, xin, cond, ctxin, weights, vectors, ident_in, rowb, out):
    stack = ExitStack()
    with stack:
        def sb(name, shape, dt=F32):
            return stack.enter_context(nc.sbuf_tensor(name, shape, dt))

        def sem(name):
            return stack.enter_context(nc.semaphore(name))

        X = sb("X", [P, B * P])
        W = sb("W", [P, W_TOTAL])
        V = sb("V", [P, V_TOTAL])
        ident = sb("ident", [P, P])
        identb = sb("identb", [P, P], BF16)

        def w(name, lo=0, n=None):
            at, size = W_COLS[name]
            return W[:, at + lo:at + lo + (size if n is None else n)]

        def vec(name, k=0):
            return V[:, V_COLS[name][0] + k:V_COLS[name][0] + k + 1]

        condr = sb("condr", [B, P])
        rows1 = sb("rows1", [1, 2 * P + 3])
        condT = sb("condT", [P, B])
        condS = sb("condS", [P, B])
        mod = sb("mod", [P, 6, B])
        gba = sb("gba", [P, B])
        gbm = sb("gbm", [P, B])
        bpr = sb("bpr", [P, 2])
        half = sb("half", [P, GB])
        eps = sb("eps", [P, GB])
        seen = sb("seen", [P, 1])
        zeros = sb("zeros", [P, GT])
        PS = [stack.enter_context(nc.psum_tensor(f"PS{k}", [P, 512], F32)) for k in range(8)]
        S_BANK, T_BANK, O_BANK, GROUP_BANK, SMALL_BANK = PS[0:2], PS[2:4], PS[4:6], PS[6], PS[7]

        load_small = sem("load_small")
        load_w = sem("load_w")
        load_w2 = sem("load_w2")
        load_x = [sem("load_x_first"), sem("load_x_second"), sem("load_x_others")]
        consts = sem("consts")
        stack_init = sem("stack_init")
        setup_pe = sem("setup_pe")
        setup_act = sem("setup_act")
        setup_dve = sem("setup_dve")

        kinds = ("s", "x", "c")
        ln_stat = [sem(f"ln_stat_{k}") for k in kinds]
        ln_mv = [sem(f"ln_mv_{k}") for k in kinds]
        ln_var = [sem(f"ln_var_{k}") for k in kinds]
        ln_rstd = [sem(f"ln_rstd_{k}") for k in kinds]
        ln_centred = [sem(f"ln_centred_{k}") for k in kinds]
        ln_done = [sem(f"ln_done_{k}") for k in kinds]
        bank_filled = {e: sem(f"filled_{e}") for e in BANK_ORDER}
        bank_read = {e: sem(f"read_{e}") for e in BANK_ORDER}
        high_ready = {e: sem(f"high_{e}") for e in ("q_s", "k_s", "q_c", "k_c")}
        middle_ready = {e: sem(f"middle_{e}") for e in ("q_s", "k_s", "q_c", "k_c")}
        low_ready = {e: sem(f"low_{e}") for e in ("q_s", "k_s", "q_c", "k_c")}
        stacked = [[sem(f"stacked_{k}_{h}") for h in range(2)] for k in ("self", "cross")]
        ctx_loaded = sem("ctx_loaded")
        score_done = sem("score_done")
        max_done = sem("max_done")
        max_high = sem("max_high")
        max_parts = sem("max_parts")
        max_turned = sem("max_turned")
        max_copied = sem("max_copied")
        max_rows = [sem(f"max_rows{k}") for k in range(2)]
        shifted_done = sem("shifted_done")
        exp_done = sem("exp_done")
        value_done = sem("value_done")
        o_copied = sem("o_copied")
        o_turned = sem("o_turned")
        den_done = sem("den_done")
        o_normed = sem("o_normed")
        o_backed = sem("o_backed")
        o_stored = sem("o_stored")

        sync_programs, gpsimd_programs, scalar_programs, vector_programs, tensor_programs = mlp_and_router(
            nc, stack, X, ctxin, w, vec, rows1, condT, mod, gbm, half, zeros, ident, PS, load_w2, out,
            bank_read["yt_c"], max_done, exp_done, o_normed, o_stored)

        XN = [sb(f"XN{k}", [P, GT]) for k in range(3)]
        XT = [sb(f"XT{k}", [P, GT]) for k in range(3)]
        CTXG = sb("CTXG", [P, GB, P])
        stat = sb("stat", [P, 3, GB, 6])
        mv = sb("mv", [P, 3, GB, 2])
        veps = sb("veps", [P, 3, GB])
        rstd = sb("rstd", [P, 3, GB])
        Qp = [sb(f"Qp{k}", [P, 3, GT], BF16) for k in range(2)]
        Kp = [sb(f"Kp{k}", [P, 3, GT], BF16) for k in range(2)]
        rest = sb("rest", [P, 2, GT])
        Qs = [sb(f"Qs{k}", [P, NJ, GT], BF16) for k in range(2)]
        Ks = [sb(f"Ks{k}", [P, NJ, GT], BF16) for k in range(2)]
        zrow = sb("zrow", [32, GT], BF16)
        orow = sb("orow", [32, GT], BF16)
        Va = [sb(f"Va{k}", [P, GB, NH, VW]) for k in range(2)]
        NM = sb("NM", [P, 2, NH])
        M2 = sb("M2", [P, 2, 2, 2, NJ], BF16)
        MT = sb("MT", [32, 2, P], BF16)
        PR = sb("PR", [P, 4, 4 * P])
        OTs = sb("OTs", [P, 4 * P])
        rden = sb("rden", [P, NH])
        On = sb("On", [P, 2, P])
        OgT = [sb(f"OgT{k}", [P, GT]) for k in range(2)]
        YT = [sb(f"YT{k}", [P, GT]) for k in range(2)]

        LN_KIND = {"ln_s": 0, "ln_x": 1, "ln_c": 2, "xt_s": 0, "xt_x": 1, "xt_c": 2}
        WEIGHT = {"q_s": "q", "k_s": "k", "q_c": "qc", "k_c": "kc", "v_s": "v", "v_c": "vc", "proj_s": "proj",
                  "proj_c": "cproj"}
        SOURCE = {"q_s": 0, "k_s": 0, "v_s": 0, "q_c": 1, "k_c": 2, "v_c": 2}
        BIAS = {"q_s": "bq", "k_s": "bk", "q_c": "bqc", "k_c": "bkc"}
        PARTS = {"q_s": Qp[0], "k_s": Kp[0], "q_c": Qp[1], "k_c": Kp[1]}
        REST = {"q_s": 0, "k_s": 1, "q_c": 0, "k_c": 1}
        KIND = {"q_s": 0, "k_s": 0, "q_c": 1, "k_c": 1, "v_s": 0, "v_c": 1, "proj_s": 0, "proj_c": 1, "yt_s": 0,
                "yt_c": 1}

        def attention_loop(eng, body, extra):
            def iteration(i):
                for ev in attention_events(i):
                    if ev[0] in ("derive", "start", "between", "behind"):
                        extra.get(ev[0], lambda: None)()
                    else:
                        body(ev)

            for i in range(-1, 3):
                iteration(i)
            with eng.Fori(3, 7) as i:
                for ev in attention_events(i, steady=True):
                    body(ev)
            for i in range(7, 10):
                iteration(i)

        block = stack.enter_context(nc.Block())

        @block.sync
        def _(sp):
            extra, remainder = sync_programs(sp)
            sp.dma_start(ident[:, :], ident_in).then_inc(load_small, 16)
            sp.dma_start(condr[:, :], cond).then_inc(load_small, 16)
            sp.dma_start(V[:, :], vectors).then_inc(load_small, 16)
            sp.dma_start(rows1[:, :], rowb).then_inc(load_w2, 16)
            sp.dma_start(W[:, 0:W_COLS["mlp1"][0]], weights[:, 0:W_COLS["mlp1"][0]]).then_inc(load_w, 16)

            def load_group(g):
                sp.dma_start(X[:, g * GT:(g + 1) * GT].rearrange("p (b h) -> p b h", b=GB),
                             xin[g * GB:(g + 1) * GB].rearrange("b p h -> p b h")).then_inc(load_x[min(g, 2)], 16)

            load_group(0)
            sp.dma_start(W[:, W_COLS["mlp1"][0]:], weights[:, W_COLS["mlp1"][0]:]).then_inc(load_w2, 16)
            load_group(1)
            sp.wait_ge(stack_init, 1)
            for k in range(2):
                sp.dma_start(Ks[k][MAX_ROW::32, :, :], orow[:, :]).then_inc(consts, 16)

            def body(ev):
                name = ev[0]
                if name == "load_rest":
                    for g in range(2, NG):
                        load_group(g)
                elif name == "stack":
                    _, kind, g, last, what, r, h = ev
                    half_group = slice(2 * h * P, 2 * (h + 1) * P)
                    if what == "zero":
                        if last is not None:
                            sp.wait_ge(shifted_done, 4 * last.n + 4)
                        to, source = Qs[kind][MAX_ROW::32, :, half_group], zrow[:, half_group]
                    else:
                        name, parts, of, to = \
                            (("k_s", "k_c")[kind], Kp[kind], K_PART, Ks[kind]) if what == "K" else \
                            (("q_s", "q_c")[kind], Qp[kind], Q_PART, Qs[kind])
                        sp.wait_ge((high_ready, middle_ready, low_ready)[of[r]][name], g + 1)
                        to, source = to[r::8, :, half_group], parts[:, of[r], half_group]
                    sp.dma_start(to, source).then_inc(stacked[kind][h], 16)
                elif name == "max_turn":
                    c = ev[1]
                    sp.wait_ge(max_copied, c.n + 1)
                    sp.dma_start(Qs[c.kind][MAX_ROW::32, :, c.b * P:(c.b + 1) * P],
                                 MT[:, c.mod % 2, :]).then_inc(max_rows[c.mod % 2], 16)
                elif name == "load":
                    g = ev[2]
                    if not isinstance(g, int) or g > 0:
                        sp.wait_ge(ln_done[2], g)
                    sp.dma_start(CTXG[:, :, :], ctxin[bass.ds(g * GB, GB)].rearrange("b p h -> p b h"))\
                        .then_inc(ctx_loaded, 16)

            attention_loop(sp, body, extra)
            remainder()

        @block.gpsimd
        def _(pool):
            extra, remainder = gpsimd_programs(pool)
            nc.gpsimd.memset(zrow[:, :], 0.0)
            nc.gpsimd.memset(orow[:, :], 1.0)
            nc.gpsimd.memset(half[:, :], -0.5)
            nc.gpsimd.memset(eps[:, :], 1e-6)
            nc.gpsimd.memset(zeros[:, :], 0.0)
            for k in range(2):
                nc.gpsimd.memset(Qs[k][:, :, :].bitcast(F32), 0.0)
                last = nc.gpsimd.memset(Ks[k][:, :, :].bitcast(F32), 0.0)
            last.then_inc(stack_init, 1)
            pool.wait_ge(stack_init, 1)

            def body(ev):
                name = ev[0]
                if name == "stats" and ev[3] == 1:
                    g, k = ev[2], LN_KIND[ev[1]]
                    pool.wait_ge(ln_mv[k], g + 1)
                    nc.gpsimd.tensor_tensor(veps[:, k, :], mv[:, k, :, 1], eps[:, :], ALU.add)\
                        .then_inc(ln_var[k], 1)
                    pool.wait_ge(ln_var[k], g + 1)
                    nc.gpsimd.tensor_tensor(rstd[:, k, :], veps[:, k, :], half[:, :], ALU.pow)\
                        .then_inc(ln_rstd[k], 1)
                elif name == "norm" and ev[1] != "ln_x":
                    g, k = ev[2], LN_KIND[ev[1]]
                    x = CTXG[:, :, :] if k == 2 else X[:, bass.ds(g * GT, GT)].rearrange("p (b h) -> p b h", b=GB)
                    to = XN[k][:, :].rearrange("p (b h) -> p b h", b=GB)
                    pool.wait_ge(ln_rstd[k], g + 1)
                    if not isinstance(g, int) or g > 0:
                        pool.wait_ge(bank_filled[("xt_s", "xt_x", "xt_c")[k]], g)
                    nc.gpsimd.tensor_tensor(to, x, mv[:, k, :, 0:1].to_broadcast([P, GB, P]), ALU.subtract)\
                        .then_inc(ln_centred[k], 1)
                    pool.wait_ge(ln_centred[k], g + 1)
                    nc.gpsimd.tensor_tensor(to, to, rstd[:, k, :].unsqueeze(2).to_broadcast([P, GB, P]), ALU.mult)\
                        .then_inc(ln_done[k], 1)
                elif name == "read" and ev[1] in PARTS and ev[3] == 1:
                    name, g = ev[1:3]
                    parts, left = PARTS[name], rest[:, REST[name], :]
                    pool.wait_ge(bank_read[name], g + 1)
                    nc.gpsimd.tensor_tensor(parts[:, 1, :], left, zeros[:, :], ALU.add)\
                        .then_inc(middle_ready[name], 1)
                    pool.wait_ge(middle_ready[name], g + 1)
                    nc.gpsimd.tensor_tensor(parts[:, 2, :], left, parts[:, 1, :], ALU.subtract)\
                        .then_inc(low_ready[name], 1)

            attention_loop(pool, body, extra)
            remainder()

        @block.scalar
        def _(act):
            extra, remainder = scalar_programs(act)
            act.wait_ge(setup_pe, 1)
            nc.scalar.activation(condS[:, :], PS[0][:, 0:B], ACT.Silu).then_inc(setup_act, 1)
            act.wait_ge(setup_pe, 2)
            for k in range(6):
                nc.scalar.activation(mod[:, k, :], PS[1][:, k * B:(k + 1) * B], ACT.Identity,
                                     bias=vec("bmod", k))
            nc.scalar.activation(bpr[:, 0:1], PS[1][:, 6 * B:6 * B + 1], ACT.Identity, bias=vec("bproj"))
            nc.scalar.activation(bpr[:, 1:2], PS[1][:, 6 * B + 1:6 * B + 2], ACT.Identity,
                                 bias=vec("bcproj")).then_inc(setup_act, 1)
            act.wait_ge(setup_dve, 3)

            def body(ev):
                name = ev[0]
                if name == "shifted":
                    _, c, u = ev
                    act.wait_ge(shifted_done, 4 * c.n + (u + 1))
                    if not isinstance(c.n, int) or c.n > 0:
                        act.wait_ge(value_done, 4 * c.n + (u - 3))
                    nc.scalar.activation(PR[:, u, :], T_BANK[u % 2][:, :], ACT.Exp, scale=SCALE)\
                        .then_inc(exp_done, 1)
                elif name == "value" and ev[2] == 3:
                    c = ev[1]
                    act.wait_ge(value_done, 4 * c.n + 4)
                    if not isinstance(c.n, int) or c.n > 0:
                        act.wait_ge(o_turned, c.n)
                    nc.scalar.activation(OTs[:, :], O_BANK[c.mod % 2][:, :], ACT.Copy).then_inc(o_copied, 1)
                elif name == "max_turn":
                    c = ev[1]
                    act.wait_ge(max_turned, c.n + 1)
                    if not isinstance(c.n, int) or c.n > 1:
                        act.wait_ge(max_rows[c.mod % 2], 16 * c.pairs)
                    nc.scalar.activation(MT[:, c.mod % 2, :], SMALL_BANK[0:32, 0:P // 2].bitcast(BF16), ACT.Copy)\
                        .then_inc(max_copied, 1)
                elif name == "o_back":
                    c = ev[1]
                    act.wait_ge(o_backed, c.n + 1)
                    e = "proj_s" if c.kind == 0 else "proj_c"
                    if not isinstance(c.group, int) or c.group > 0:
                        act.wait_ge(bank_filled[e], c.group)
                    nc.scalar.activation(OgT[c.kind][:, c.b * P:(c.b + 1) * P], SMALL_BANK[:, 0:P], ACT.Copy)\
                        .then_inc(o_stored, 1)
                elif ev[:2] == ("read", "xt_s"):
                    _, name, g, part = ev
                    act.wait_ge(bank_filled[name], g + 1)
                    for b in range(2 * part, 2 * part + 2):
                        nb = bass.ds(g * GB + b, 1)
                        last = nc.scalar.activation(XT[0][:, b * P:(b + 1) * P], GROUP_BANK[:, b * P:(b + 1) * P],
                                                    ACT.Identity, scale=mod[:, 1, nb], bias=mod[:, 0, nb])
                    if part == 1:
                        last.then_inc(bank_read[name], 1)
                elif name == "read" and ev[1] in ("xt_x", "xt_c"):
                    name, g = ev[1:3]
                    act.wait_ge(bank_filled[name], g + 1)
                    nc.scalar.activation(XT[LN_KIND[name]][:, :], GROUP_BANK[:, :], ACT.Copy)\
                        .then_inc(bank_read[name], 1)
                elif name == "read" and ev[1] in PARTS and ev[3] == 0:
                    name, g = ev[1:3]
                    act.wait_ge(bank_filled[name], g + 1)
                    if not isinstance(g, int) or g > 0:
                        for h in range(2):
                            act.wait_ge(stacked[KIND[name]][h], HALF_DMAS * g)
                    nc.scalar.activation(PARTS[name][:, 0, :], GROUP_BANK[:, :], ACT.Identity,
                                         bias=vec(BIAS[name])).then_inc(high_ready[name], 1)
                elif name == "read" and ev[1] in ("v_s", "v_c"):
                    name, g = ev[1:3]
                    kind = KIND[name]
                    act.wait_ge(bank_filled[name], g + 1)
                    nc.scalar.activation(Va[kind][:, :, :, 0:HD].rearrange("p b h d -> p (b h) d"),
                                         GROUP_BANK[:, :].rearrange("p (n d) -> p n d", d=HD), ACT.Copy)\
                        .then_inc(bank_read[name], 1)
                elif ev[:2] == ("read", "proj_c"):
                    name, g = ev[1:3]
                    act.wait_ge(bank_filled[name], g + 1)
                    if not isinstance(g, int) or g > 0:
                        act.wait_ge(bank_filled["yt_c"], g)
                    nc.scalar.activation(YT[1][:, :], GROUP_BANK[:, :], ACT.Identity, bias=bpr[:, 1:2])\
                        .then_inc(bank_read[name], 1)

            attention_loop(act, body, extra)
            remainder()

        @block.vector
        def _(dve):
            extra, remainder = vector_programs(dve)
            for k in range(2):
                nc.vector.memset(Va[k][:, :, :, :], 0.0)
            dve.drain()
            for k in range(2):
                nc.vector.memset(Va[k][:, :, :, HD:HD + 1], 1.0)
            dve.wait_ge(load_small, 48)
            nc.vector.tensor_copy(identb[:, :], ident[:, :]).then_inc(setup_dve, 1)
            dve.wait_ge(setup_pe, 1)
            dve.wait_ge(setup_act, 2)
            nc.vector.tensor_copy(condT[:, :], PS[0][:, 0:B])
            nc.vector.tensor_scalar(mod[:, 1, :], mod[:, 1, :], 1.0, None, ALU.add)
            nc.vector.tensor_scalar(mod[:, 4, :], mod[:, 4, :], 1.0, None, ALU.add).then_inc(setup_dve, 1)
            nc.vector.tensor_scalar(gba[:, :], mod[:, 2, :], bpr[:, 0:1], None, ALU.mult)
            nc.vector.tensor_scalar(gbm[:, :], mod[:, 5, :], vec("bmlp2"), None, ALU.mult).then_inc(setup_dve, 1)
            dve.wait_ge(setup_dve, 3)

            def ln_source(k, g, b):
                return CTXG[:, b, :] if k == 2 else X[:, bass.ds(g * GT + b * P, P)]

            def body(ev):
                name = ev[0]
                if name == "score":
                    _, c, u = ev
                    r = c.mod % 2
                    dve.wait_ge(score_done, 4 * c.n + (u + 1))
                    nc.vector.tensor_reduce(out=NM[:, r, 4 * u:4 * u + 4],
                                            in_=S_BANK[u % 2][:, :].rearrange("p (h k) -> p h k", k=P),
                                            axis=AX.X, op=ALU.max, negate=True).then_inc(max_done, 1)
                elif name == "max_parts":
                    c = ev[1]
                    r = c.mod % 2
                    nm = NM[:, r, :].rearrange("p (e j) -> p e j", e=2)
                    dve.wait_ge(max_done, 4 * c.n + 4)
                    if not isinstance(c.n, int) or c.n > 1:
                        dve.wait_ge(max_turned, c.n - 1)
                    nc.vector.tensor_copy(M2[:, r, :, 0, :], nm).then_inc(max_high, 1)
                    dve.wait_ge(max_high, c.n + 1)
                    nc.vector.tensor_tensor(M2[:, r, :, 1, :], nm, M2[:, r, :, 0, :], ALU.subtract)\
                        .then_inc(max_parts, 1)
                elif name == "o_norm":
                    c = ev[1]
                    r = c.mod % 2
                    turned = O_BANK[c.mod % 2][:, :].rearrange("p (h d) -> p h d", d=VW)
                    dve.wait_ge(o_turned, c.n + 1)
                    nc.vector.reciprocal(rden[:, :].unsqueeze(2), turned[:, :, HD:HD + 1]).then_inc(den_done, 1)
                    dve.wait_ge(den_done, c.n + 1)
                    if not isinstance(c.n, int) or c.n > 1:
                        dve.wait_ge(o_backed, c.n - 1)
                    nc.vector.tensor_tensor(On[:, r, :].rearrange("p (h d) -> p h d", d=HD), turned[:, :, 0:HD],
                                            rden[:, :].unsqueeze(2).to_broadcast([P, NH, HD]), ALU.mult)\
                        .then_inc(o_normed, 1)
                elif name == "stats":
                    g, k, part = ev[2], LN_KIND[ev[1]], ev[3]
                    if k == 0 and part == 0:
                        dve.wait_ge(load_x[0], 16)
                        if not isinstance(g, int) or g > 0:
                            dve.wait_ge(load_x[1], 16)
                        if not isinstance(g, int) or g > 1:
                            dve.wait_ge(load_x[2], 16 * (NG - 2))
                    if k > 0 and part == 0:
                        if k == 1:
                            dve.wait_ge(bank_read["yt_s"], g + 1)
                        else:
                            dve.wait_ge(ctx_loaded, 16 * (g + 1))
                        nc.vector.tensor_copy(seen[:, :], half[:, 0:1])
                    for b in range(2 * part, 2 * part + 2):
                        last = nc.vector.bn_stats(stat[:, k, b, :], ln_source(k, g, b))
                    if part == 1:
                        last.then_inc(ln_stat[k], 1)
                        dve.wait_ge(ln_stat[k], g + 1)
                        nc.vector.tensor_copy(seen[:, :], stat[:, k, GB - 1, 0:1])
                        for b in range(GB):
                            last = nc.vector.bn_aggr(mv[:, k, b, :], stat[:, k, b, :])
                        last.then_inc(ln_mv[k], 1)
                elif ev[:2] == ("norm", "ln_x"):
                    g, k, b = ev[2], LN_KIND[ev[1]], ev[3]
                    if b == 0:
                        dve.wait_ge(ln_rstd[k], g + 1)
                        if not isinstance(g, int) or g > 0:
                            dve.wait_ge(bank_filled[("xt_s", "xt_x", "xt_c")[k]], g)
                    last = nc.vector.tensor_scalar(XN[k][:, b * P:(b + 1) * P], ln_source(k, g, b),
                                                   mv[:, k, b, 0:1], rstd[:, k, b:b + 1], ALU.subtract, ALU.mult)
                    if b == GB - 1:
                        last.then_inc(ln_done[k], 1)
                elif ev[:2] == ("read", "proj_s"):
                    _, name, g, part = ev
                    if part == 0:
                        dve.wait_ge(bank_filled[name], g + 1)
                        if not isinstance(g, int) or g > 0:
                            dve.wait_ge(bank_filled["yt_s"], g)
                    for b in range(2 * part, 2 * part + 2):
                        nb = bass.ds(g * GB + b, 1)
                        last = nc.vector.tensor_scalar(YT[0][:, b * P:(b + 1) * P],
                                                       GROUP_BANK[:, b * P:(b + 1) * P], mod[:, 2, nb],
                                                       gba[:, nb], ALU.mult, ALU.add)
                    if part == 1:
                        last.then_inc(bank_read[name], 1)
                elif name == "read" and ev[1] in PARTS and ev[3] == 1:
                    name, g = ev[1:3]
                    before = {"q_s": g - 1, "k_s": g - 1, "q_c": g + 2, "k_c": g + 2}[name]
                    other = {"q_s": "q_c", "k_s": "k_c", "q_c": "q_s", "k_c": "k_s"}[name]
                    if isinstance(before, int):
                        before = min(before, NG)
                    if not isinstance(before, int) or before > 0:
                        dve.wait_ge(low_ready[other], before)
                    dve.wait_ge(high_ready[name], g + 1)
                    nc.vector.scalar_tensor_tensor(rest[:, REST[name], :], GROUP_BANK[:, :], vec(BIAS[name]),
                                                   PARTS[name][:, 0, :], ALU.add, ALU.subtract)\
                        .then_inc(bank_read[name], 1)
                elif name == "read" and ev[1] in ("yt_s", "yt_c"):
                    name, g = ev[1:3]
                    x = X[:, bass.ds(g * GT, GT)]
                    dve.wait_ge(bank_filled[name], g + 1)
                    nc.vector.tensor_tensor(x, GROUP_BANK[:, :], x, ALU.add).then_inc(bank_read[name], 1)

            attention_loop(dve, body, extra)
            remainder()

        @block.tensor
        def _(pe):
            extra, remainder = tensor_programs(pe)
            pe.wait_ge(load_small, 48)
            pe.wait_ge(load_w, 16)
            nc.tensor.transpose(PS[0][:, 0:B], condr[:, :], ident[0:B, 0:B]).then_inc(setup_pe, 1)
            pe.wait_ge(setup_act, 1)
            for k in range(6):
                nc.tensor.matmul(PS[1][:, k * B:(k + 1) * B], w("mod", k * P, P), condS[:, :], start=True, stop=True)
            nc.tensor.matmul(PS[1][:, 6 * B:6 * B + 1], w("proj"), vec("bv"), start=True, stop=True)
            nc.tensor.matmul(PS[1][:, 6 * B + 1:6 * B + 2], w("cproj"), vec("bvc"), start=True, stop=True)\
                .then_inc(setup_pe, 1)
            pe.wait_ge(setup_dve, 3)

            def body(ev):
                name = ev[0]
                if name == "score":
                    _, c, u = ev
                    e, lo = u // 2, (u % 2) * 4
                    if u == 0 and isinstance(c.n, int) and c.n == 0:
                        pe.wait_ge(consts, 32)
                    if u == 0 and c.b % 2 == 0:
                        pe.wait_ge(stacked[c.kind][c.b // 2], HALF_DMAS * (c.group + 1))
                    if not isinstance(c.n, int) or 4 * c.n + u > 1:
                        pe.wait_ge(max_done, 4 * c.n + (u - 1))
                    for j in range(4):
                        rows, cols = slice(64 * e, 64 * e + 64), slice(c.b * P, (c.b + 1) * P)
                        last = nc.tensor.matmul(S_BANK[u % 2][:, j * P:(j + 1) * P], Qs[c.kind][rows, lo + j, cols],
                                                Ks[c.kind][rows, lo + j, cols], start=True, stop=True)
                    last.then_inc(score_done, 1)
                elif name == "shifted":
                    _, c, u = ev
                    e, lo = u // 2, (u % 2) * 4
                    if u == 0:
                        pe.wait_ge(max_rows[c.mod % 2], 16 * (c.pairs + 1))
                    if not isinstance(c.n, int) or 4 * c.n + u > 1:
                        pe.wait_ge(exp_done, 4 * c.n + (u - 1))
                    for j in range(4):
                        rows, cols = slice(64 * e, 64 * e + 64), slice(c.b * P, (c.b + 1) * P)
                        last = nc.tensor.matmul(T_BANK[u % 2][:, j * P:(j + 1) * P], Ks[c.kind][rows, lo + j, cols],
                                                Qs[c.kind][rows, lo + j, cols], start=True, stop=True)
                    last.then_inc(shifted_done, 1)
                elif name == "value":
                    _, c, u = ev
                    pe.wait_ge(exp_done, 4 * c.n + (u + 1))
                    if u == 0:
                        if not isinstance(c.n, int) or c.n > 1:
                            pe.wait_ge(o_normed, c.n - 1)
                        if c.b == 0:
                            pe.wait_ge(bank_read["v_s" if c.kind == 0 else "v_c"], c.group + 1)
                    for j in range(4):
                        last = nc.tensor.matmul(O_BANK[c.mod % 2][32 * j:32 * j + 32, u * P:(u + 1) * P],
                                                Va[c.kind][:, c.b, 4 * u + j, :], PR[:, u, j * P:(j + 1) * P],
                                                start=True, stop=True)
                    last.then_inc(value_done, 1)
                elif name == "max_turn":
                    _, c, stored = ev
                    pe.wait_ge(max_parts, c.n + 1)
                    if not isinstance(c.n, int) or stored > 0:
                        pe.wait_ge(o_stored, stored)
                    if isinstance(c.n, int) and c.n > 0:
                        pe.wait_ge(max_copied, c.n)
                    nc.tensor.transpose(SMALL_BANK[0:32, 0:P // 2].bitcast(BF16),
                                        M2[:, c.mod % 2, :, :, :].rearrange("p e t j -> p (e t j)"), identb[:, :])\
                        .then_inc(max_turned, 1)
                elif name == "o_turn":
                    c = ev[1]
                    pe.wait_ge(o_copied, c.n + 1)
                    for u in range(4):
                        last = nc.tensor.transpose(O_BANK[c.mod % 2][:, u * P:(u + 1) * P], OTs[:, u * P:(u + 1) * P],
                                                   ident[:, :])
                    last.then_inc(o_turned, 1)
                elif name == "o_back":
                    _, c, copied = ev
                    pe.wait_ge(o_normed, c.n + 1)
                    pe.wait_ge(max_copied, copied)
                    if isinstance(c.n, int) and c.n > 0:
                        pe.wait_ge(o_stored, c.n)
                    nc.tensor.transpose(SMALL_BANK[:, 0:P], On[:, c.mod % 2, :], ident[:, :]).then_inc(o_backed, 1)
                elif name == "fill":
                    _, name, g, before, last_core = ev
                    if before is not None:
                        pe.wait_ge(bank_read[before[0]], before[1] + 1)
                    if name in ("xt_s", "xt_x", "xt_c"):
                        k = LN_KIND[name]
                        pe.wait_ge(ln_done[k], g + 1)
                        for b in range(GB):
                            last = nc.tensor.transpose(GROUP_BANK[:, b * P:(b + 1) * P], XN[k][:, b * P:(b + 1) * P],
                                                       ident[:, :])
                    elif name in PARTS:
                        last = nc.tensor.matmul(GROUP_BANK[:, :], w(WEIGHT[name]), XT[SOURCE[name]][:, :],
                                                start=True, stop=True)
                    elif name in ("v_s", "v_c"):
                        for b in range(GB):
                            last = nc.tensor.matmul(GROUP_BANK[:, b * P:(b + 1) * P],
                                                    XT[SOURCE[name]][:, b * P:(b + 1) * P], w(WEIGHT[name]),
                                                    start=True, stop=True)
                    elif name in ("proj_s", "proj_c"):
                        pe.wait_ge(o_stored, last_core.n + 1)
                        last = nc.tensor.matmul(GROUP_BANK[:, :], w(WEIGHT[name]), OgT[KIND[name]][:, :],
                                                start=True, stop=True)
                    else:
                        for b in range(GB):
                            last = nc.tensor.transpose(GROUP_BANK[:, b * P:(b + 1) * P],
                                                       YT[KIND[name]][:, b * P:(b + 1) * P], ident[:, :])
                    last.then_inc(bank_filled[name], 1)

            attention_loop(pe, body, extra)
            remainder()


_OUT = ((B, P, P), "float32")


def head_channel_last_to_stack(a):
    n = a.shape[0]
    return a.reshape(n, 2, NJ, HD).transpose(0, 1, 3, 2).reshape(n, P)


def rows_of_chunks(a):
    k, n = a.shape[0] // P, a.shape[1]
    return a.reshape(k, P, n).transpose(1, 0, 2).reshape(P, k * n)


def pack(inputs):
    import numpy as np
    a = {k: np.asarray(v) for k, v in inputs.items()}
    l0 = {k[9:]: v for k, v in a.items() if k.startswith("L0_")}
    l1 = {k[9:]: v for k, v in a.items() if k.startswith("L1_")}
    qkv, kvc = l0["W_qkv"], l0["W_kvc"]
    ew1, gw1, rw = l1["e_w1"], l1["gate_w1"], l1["router_W"]

    def experts(lo):
        return ew1[:, lo:lo + P, :].transpose(1, 0, 2).reshape(P, -1)

    w = {
        "mod": l0["W_mod"],
        "q": head_channel_last_to_stack(qkv[:, 0:P]), "k": head_channel_last_to_stack(qkv[:, P:2 * P]),
        "v": qkv[:, 2 * P:], "proj": l0["W_proj"],
        "qc": head_channel_last_to_stack(l0["W_qc"]), "kc": head_channel_last_to_stack(kvc[:, 0:P]),
        "vc": kvc[:, P:], "cproj": l0["W_cproj"],
        "mlp1": l0["W_mlp1"], "mlp2": rows_of_chunks(l0["W_mlp2"]),
        "wqT": l1["Wq"].T, "wkT": l1["Wk"].T, "wvT": l1["Wv"].T,
        "r_nx": rw[0:P], "r_ev": rw[P:2 * P], "r_an": rw[2 * P:],
        "e_nx": experts(0), "g_nx": gw1[0:P], "e_ev": experts(P), "g_ev": gw1[P:2 * P],
        "e_an": experts(2 * P), "g_an": gw1[2 * P:], "gate2": l1["gate_w2"],
        "e2T": l1["e_w2"].transpose(2, 0, 1).reshape(P, -1), "outw": l1["out_w"],
    }
    bq = l0["b_qkv"]
    v = {
        "bmod": l0["b_mod"].reshape(6, P).T,
        "bq": head_channel_last_to_stack(bq[None, 0:P]).T, "bk": head_channel_last_to_stack(bq[None, P:2 * P]).T,
        "bv": bq[2 * P:, None], "bproj": l0["b_proj"][:, None],
        "bqc": head_channel_last_to_stack(l0["b_qc"][None]).T,
        "bkc": head_channel_last_to_stack(l0["b_kvc"][None, 0:P]).T, "bvc": l0["b_kvc"][P:, None],
        "bcproj": l0["b_cproj"][:, None], "bmlp1": l0["b_mlp1"].reshape(4, P).T, "bmlp2": l0["b_mlp2"][:, None],
        "gamma": l1["ln_gamma"][:, None], "beta": l1["ln_beta"][:, None],
        "be1": l1["e_b1"].reshape(6, P).T, "bg1": l1["gate_b1"][:, None], "be2": l1["e_b2"].T,
    }
    rows = np.concatenate([l1["out_b"], l1["gate_b2"], l1["router_b"]])[None]
    return {
        "x": a["x"], "cond": a["cond_1024"], "ctx": a["ctx_1024"],
        "weights": np.ascontiguousarray(np.concatenate([w[k] for k in W_COLS], axis=1)),
        "vectors": np.ascontiguousarray(np.concatenate([v[k] for k in V_COLS], axis=1)),
        "ident": np.eye(P, dtype=np.float32), "rows": np.ascontiguousarray(rows),
    }


def kernel(**inputs):
    import concourse.bacc as bacc
    from concourse.bass_utils import run_bass_kernel_spmd

    nc = bacc.Bacc("TRN2", target_bir_lowering=False, num_devices=1)
    arrays, args = {}, []
    for name, a in pack(inputs).items():
        arrays[f"in_{name}"] = a
        args.append(nc.dram_tensor(f"in_{name}", a.shape, mybir.dt.from_np(a.dtype), kind="ExternalInput").ap())
    args.append(nc.dram_tensor("out", _OUT[0], F32, kind="ExternalOutput").ap())
    build_block(nc, *args)
    r = run_bass_kernel_spmd(nc, [arrays], core_ids=[0])
    return r.results[0]["out"]
```
